# Optimizing a Trainium2 kernel written in Bass

```python
import numpy as np
import jax
import jax.numpy as jnp

def _softmax(x, axis=-1):
    return jax.nn.softmax(x, axis=axis)

def _gelu(x):
    return jax.nn.gelu(x, approximate=True)

def _silu(x):
    return jax.nn.silu(x)

def _sigmoid(x):
    return jax.nn.sigmoid(x)

def _layernorm(x, axis=-1, eps=1e-05):
    m = jnp.mean(x, axis=axis, keepdims=True)
    v = jnp.var(x, axis=axis, keepdims=True)
    return (x - m) / jnp.sqrt(v + eps)

def _scatter_add(tgt, idx, src, axis=0):
    return tgt.at[idx].add(src)

def _segment_sum(src, seg, n):
    return jax.ops.segment_sum(src, seg, n)
kernel_name = 'mk_decoder_preln_d1_seqx_r4_f554ef'

def setup_inputs(seed: int=0):
    np.random.seed(seed)
    _w = jnp.asarray

    def _rec_inputs():
        import jax
        import jax.numpy as jnp
        _rk = jax.random.key(seed)
        x = 0.0002417 + 0.9998 * jax.random.normal(jax.random.fold_in(_rk, 1), (4, 1024, 256), jnp.float32)
        _lenS = 1024 - jax.random.randint(jax.random.fold_in(_rk, 7), (4,), 0, max(1, 1024 // 4) + 1, jnp.int32)
        _lenS2 = 77 - jax.random.randint(jax.random.fold_in(_rk, 8), (4,), 0, max(1, 77 // 4) + 1, jnp.int32)
        _ctx_1024P = jax.random.normal(jax.random.fold_in(_rk, 11), (4, 16, 256), jnp.float32)
        _ctx_1024c = jax.random.dirichlet(jax.random.fold_in(_rk, 511), 0.3 * jnp.ones((16,), jnp.float32), (4, 77))
        _ctx_1024t = jnp.einsum('bsk,bkd->bsd', _ctx_1024c, _ctx_1024P)
        _ctx_1024t = _ctx_1024t * jax.lax.rsqrt(jnp.mean(jnp.square(_ctx_1024t)) + 1e-12) * 0.953939
        ctx_1024 = 7.22013e-05 + 1.00017 * (_ctx_1024t + 0.3 * jax.random.normal(jax.random.fold_in(_rk, 611), (4, 77, 256), jnp.float32))
        _validS = jnp.arange(1024)[None, :] < _lenS[:, None]
        _validS2 = jnp.arange(77)[None, :] < _lenS2[:, None]
        _causal = jnp.tril(jnp.ones((1024, 1024), dtype=bool))
        mask_Bx1xS2_bf1 = jnp.ones((4, 1, 77), dtype=bool)
        return (x, ctx_1024, mask_Bx1xS2_bf1)
    x, ctx_1024, mask_Bx1xS2_bf1 = _rec_inputs()

    def _L0_attn_setup():
        import jax, jax.numpy as jnp
        import numpy as np
        DIM = 256
        DIM_HEAD = 128
        HEADS = 8
        DIM_INNER = DIM_HEAD * HEADS
        key = jax.random.key(seed)
        k_x, k_qkv, k_out = jax.random.split(key, 3)
        x = jax.random.normal(k_x, (2, 512, DIM), dtype=jnp.float32)
        gamma = jnp.ones((DIM,), dtype=jnp.float32)
        w_qkv = jax.random.uniform(k_qkv, (DIM_INNER * 3, DIM), dtype=jnp.float32, minval=-1.0, maxval=1.0) / np.sqrt(DIM)
        w_out = jax.random.uniform(k_out, (DIM, DIM_INNER), dtype=jnp.float32, minval=-1.0, maxval=1.0) / np.sqrt(DIM_INNER)
        return {'x': x, 'gamma': gamma, 'w_qkv': w_qkv, 'w_out': w_out}
    _L0_attn_all = _L0_attn_setup()
    _L0_attn_in = {k: v for k, v in _L0_attn_all.items() if k in ('gamma', 'w_qkv', 'w_out')}
    del _L0_attn_all

    def _L0_xattn_setup():
        import jax, jax.numpy as jnp
        import numpy as np
        H = 16
        D = 256
        HD = D // H
        key = jax.random.key(seed)
        ks = jax.random.split(key, 12)
        B, S = (4, 512)
        scale = 1.0 / np.sqrt(D)
        inp = {'k': jax.random.normal(ks[0], (B, S, D), jnp.float32), 'v': jax.random.normal(ks[1], (B, S, D), jnp.float32), 'q': jax.random.normal(ks[2], (B, S, D), jnp.float32), 'mask': jnp.ones((B, 1, S), dtype=bool), 'Wk': jax.random.normal(ks[3], (D, D), jnp.float32) * scale, 'bk': jax.random.normal(ks[4], (D,), jnp.float32) * 0.01, 'Wv': jax.random.normal(ks[5], (D, D), jnp.float32) * scale, 'bv': jax.random.normal(ks[6], (D,), jnp.float32) * 0.01, 'Wq': jax.random.normal(ks[7], (D, D), jnp.float32) * scale, 'bq': jax.random.normal(ks[8], (D,), jnp.float32) * 0.01, 'Wo': jax.random.normal(ks[9], (D, D), jnp.float32) * scale, 'bo': jax.random.normal(ks[10], (D,), jnp.float32) * 0.01}
        return inp
    _L0_xattn_all = _L0_xattn_setup()
    _L0_xattn_in = {k: v for k, v in _L0_xattn_all.items() if k in ('Wk', 'bk', 'Wv', 'bv', 'Wq', 'bq', 'Wo', 'bo')}
    del _L0_xattn_all

    def _L0_ffn_setup():
        import jax, jax.numpy as jnp
        import numpy as np
        D_MODEL = 256
        N_HEADS = 16
        HEAD_DIM = D_MODEL // N_HEADS
        KV_LATENT = 128
        N_EXPERTS = 4
        D_HIDDEN = 4 * D_MODEL
        B, T = (2, 256)

        def rmsnorm(x, w, eps=1e-06):
            return w * (x * jax.lax.rsqrt(jnp.mean(x * x, axis=-1, keepdims=True) + eps))

        def layernorm(x, g, b, eps=1e-05):
            mu = jnp.mean(x, axis=-1, keepdims=True)
            var = jnp.mean((x - mu) ** 2, axis=-1, keepdims=True)
            return (x - mu) * jax.lax.rsqrt(var + eps) * g + b

        def apply_rope(x):
            t, d = (x.shape[2], x.shape[3])
            half = d // 2
            pos = jnp.arange(t, dtype=x.dtype)[:, None]
            inv_freq = 1.0 / 10000.0 ** (jnp.arange(half, dtype=x.dtype) / half)
            ang = pos * inv_freq[None, :]
            sin, cos = (jnp.sin(ang), jnp.cos(ang))
            x1, x2 = (x[..., :half], x[..., half:])
            return jnp.concatenate([x1 * cos - x2 * sin, x1 * sin + x2 * cos], axis=-1)

        def mla_attention(x, Wq, Wdkv, Wuk, Wuv, Wo, ln_g, ln_b):
            b, t, _ = x.shape
            q = (x @ Wq.T).reshape(b, t, N_HEADS, HEAD_DIM).transpose(0, 2, 1, 3)
            latent = layernorm(x @ Wdkv.T, ln_g, ln_b)
            k = (latent @ Wuk.T).reshape(b, t, N_HEADS, HEAD_DIM).transpose(0, 2, 1, 3)
            v = (latent @ Wuv.T).reshape(b, t, N_HEADS, HEAD_DIM).transpose(0, 2, 1, 3)
            q = apply_rope(q)
            k = apply_rope(k)
            scores = jnp.einsum('bhqd,bhkd->bhqk', q, k) / np.sqrt(HEAD_DIM)
            causal = jnp.tril(jnp.ones((t, t), dtype=bool))
            scores = jnp.where(causal, scores, -jnp.inf)
            attn = jax.nn.softmax(scores, axis=-1)
            out = jnp.einsum('bhqk,bhkd->bhqd', attn, v).transpose(0, 2, 1, 3).reshape(b, t, D_MODEL)
            return out @ Wo.T

        def moe(x, gate_w, gate_b, W1, b1, W2, b2):
            logits = x @ gate_w.T + gate_b
            top = jnp.argmax(logits, axis=-1)
            onehot = jax.nn.one_hot(top, N_EXPERTS, dtype=x.dtype)
            h = jax.nn.relu(jnp.einsum('btd,ehd->bteh', x, W1) + b1)
            y = jnp.einsum('bteh,edh->bted', h, W2) + b2
            return jnp.einsum('bted,bte->btd', y, onehot)
        key = jax.random.key(seed)
        ks = jax.random.split(key, 16)
        s = lambda fan_in: 1.0 / np.sqrt(fan_in)
        return {'x': jax.random.normal(ks[0], (B, T, D_MODEL), jnp.float32), 'norm1_w': jnp.ones((D_MODEL,), jnp.float32), 'norm2_w': jnp.ones((D_MODEL,), jnp.float32), 'Wq': jax.random.normal(ks[1], (D_MODEL, D_MODEL), jnp.float32) * s(D_MODEL), 'Wdkv': jax.random.normal(ks[2], (KV_LATENT, D_MODEL), jnp.float32) * s(D_MODEL), 'Wuk': jax.random.normal(ks[3], (D_MODEL, KV_LATENT), jnp.float32) * s(KV_LATENT), 'Wuv': jax.random.normal(ks[4], (D_MODEL, KV_LATENT), jnp.float32) * s(KV_LATENT), 'Wo': jax.random.normal(ks[5], (D_MODEL, D_MODEL), jnp.float32) * s(D_MODEL), 'ln_g': jnp.ones((KV_LATENT,), jnp.float32), 'ln_b': jnp.zeros((KV_LATENT,), jnp.float32), 'gate_w': jax.random.normal(ks[6], (N_EXPERTS, D_MODEL), jnp.float32) * s(D_MODEL), 'gate_b': jnp.zeros((N_EXPERTS,), jnp.float32), 'W1': jax.random.normal(ks[7], (N_EXPERTS, D_HIDDEN, D_MODEL), jnp.float32) * s(D_MODEL), 'b1': jnp.zeros((N_EXPERTS, D_HIDDEN), jnp.float32), 'W2': jax.random.normal(ks[8], (N_EXPERTS, D_MODEL, D_HIDDEN), jnp.float32) * s(D_HIDDEN), 'b2': jnp.zeros((N_EXPERTS, D_MODEL), jnp.float32)}
    _L0_ffn_all = _L0_ffn_setup()
    _L0_ffn_in = {k: v for k, v in _L0_ffn_all.items() if k in ('norm1_w', 'norm2_w', 'Wq', 'Wdkv', 'Wuk', 'Wuv', 'Wo', 'ln_g', 'ln_b', 'gate_w', 'gate_b', 'W1', 'b1', 'W2', 'b2')}
    del _L0_ffn_all
    return {'x': x, 'ctx_1024': ctx_1024, 'mask_Bx1xS2_bf1': mask_Bx1xS2_bf1, 'L0_attn_gamma': _L0_attn_in['gamma'], 'L0_attn_w_qkv': _L0_attn_in['w_qkv'], 'L0_attn_w_out': _L0_attn_in['w_out'], 'L0_xattn_Wk': _L0_xattn_in['Wk'], 'L0_xattn_bk': _L0_xattn_in['bk'], 'L0_xattn_Wv': _L0_xattn_in['Wv'], 'L0_xattn_bv': _L0_xattn_in['bv'], 'L0_xattn_Wq': _L0_xattn_in['Wq'], 'L0_xattn_bq': _L0_xattn_in['bq'], 'L0_xattn_Wo': _L0_xattn_in['Wo'], 'L0_xattn_bo': _L0_xattn_in['bo'], 'L0_ffn_norm1_w': _L0_ffn_in['norm1_w'], 'L0_ffn_norm2_w': _L0_ffn_in['norm2_w'], 'L0_ffn_Wq': _L0_ffn_in['Wq'], 'L0_ffn_Wdkv': _L0_ffn_in['Wdkv'], 'L0_ffn_Wuk': _L0_ffn_in['Wuk'], 'L0_ffn_Wuv': _L0_ffn_in['Wuv'], 'L0_ffn_Wo': _L0_ffn_in['Wo'], 'L0_ffn_ln_g': _L0_ffn_in['ln_g'], 'L0_ffn_ln_b': _L0_ffn_in['ln_b'], 'L0_ffn_gate_w': _L0_ffn_in['gate_w'], 'L0_ffn_gate_b': _L0_ffn_in['gate_b'], 'L0_ffn_W1': _L0_ffn_in['W1'], 'L0_ffn_b1': _L0_ffn_in['b1'], 'L0_ffn_W2': _L0_ffn_in['W2'], 'L0_ffn_b2': _L0_ffn_in['b2']}

def reference(x, ctx_1024, mask_Bx1xS2_bf1, L0_attn_gamma, L0_attn_w_qkv, L0_attn_w_out, L0_xattn_Wk, L0_xattn_bk, L0_xattn_Wv, L0_xattn_bv, L0_xattn_Wq, L0_xattn_bq, L0_xattn_Wo, L0_xattn_bo, L0_ffn_norm1_w, L0_ffn_norm2_w, L0_ffn_Wq, L0_ffn_Wdkv, L0_ffn_Wuk, L0_ffn_Wuv, L0_ffn_Wo, L0_ffn_ln_g, L0_ffn_ln_b, L0_ffn_gate_w, L0_ffn_gate_b, L0_ffn_W1, L0_ffn_b1, L0_ffn_W2, L0_ffn_b2):
    import jax
    import jax.numpy as jnp

    def _L0_attn_ref(x, gamma, w_qkv, w_out):
        import jax, jax.numpy as jnp
        import numpy as np
        DIM = 256
        DIM_HEAD = 128
        HEADS = 8
        DIM_INNER = DIM_HEAD * HEADS
        scale_norm = DIM ** 0.5
        scale_attn = DIM_HEAD ** (-0.5)
        l2 = jnp.sqrt(jnp.sum(x * x, axis=-1, keepdims=True))
        xn = x / jnp.maximum(l2, 1e-12) * scale_norm * gamma
        qkv = jnp.einsum('bnc,fc->bnf', xn, w_qkv)
        b, n, _ = qkv.shape
        qkv = qkv.reshape(b, n, 3, HEADS, DIM_HEAD)
        q, k, v = (qkv[:, :, 0], qkv[:, :, 1], qkv[:, :, 2])
        q = q * scale_attn
        sim = jnp.einsum('bihd,bjhd->bhij', q, k)
        causal_mask = jnp.triu(jnp.ones((n, n), dtype=bool), k=1)
        neg = -jnp.finfo(sim.dtype).max
        sim = jnp.where(causal_mask, neg, sim)
        attn = jax.nn.softmax(sim, axis=-1)
        out = jnp.einsum('bhij,bjhd->bihd', attn, v)
        out = out.reshape(b, n, DIM_INNER)
        return jnp.einsum('bnf,cf->bnc', out, w_out)

    def _L0_xattn_ref(k, v, q, mask, Wk, bk, Wv, bv, Wq, bq, Wo, bo):
        import jax, jax.numpy as jnp
        import numpy as np
        H = 16
        D = 256
        HD = D // H
        B, Sq, _ = q.shape
        Sk = k.shape[1]
        kh = (k @ Wk.T + bk).reshape(B, Sk, H, HD).transpose(0, 2, 1, 3)
        vh = (v @ Wv.T + bv).reshape(B, Sk, H, HD).transpose(0, 2, 1, 3)
        qh = (q @ Wq.T + bq).reshape(B, Sq, H, HD).transpose(0, 2, 1, 3)
        qh = qh / jnp.sqrt(jnp.asarray(HD, qh.dtype))
        scores = jnp.einsum('bhqd,bhkd->bhqk', qh, kh)
        scores = jnp.where(mask[:, None, :, :], scores, jnp.asarray(-jnp.inf, scores.dtype))
        attn = jax.nn.softmax(scores, axis=-1)
        ctx = jnp.einsum('bhqk,bhkd->bhqd', attn, vh)
        ctx = ctx.transpose(0, 2, 1, 3).reshape(B, Sq, H * HD)
        out = ctx @ Wo.T + bo
        return out

    def _L0_ffn_ref(x, norm1_w, norm2_w, Wq, Wdkv, Wuk, Wuv, Wo, ln_g, ln_b, gate_w, gate_b, W1, b1, W2, b2):
        import jax, jax.numpy as jnp
        import numpy as np
        D_MODEL = 256
        N_HEADS = 16
        HEAD_DIM = D_MODEL // N_HEADS
        KV_LATENT = 128
        N_EXPERTS = 4
        D_HIDDEN = 4 * D_MODEL
        B, T = (2, 256)

        def rmsnorm(x, w, eps=1e-06):
            return w * (x * jax.lax.rsqrt(jnp.mean(x * x, axis=-1, keepdims=True) + eps))

        def layernorm(x, g, b, eps=1e-05):
            mu = jnp.mean(x, axis=-1, keepdims=True)
            var = jnp.mean((x - mu) ** 2, axis=-1, keepdims=True)
            return (x - mu) * jax.lax.rsqrt(var + eps) * g + b

        def apply_rope(x):
            t, d = (x.shape[2], x.shape[3])
            half = d // 2
            pos = jnp.arange(t, dtype=x.dtype)[:, None]
            inv_freq = 1.0 / 10000.0 ** (jnp.arange(half, dtype=x.dtype) / half)
            ang = pos * inv_freq[None, :]
            sin, cos = (jnp.sin(ang), jnp.cos(ang))
            x1, x2 = (x[..., :half], x[..., half:])
            return jnp.concatenate([x1 * cos - x2 * sin, x1 * sin + x2 * cos], axis=-1)

        def mla_attention(x, Wq, Wdkv, Wuk, Wuv, Wo, ln_g, ln_b):
            b, t, _ = x.shape
            q = (x @ Wq.T).reshape(b, t, N_HEADS, HEAD_DIM).transpose(0, 2, 1, 3)
            latent = layernorm(x @ Wdkv.T, ln_g, ln_b)
            k = (latent @ Wuk.T).reshape(b, t, N_HEADS, HEAD_DIM).transpose(0, 2, 1, 3)
            v = (latent @ Wuv.T).reshape(b, t, N_HEADS, HEAD_DIM).transpose(0, 2, 1, 3)
            q = apply_rope(q)
            k = apply_rope(k)
            scores = jnp.einsum('bhqd,bhkd->bhqk', q, k) / np.sqrt(HEAD_DIM)
            causal = jnp.tril(jnp.ones((t, t), dtype=bool))
            scores = jnp.where(causal, scores, -jnp.inf)
            attn = jax.nn.softmax(scores, axis=-1)
            out = jnp.einsum('bhqk,bhkd->bhqd', attn, v).transpose(0, 2, 1, 3).reshape(b, t, D_MODEL)
            return out @ Wo.T

        def moe(x, gate_w, gate_b, W1, b1, W2, b2):
            logits = x @ gate_w.T + gate_b
            top = jnp.argmax(logits, axis=-1)
            onehot = jax.nn.one_hot(top, N_EXPERTS, dtype=x.dtype)
            h = jax.nn.relu(jnp.einsum('btd,ehd->bteh', x, W1) + b1)
            y = jnp.einsum('bteh,edh->bted', h, W2) + b2
            return jnp.einsum('bted,bte->btd', y, onehot)
        x = x + mla_attention(rmsnorm(x, norm1_w), Wq, Wdkv, Wuk, Wuv, Wo, ln_g, ln_b)
        x = x + moe(rmsnorm(x, norm2_w), gate_w, gate_b, W1, b1, W2, b2)
        return x
    x = x + _L0_attn_ref(_layernorm(x, axis=-1), L0_attn_gamma, L0_attn_w_qkv, L0_attn_w_out)
    x = x + _L0_xattn_ref(ctx_1024, ctx_1024, _layernorm(x, axis=-1), mask_Bx1xS2_bf1, L0_xattn_Wk, L0_xattn_bk, L0_xattn_Wv, L0_xattn_bv, L0_xattn_Wq, L0_xattn_bq, L0_xattn_Wo, L0_xattn_bo)
    x = x + _L0_ffn_ref(_layernorm(x, axis=-1), L0_ffn_norm1_w, L0_ffn_norm2_w, L0_ffn_Wq, L0_ffn_Wdkv, L0_ffn_Wuk, L0_ffn_Wuv, L0_ffn_Wo, L0_ffn_ln_g, L0_ffn_ln_b, L0_ffn_gate_w, L0_ffn_gate_b, L0_ffn_W1, L0_ffn_b1, L0_ffn_W2, L0_ffn_b2)
    return x

_drawn_inputs = setup_inputs


def setup_inputs(seed=0):
    import zlib

    import numpy as np

    out = dict(_drawn_inputs(seed))
    spreads = {'L0_attn_gamma': (1.0, 0.2),
     'L0_ffn_norm1_w': (1.0, 0.2),
     'L0_ffn_norm2_w': (1.0, 0.2),
     'L0_ffn_ln_g': (1.0, 0.2),
     'L0_ffn_ln_b': (0.0, 0.1),
     'L0_ffn_gate_b': (0.0, 0.1),
     'L0_ffn_b1': (0.0, 0.268),
     'L0_ffn_b2': (0.0, 0.1)}
    factors = {'L0_xattn_bk': 8.0, 'L0_xattn_bq': 4.776}
    for name, (base, spread) in spreads.items():
        noise = np.random.default_rng([zlib.crc32(name.encode()), seed]).standard_normal(out[name].shape)
        drawn = base * np.exp(spread * noise) if base else spread * noise
        out[name] = jnp.asarray(drawn.astype(out[name].dtype))
    for name, factor in factors.items():
        out[name] = (out[name] * factor).astype(out[name].dtype)
    return out
```

```python
from contextlib import ExitStack

import numpy as np

import concourse.bass as bass
from concourse import mybir

F32 = mybir.dt.float32
BF16 = mybir.dt.bfloat16
I32 = mybir.dt.int32
U32 = mybir.dt.uint32
U8 = mybir.dt.uint8
U16 = mybir.dt.uint16
ALU = mybir.AluOpType
ACT = mybir.ActivationFunctionType
AX = mybir.AxisListType

P = 128
BATCH, T, D = 4, 1024, 256
NT = T // P
KT = D // P
BANK = 512
HEADS, HD = 8, 128
XHEADS, XHD, CTX = 16, 16, 77
MHEADS, MHD, LAT = 16, 16, 128
GROUP = 4
NG = MHEADS // GROUP
SLOT = 32
EXPERTS, HID = 4, 1024
ROW_TILES = BATCH * NT
MOE_TILES = ROW_TILES + EXPERTS
HK = HID // P
MASKED = -3.0e38
TRI = [P * t * (t + 1) // 2 for t in range(NT + 1)]

TURN_SELF, TURN_CROSS, TURN_CROSS_OUT, TURN_LATENT, TURN_LATENT_OUT, TURN_GATE = range(6)
TURNS = 6
PROJ_SELF, PROJ_CROSS, PROJ_LATENT = range(3)
PROJS = 3
NORM_SELF, NORM_CROSS, NORM_LATENT, NORM_KV, NORM_GATE = range(5)
NORMS = 5


MAX_CHUNKS = [(j, t, c) for j in range(GROUP) for t in range(NT) for c in range(t // 4 + 1)]
FIRST_CHUNKS = sorted(MAX_CHUNKS, key=lambda x: (x[1], x[0], x[2]))
CHUNKS = len(MAX_CHUNKS)


class Count:

    def __init__(self, base=0):
        self.base, self.n = base, 0

    def __call__(self, more=1):
        self.n += more
        return self.base + self.n


DVE_STEPS, POOL_STEPS = 70, 24


def decoder_block(nc, d):
    with ExitStack() as ctx:
        def sb(name, shape, dt=F32):
            return ctx.enter_context(nc.sbuf_tensor(name, shape, dt))

        def sem(name):
            return ctx.enter_context(nc.semaphore(name))

        ident = sb("ident", [P, P])
        ident_b = sb("ident_b", [P, P], BF16)
        causal_b = sb("causal_b", [P, P], BF16)
        causal_t_b = sb("causal_t_b", [P, P], BF16)
        before_b = sb("before_b", [P, P], BF16)
        ones_b = sb("ones_b", [P, P], BF16)
        ones_f = sb("ones_f", [1, P])
        gamma = sb("gamma", [P, KT])
        norm1 = sb("norm1", [P, KT])
        lat_gb = sb("lat_gb", [P, 2])
        bq = sb("bq", [P, KT])
        bk = sb("bk", [P, KT])
        bv = sb("bv", [CTX, D])
        bo = sb("bo", [1, D])
        norm2 = sb("norm2", [P, D])
        gate_b = sb("gate_b", [P, EXPERTS])
        head_rows = sb("head_rows", [P, NT])
        rope_q = sb("rope_q", [P, NT, 2 * MHD])
        rope_k = sb("rope_k", [P, NT, 2 * MHD])
        tile_at = sb("tile_at", [P, MOE_TILES])
        w_out = sb("w_out", [P, HEADS, D])
        xw_q = sb("xw_q", [P, KT, D])
        xw_k = sb("xw_k", [P, KT, D])
        xw_v = sb("xw_v", [P, KT, D])
        xw_o = sb("xw_o", [P, KT, D])
        mw_qd = sb("mw_qd", [P, KT, D + LAT])
        mw_kv = sb("mw_kv", [P, 2 * D])
        mw_o = sb("mw_o", [P, KT, D])
        w_gate = sb("w_gate", [P, KT, EXPERTS])
        consts = [
            (ident, "ident"), (ident_b, "ident_b"), (causal_b, "causal_b"), (causal_t_b, "causal_t_b"),
            (before_b, "before_b"), (gamma, "gamma"), (norm1, "norm1"), (lat_gb, "lat_gb"), (bq, "bq"),
            (bk, "bk"), (bv, "bv"), (bo, "bo"), (norm2, "norm2"), (gate_b, "gate_b"),
            (head_rows, "head_rows"), (rope_q, "rope_q"), (rope_k, "rope_k"), (tile_at, "tile_at"),
            (w_out, "w_out"), (xw_q, "xw_q"), (xw_k, "xw_k"), (xw_v, "xw_v"), (xw_o, "xw_o"),
            (mw_qd, "mw_qd"), (mw_kv, "mw_kv"), (mw_o, "mw_o"), (w_gate, "w_gate"),
        ]
        CONSTS = 16 * len(consts)
        MADE = 13

        xin = sb("xin", [P, NT, D])
        xres = sb("xres", [P, NT, D])
        xp = sb("xp", [P, NT, D])
        rows = sb("rows", [P, NT, D])
        turned_t = sb("turned_t", [P, KT, T])
        stats = sb("stats", [P, NT, 6])
        mv = sb("mv", [P, NT, 2])
        scale = sb("scale", [P, NT])
        scale2 = sb("scale2", [P, NT])
        tmp1 = sb("tmp1", [P, NT])
        tmp2 = sb("tmp2", [P, NT])
        pause = sb("pause", [P, 1])
        pool_pause = sb("pool_pause", [P, NT])
        c_eps5 = sb("c_eps5", [P, NT])
        c_eps6 = sb("c_eps6", [P, NT])
        c_nhalf = sb("c_nhalf", [P, NT])
        c_half = sb("c_half", [P, NT])
        c_neg1 = sb("c_neg1", [P, NT])
        c_root = sb("c_root", [P, NT])
        logits = sb("logits", [P, ROW_TILES, EXPERTS])
        ctx_t = sb("ctx_t", [P, KT, CTX])
        mask_u8 = sb("mask_u8", [1, CTX], U8)
        mask_row = sb("mask_row", [1, GROUP, CTX], BF16)
        xv = sb("xv", [CTX, XHEADS, SLOT])
        mv_rows = sb("mv_rows", [P, NT, MHEADS, SLOT])
        neg_max = sb("neg_max", [P, 2, NT])
        row_sum = sb("row_sum", [P, 2, NT])
        inv_sum = sb("inv_sum", [P, 2, NT])

        ARENA = 29800
        arena = sb("arena", [P, ARENA])

        class Region:
            def __init__(self, at=0):
                self.at = at

            def __call__(self, *dims, dt=F32, rows=P):
                n = int(np.prod(dims))
                words = n // 2 if dt == BF16 else n
                ap = arena[0:rows, self.at:self.at + words]
                self.at += words
                assert self.at <= ARENA, self.at
                if dt != F32:
                    ap = ap.bitcast(dt)
                if len(dims) == 1:
                    return ap
                names = "abcd"[:len(dims)]
                return ap.rearrange(f"p ({' '.join(names)}) -> p {' '.join(names)}",
                                    **dict(zip(names[1:], dims[1:])))

        r = Region()
        attn_t = r(HEADS, T)
        q_t = [r(T) for _ in range(2)]
        k_t = [r(T) for _ in range(2)]
        v_rows = [r(NT, HD) for _ in range(2)]
        w_head = [r(KT, 3 * HD) for _ in range(2)]
        probs = [r(TRI[NT]) for _ in range(2)]
        probs_t = [r(BANK) for _ in range(4)]
        r = Region()
        xprobs_t = r(XHEADS, BANK, rows=CTX)
        xout_t = r(NG, T)
        xq_t = r(KT, T)
        xk_blocks = r(KT, NT, CTX)
        xs = [r(XHEADS, CTX) for _ in range(2)]
        xinv = r(NT, XHEADS)
        xneg = [r(XHEADS // 2) for _ in range(2)]
        r = Region()
        q_stack_t = r(MHEADS, T, dt=BF16)
        k_stack_t = r(MHEADS, T, dt=BF16)
        at = r.at
        lat_rows = r(NT, LAT)
        lat_t = r(T)
        q_rest = r(2, MHEADS, MHD)
        k_rest = r(2, MHEADS, MHD)
        r = Region(at)
        mout_t = r(NG, T)
        v_group = rows[:, 0:4, :].rearrange("p t (a n) -> p (t a) n", n=P)
        max_part = r(GROUP, NT, 2)
        max_neg = r(NT, GROUP)
        max_rest = r(NT, GROUP)
        max_stack = r(NT, GROUP, SLOT, dt=BF16)
        minv = r(NT, MHEADS)
        at = r.at
        q_rope = r(NT, D)
        k_rope = r(NT, D)
        q_stack = [r(MHEADS, P, dt=BF16) for _ in range(2)]
        k_stack = [r(MHEADS, P, dt=BF16) for _ in range(2)]
        r = Region(at)
        mprobs_t = [r(GROUP, T) for _ in range(2)]
        r = Region()
        w1 = r(KT, EXPERTS * HID)
        w2 = r(EXPERTS * HK, D)
        moe_rows = r(ROW_TILES, D)
        best = r(ROW_TILES)
        onehot = r(ROW_TILES, EXPERTS)
        onehot_b = r(ROW_TILES, EXPERTS, dt=BF16)
        cum = [r(ROW_TILES, EXPERTS) for _ in range(2)]
        e_tiles = r(EXPERTS)
        e_more = r(EXPERTS, ROW_TILES)
        e_start = r(EXPERTS)
        dest_f = r(ROW_TILES)
        dest = r(ROW_TILES, dt=U32)
        tile_e = r(MOE_TILES)
        tile_ei = r(MOE_TILES, dt=I32)
        b1 = mv_rows[:].rearrange("p t h e -> p (t h e)")
        b2 = turned_t[:, 1, :]
        h_rows = [xp[:, 4 * i:4 * i + 4, :].rearrange("p t n -> p (t n)") for i in range(2)]
        h_t = [rows[:, 4 * i:4 * i + 4, :].rearrange("p t (a n) -> p (t a) n", n=P) for i in range(2)]
        xs_t = [turned_t[:, 0, KT * P * i:KT * P * (i + 1)].rearrange("p (a n) -> p a n", a=KT) for i in range(2)]
        xs_in = [xin[:, 2 * i, :] for i in range(2)]
        y_rows = [xin[:, 4 + i, :] for i in range(2)]

        ps = ctx.enter_context(nc.psum_tensor("ps", [P, 8, BANK], F32))

        consts_in = sem("consts_in")
        consts_made = sem("consts_made")
        x_in = sem("x_in")
        ctx_in = sem("ctx_in")
        w_in = [sem(f"w_in{i}") for i in range(2)]
        dve_step = sem("dve_step")
        pool_step = sem("pool_step")
        act_step = sem("act_step")
        stats_ready = sem("stats_ready")
        scales_ready = sem("scales_ready")
        rows_ready = sem("rows_ready")
        turn_done = sem("turn_done")
        turn_taken = sem("turn_taken")
        qk_done = sem("qk_done")
        qk_taken = sem("qk_taken")
        v_done = sem("v_done")
        v_taken = sem("v_taken")
        scores_done = sem("scores_done")
        max_done = sem("max_done")
        exp_done = sem("exp_done")
        inv_done = sem("inv_done")
        probs_done = sem("probs_done")
        pt_done = sem("pt_done")
        pt_taken = sem("pt_taken")
        pv_done = sem("pv_done")
        out_taken = sem("out_taken")
        proj_done = sem("proj_done")
        proj_added = sem("proj_added")
        mask_made = sem("mask_made")
        xkv_done = sem("xkv_done")
        xkv_taken = sem("xkv_taken")
        xq_done = sem("xq_done")
        xq_taken = sem("xq_taken")
        xs_done = sem("xs_done")
        xs_taken = sem("xs_taken")
        xneg_done = sem("xneg_done")
        xexp_done = sem("xexp_done")
        xpt_done = sem("xpt_done")
        xpt_taken = sem("xpt_taken")
        xpv_done = sem("xpv_done")
        xpv_taken = sem("xpv_taken")
        back_done = sem("back_done")
        mq_done = sem("mq_done")
        mq_taken = sem("mq_taken")
        mlat_taken = sem("mlat_taken")
        lat_ready = sem("lat_ready")
        lat_turned = sem("lat_turned")
        lat_taken = sem("lat_taken")
        mkv_done = sem("mkv_done")
        mk_taken = sem("mk_taken")
        mv_taken = sem("mv_taken")
        q_high = sem("q_high")
        k_high = sem("k_high")
        q_split = sem("q_split")
        k_split = sem("k_split")
        q_rest_done = sem("q_rest_done")
        k_rest_done = sem("k_rest_done")
        qs_turned = sem("qs_turned")
        qs_taken = sem("qs_taken")
        ks_turned = sem("ks_turned")
        ks_taken = sem("ks_taken")
        ms_done = sem("ms_done")
        ms_taken = sem("ms_taken")
        mmax_step = sem("mmax_step")
        mx_turned = sem("mx_turned")
        mx_taken = sem("mx_taken")
        mst_done = sem("mst_done")
        mexp_done = sem("mexp_done")
        vg_ready = sem("vg_ready")
        mpv_done = sem("mpv_done")
        mout_taken = sem("mout_taken")
        gate_done = sem("gate_done")
        logits_done = sem("logits_done")
        rows_free = sem("rows_free")
        resid_ready = sem("resid_ready")
        xres_free = sem("xres_free")
        zeros_out = sem("zeros_out")
        moe_w_in = sem("moe_w_in")
        moe_rows_in = sem("moe_rows_in")
        counts_ready = sem("counts_ready")
        counts_done = sem("counts_done")
        route_step = sem("route_step")
        route_ready = sem("route_ready")
        scattered = sem("scattered")
        et_in = [sem(f"et_in{i}") for i in range(2)]
        ex_turned = sem("ex_turned")
        ex_taken = sem("ex_taken")
        eh_done = sem("eh_done")
        eh_taken = sem("eh_taken")
        eh_turned = sem("eh_turned")
        ehT_taken = sem("ehT_taken")
        ey_done = sem("ey_done")
        ey_taken = sem("ey_taken")
        ey_out = [sem(f"ey_out{i}") for i in range(2)]
        resid_in = sem("resid_in")
        gathered = sem("gathered")
        fin_ready = sem("fin_ready")
        fin_out = sem("fin_out")

        block = ctx.enter_context(nc.Block())

        @block.sync
        def _(sp):
            for tile, name in consts:
                sp.dma_start(tile[:].bitcast(U16) if tile.dtype == BF16 else tile[:], d[name]).then_inc(consts_in, 16)

            def load_head(b, h, slot):
                sp.dma_start(w_head[slot], d["w_qkv"][h].rearrange("p (a c) -> p a c", a=KT)).then_inc(w_in[slot], 16)

            sp.wait_ge(consts_made, MADE)
            sp.dma_start(d["sorted_rows"].rearrange("(p a) n -> p a n", p=P),
                         xp[:, 0:1, :].to_broadcast([P, MOE_TILES, D])).then_inc(zeros_out, 16)

            def batch_io(b, last):
                load_head(b, 0, 0)
                load_head(b, 1, 1)
                sp.dma_start(ctx_t[:], d["ctx"][b]).then_inc(ctx_in, 16)
                sp.dma_start(mask_u8[:], d["mask"][b]).then_inc(ctx_in, 16)
                for h in range(2, HEADS):
                    sp.wait_ge(v_done, b * (2 * HEADS) + 2 * (h - 1))
                    load_head(b, h, h % 2)
                if not last:
                    row = sp.snap(b * T + T)
                    sp.wait_ge(proj_added, b * (PROJS * NT) + NT)
                    load_rows(row)
                sp.wait_ge(rows_ready, b * (TURNS * NT) + TURNS * NT)
                sp.dma_start(d["gate_rows"][b].rearrange("(t p) n -> p t n", p=P), rows[:]).then_inc(rows_free, 16)
                sp.wait_ge(resid_ready, b + 1)
                sp.dma_start(d["resid"][b].rearrange("(t p) n -> p t n", p=P), xres[:]).then_inc(xres_free, 16)

            def load_rows(row):
                sp.dma_start(xin[:], d["x"].rearrange("b t n -> (b t) n")[bass.ds(row, T), :].rearrange(
                    "(t p) n -> p t n", p=P)).then_inc(x_in, 16)

            load_rows(0)
            with sp.Fori(0, BATCH - 1) as b:
                batch_io(b, False)
            batch_io(BATCH - 1, True)

            sp.wait_ge(logits_done, BATCH)
            sp.wait_ge(rows_free, 16 * BATCH + 16)
            sp.wait_ge(xres_free, 16 * BATCH + 16)
            sp.dma_start(moe_rows, d["gate_rows"].rearrange("b (t p) n -> p (b t) n", p=P)).then_inc(moe_rows_in, 16)
            sp.dma_start(w1, d["w1"]).then_inc(moe_w_in, 16)
            sp.dma_start(w2, d["w2"]).then_inc(moe_w_in, 16)
            sp.dma_start(b1, d["b1"].partition_broadcast(P).rearrange("p o n -> p (o n)")).then_inc(moe_w_in, 16)
            sp.dma_start(b2, d["b2"].partition_broadcast(P).rearrange("p o n -> p (o n)")).then_inc(moe_w_in, 16)
            sp.wait_ge(scattered, 16 * ROW_TILES)

            def load_tile(row, slot):
                sp.dma_start(xs_in[slot], d["sorted_rows"][bass.ds(row, P), :]).then_inc(et_in[slot], 16)

            def store_tile(row, slot):
                sp.dma_start(d["sorted_out"][bass.ds(row, P), :], y_rows[slot]).then_inc(ey_out[slot], 16)

            load_tile(0, 0)
            load_tile(P, 1)
            with sp.Fori(0, MOE_TILES // 2 - 1) as i:
                for u in range(2):
                    row, row_ahead = sp.snap((i * 2 + u) * P), sp.snap((i * 2 + u + 2) * P)
                    sp.wait_ge(ex_turned, i * 2 + u + 1)
                    load_tile(row_ahead, u)
                    sp.wait_ge(ey_taken, i * 2 + u + 1)
                    store_tile(row, u)
            for u in range(2):
                sp.wait_ge(ey_taken, MOE_TILES - 1 + u)
                store_tile((MOE_TILES - 2 + u) * P, u)

        @block.gpsimd
        def _(pool):
            nc.gpsimd.memset(mv_rows[:], 0.0).then_inc(consts_made, 1)
            pool.wait_ge(consts_made, 1)
            nc.gpsimd.memset(mv_rows[:, :, :, MHD:MHD + 1], 1.0).then_inc(consts_made, 1)
            nc.gpsimd.memset(xv[:], 0.0).then_inc(consts_made, 1)
            pool.wait_ge(consts_made, 3)
            nc.gpsimd.memset(xv[:, :, XHD:XHD + 1], 1.0).then_inc(consts_made, 1)
            nc.gpsimd.memset(ones_b[:], 1.0).then_inc(consts_made, 1)
            nc.gpsimd.memset(ones_f[:], 1.0).then_inc(consts_made, 1)
            nc.gpsimd.memset(xp[:, 0, :], 0.0).then_inc(consts_made, 1)
            for tile, value in ((c_eps5, 1e-5), (c_eps6, 1e-6), (c_nhalf, -0.5), (c_half, 0.5), (c_neg1, -1.0),
                                (c_root, float(D) ** 0.5)):
                nc.gpsimd.memset(tile[:], value).then_inc(consts_made, 1)
            pool.wait_ge(consts_made, MADE)
            pool.wait_ge(consts_in, CONSTS)
            pool.sem_inc(rows_free, 16)
            pool.sem_inc(xres_free, 16)
            mean, var = mv[:, :, 0], mv[:, :, 1]

            with pool.Fori(0, BATCH) as b:
                step = Count(b * POOL_STEPS)

                def inv_root(out, x, eps):
                    nc.gpsimd.tensor_tensor(tmp1[:], x, eps[:], ALU.add).then_inc(pool_step, 1)
                    pool.wait_ge(pool_step, step())
                    nc.gpsimd.tensor_tensor(out, tmp1[:], c_nhalf[:], ALU.pow).then_inc(pool_step, 1)
                    pool.wait_ge(pool_step, step())

                pool.wait_ge(stats_ready, b * NORMS + NORM_SELF + 1)
                inv_root(scale2[:], var, c_eps5)
                nc.gpsimd.tensor_tensor(tmp1[:], var, c_half[:], ALU.pow).then_inc(pool_step, 1)
                pool.wait_ge(pool_step, step())
                nc.gpsimd.tensor_tensor(tmp2[:], tmp1[:], scale2[:], ALU.mult).then_inc(pool_step, 1)
                pool.wait_ge(pool_step, step())
                nc.gpsimd.tensor_tensor(pool_pause[:], c_half[:], c_half[:], ALU.add)
                nc.gpsimd.tensor_scalar(tmp1[:], tmp2[:], float(D) ** 0.5, 1e-12, ALU.mult, ALU.max).then_inc(pool_step, 1)
                pool.wait_ge(pool_step, step())
                nc.gpsimd.tensor_tensor(tmp2[:], tmp1[:], c_neg1[:], ALU.pow).then_inc(pool_step, 1)
                pool.wait_ge(pool_step, step())
                nc.gpsimd.tensor_tensor(tmp1[:], tmp2[:], scale2[:], ALU.mult).then_inc(pool_step, 1)
                pool.wait_ge(pool_step, step())
                nc.gpsimd.tensor_tensor(scale[:], tmp1[:], c_root[:], ALU.mult).then_inc(scales_ready, 1)

                pool.wait_ge(stats_ready, b * NORMS + NORM_CROSS + 1)
                nc.gpsimd.tensor_tensor(tmp1[:], var, c_eps5[:], ALU.add).then_inc(pool_step, 1)
                pool.wait_ge(pool_step, step())
                nc.gpsimd.tensor_tensor(scale[:], tmp1[:], c_nhalf[:], ALU.pow).then_inc(scales_ready, 1)

                pool.wait_ge(stats_ready, b * NORMS + NORM_LATENT + 1)
                inv_root(scale[:], var, c_eps5)
                nc.gpsimd.tensor_tensor(tmp1[:], scale[:], scale[:], ALU.mult).then_inc(pool_step, 1)
                pool.wait_ge(pool_step, step())
                nc.gpsimd.tensor_tensor(tmp2[:], tmp1[:], var, ALU.mult).then_inc(pool_step, 1)
                pool.wait_ge(pool_step, step())
                nc.gpsimd.tensor_tensor(tmp1[:], tmp2[:], c_eps6[:], ALU.add).then_inc(pool_step, 1)
                pool.wait_ge(pool_step, step())
                nc.gpsimd.tensor_tensor(scale2[:], tmp1[:], c_nhalf[:], ALU.pow).then_inc(scales_ready, 1)

                pool.wait_ge(rows_ready, b * (TURNS * NT) + (TURN_LATENT + 1) * NT)
                nc.gpsimd.tensor_tensor(pool_pause[:], c_half[:], c_half[:], ALU.add)
                for s in range(2):
                    nc.gpsimd.memset(q_stack[s][:, :, 6 * MHD:P], 0.0).then_inc(pool_step, 1)
                    nc.gpsimd.memset(k_stack[s][:, :, 6 * MHD + 3:P], 0.0).then_inc(pool_step, 1)
                    nc.gpsimd.memset(k_stack[s][:, :, 6 * MHD:6 * MHD + 3], 1.0).then_inc(pool_step, 1)
                nc.gpsimd.memset(max_stack, 0.0).then_inc(pool_step, 1)
                pool.wait_ge(pool_step, step(7))

                pool.wait_ge(stats_ready, b * NORMS + NORM_KV + 1)
                nc.gpsimd.tensor_tensor(tmp1[:], var, c_eps5[:], ALU.add).then_inc(pool_step, 1)
                pool.wait_ge(pool_step, step())
                nc.gpsimd.tensor_tensor(scale[:], tmp1[:], c_nhalf[:], ALU.pow).then_inc(scales_ready, 1)

                for t in range(NT):
                    s = t % 2
                    kr = k_rope[:, t, :].rearrange("p (h e) -> p h e", h=MHEADS)
                    ks = k_stack[s].rearrange("p h (c e) -> p h c e", e=MHD)
                    pool.wait_ge(k_high, b * NT + t + 1)
                    nc.gpsimd.tensor_tensor(k_rest[:, s, :, :], kr, ks[:, :, 0, :], ALU.subtract).then_inc(k_rest_done, 1)
                    nc.gpsimd.tensor_tensor(ks[:, :, 1, :], kr, ks[:, :, 0, :], ALU.subtract).then_inc(k_rest_done, 1)
                    nc.gpsimd.tensor_tensor(ks[:, :, 3, :], kr, ks[:, :, 0, :], ALU.subtract).then_inc(k_rest_done, 1)
                    pool.wait_ge(k_rest_done, b * (3 * NT) + 3 * t + 3)
                    nc.gpsimd.tensor_tensor(ks[:, :, 2, :], k_rest[:, s, :, :], ks[:, :, 1, :],
                                            ALU.subtract).then_inc(k_split, 1)

                pool.wait_ge(mv_taken, b * NT + NT)
                nc.gpsimd.tensor_tensor(pool_pause[:], c_half[:], c_half[:], ALU.add)
                nc.gpsimd.tensor_copy(v_group.rearrange("p t (h e) -> p t h e", e=SLOT),
                                      mv_rows[:, :, 0:GROUP, :]).then_inc(vg_ready, 1)
                with pool.Fori(1, NG) as g:
                    pool.wait_ge(mpv_done, b * (NG * NT) + g * NT)
                    nc.gpsimd.tensor_tensor(pool_pause[:], c_half[:], c_half[:], ALU.add)
                    nc.gpsimd.tensor_copy(v_group.rearrange("p t (h e) -> p t h e", e=SLOT),
                                          mv_rows[:, :, bass.ds(g * GROUP, GROUP), :]).then_inc(vg_ready, 1)

                pool.wait_ge(stats_ready, b * NORMS + NORM_GATE + 1)
                nc.gpsimd.tensor_tensor(tmp2[:], mean, mean, ALU.mult).then_inc(pool_step, 1)
                pool.wait_ge(pool_step, step())
                nc.gpsimd.tensor_tensor(scale2[:], tmp2[:], var, ALU.add).then_inc(pool_step, 1)
                pool.wait_ge(pool_step, step())
                nc.gpsimd.tensor_tensor(tmp1[:], scale2[:], c_eps6[:], ALU.add).then_inc(pool_step, 1)
                pool.wait_ge(pool_step, step())
                nc.gpsimd.tensor_tensor(scale[:], tmp1[:], c_nhalf[:], ALU.pow).then_inc(scales_ready, 1)
                assert step.n == POOL_STEPS, ("POOL_STEPS", step.n)

            pool.wait_ge(zeros_out, 16)
            pool.wait_ge(moe_rows_in, 16)
            pool.wait_ge(route_ready, 1)
            for t in range(ROW_TILES):
                nc.gpsimd.indirect_dma_start(d["sorted_rows"], bass.IndirectOffsetOnAxis(ap=dest[:, t:t + 1], axis=0),
                                             moe_rows[:, t, :], None).then_inc(scattered, 16)
            for u in range(2):
                pool.wait_ge(ey_out[u], 16 * (MOE_TILES // 2))
            for t in range(ROW_TILES):
                nc.gpsimd.indirect_dma_start(moe_rows[:, t, :], None, d["sorted_out"],
                                             bass.IndirectOffsetOnAxis(ap=dest[:, t:t + 1], axis=0)).then_inc(gathered, 16)

        @block.scalar
        def _(act):
            act.wait_ge(consts_in, CONSTS)
            act.wait_ge(consts_made, MADE)

            with act.Fori(0, BATCH) as b:
                def turn_copy(use, vec):
                    for n in range(2):
                        for kt in range(KT):
                            i = KT * n + kt
                            act.wait_ge(turn_done, b * (4 * TURNS) + 4 * use + i + 1)
                            nc.scalar.activation(turned_t[:, kt, n * BANK:(n + 1) * BANK], ps[:, 4 + i, :], ACT.Copy,
                                                 scale=vec[:, kt:kt + 1] if vec is not None else 1.0).then_inc(turn_taken, 1)

                turn_copy(TURN_SELF, gamma)

                def take_qkv(h, par):
                    for i in range(4):
                        act.wait_ge(qk_done, b * (4 * HEADS) + h * 4 + i + 1)
                        dst = (q_t if i < 2 else k_t)[par][:, (i % 2) * BANK:(i % 2 + 1) * BANK]
                        nc.scalar.activation(dst, ps[:, 4 + i % 3, :], ACT.Copy,
                                             scale=float(HD) ** -0.5 if i < 2 else 1.0).then_inc(qk_taken, 1)
                    for i in range(2):
                        act.wait_ge(v_done, b * (2 * HEADS) + h * 2 + i + 1)
                        nc.scalar.activation(v_rows[par][:, 4 * i:4 * i + 4, :].rearrange("p t e -> p (t e)"),
                                             ps[:, 4 + (4 + i) % 3, :], ACT.Copy).then_inc(v_taken, 1)

                def take_probs(h, part):
                    for u in range((12 * part) // 8, (12 * (part + 1)) // 8):
                        g, kb = (0, u) if u < 4 else (1, u - 4)
                        lo = max(kb - 4 * g, 0) * P
                        act.wait_ge(pt_done, b * (HEADS * 12) + h * 12 + u + 1)
                        if u >= 4:
                            act.wait_ge(pv_done, b * (HEADS * 12) + h * 12 + u - 3)
                        nc.scalar.activation(probs_t[u % 4][:, lo:BANK], ps[:, 4 + u % 2, lo:BANK], ACT.Copy).then_inc(pt_taken, 1)

                def self_exps(h, par, before):
                    for t in range(NT):
                        if before is not None:
                            take_probs(before, t)
                        n = (t + 1) * P
                        buf = 2 * (t % 2)
                        act.wait_ge(max_done, b * (HEADS * NT) + h * NT + t + 1)
                        nc.scalar.activation(probs[par][:, TRI[t]:TRI[t] + n],
                                             ps[:, buf:buf + 2, :].rearrange("p a n -> p (a n)")[:, 0:n], ACT.Exp,
                                             bias=neg_max[:, par, t:t + 1],
                                             accum_out=row_sum[:, par, t:t + 1]).then_inc(exp_done, 1)

                take_qkv(0, 0)
                self_exps(0, 0, None)
                take_qkv(1, 1)
                with act.Fori(0, HEADS // 2 - 1) as i:
                    for u in range(2):
                        self_exps(i * 2 + u + 1, (u + 1) % 2, i * 2 + u)
                        take_qkv(i * 2 + u + 2, u % 2)
                self_exps(HEADS - 1, (HEADS - 1) % 2, HEADS - 2)
                for part in range(8):
                    take_probs(HEADS - 1, part)

                turn_copy(TURN_CROSS, None)
                def cross_exp(u):
                    act.wait_ge(xs_taken, b * (2 * NT) + u + 1)
                    half = xs[u // 2 % 2][:, 8 * (u % 2):8 * (u % 2) + 8, :]
                    nc.scalar.activation(half, half, ACT.Exp).then_inc(xexp_done, 1)

                cross_exp(0)
                for u in range(2 * NT):
                    t = u // 2
                    if u + 1 < 2 * NT:
                        cross_exp(u + 1)
                    for j in range(2 * (u % 2), 2 * (u % 2) + 2):
                        act.wait_ge(xpt_done, b * (NT * NG) + NG * t + j + 1)
                        if t >= 4:
                            act.wait_ge(xpv_done, b * (2 * NG) + j + 1)
                        nc.scalar.activation(xprobs_t[:, GROUP * j:GROUP * (j + 1), (t % 4) * P:(t % 4 + 1) * P],
                                             ps[0:CTX, 4 + j % 2, :].rearrange("p (h n) -> p h n", h=GROUP),
                                             ACT.Copy).then_inc(xpt_taken, 1)
                turn_copy(TURN_CROSS_OUT, None)

                turn_copy(TURN_LATENT, norm1)
                for t in range(NT):
                    act.wait_ge(mq_taken, b * NT + t + 1)
                    nc.scalar.activation(lat_rows[:, t, :], ps[:, t % 4, D:D + LAT], ACT.Copy).then_inc(mlat_taken, 1)
                for n in range(2):
                    act.wait_ge(lat_turned, b * 2 + n + 1)
                    nc.scalar.activation(lat_t[:, n * BANK:(n + 1) * BANK], ps[:, 4 + n, :], ACT.Identity,
                                         scale=lat_gb[:, 0:1], bias=lat_gb[:, 1:2]).then_inc(lat_taken, 1)
                for t in range(NT):
                    act.wait_ge(mk_taken, b * NT + t + 1)
                    nc.scalar.activation(mv_rows[:, t, :, 0:MHD],
                                         ps[:, t % 4, D:2 * D].rearrange("p (h e) -> p h e", h=MHEADS),
                                         ACT.Copy).then_inc(mv_taken, 1)
                def high_parts(t):
                    s = t % 2
                    if t >= 2:
                        act.wait_ge(qs_turned, b * (2 * NT) + 2 * (t - 1))
                        act.wait_ge(ks_turned, b * (2 * NT) + 2 * (t - 1))
                    qr = q_rope[:, t, :].rearrange("p (h e) -> p h e", h=MHEADS).unsqueeze(2)
                    kr = k_rope[:, t, :].rearrange("p (h e) -> p h e", h=MHEADS).unsqueeze(2)
                    qs = q_stack[s].rearrange("p h (c e) -> p h c e", e=MHD)
                    ks = k_stack[s].rearrange("p h (c e) -> p h c e", e=MHD)
                    act.wait_ge(mq_taken, b * NT + t + 1)
                    nc.scalar.activation(qs[:, :, 0:3, :], qr.to_broadcast([P, MHEADS, 3, MHD]),
                                         ACT.Copy).then_inc(q_high, 1)
                    act.wait_ge(mk_taken, b * NT + t + 1)
                    nc.scalar.activation(ks[:, :, 4:6, :], kr.to_broadcast([P, MHEADS, 2, MHD]), ACT.Copy).then_inc(act_step, 1)
                    act.wait_ge(act_step, b * NT + t + 1)
                    nc.scalar.activation(ks[:, :, 0, :], k_rope[:, t, :].rearrange("p (h e) -> p h e", h=MHEADS),
                                         ACT.Copy).then_inc(k_high, 1)

                high_parts(0)
                for t in range(NT):
                    if t + 1 < NT:
                        high_parts(t + 1)
                    for i in range(2):
                        act.wait_ge(ks_turned, b * (2 * NT) + 2 * t + i + 1)
                        nc.scalar.activation(k_stack_t[:, 8 * i:8 * i + 8, t * P:(t + 1) * P],
                                             ps[:, 6 + i, :].bitcast(BF16).rearrange("p (h n) -> p h n", h=8),
                                             ACT.Copy).then_inc(ks_taken, 1)

                with act.Fori(0, NG) as g:
                    use = 0
                    for kb in range(NT):
                        for j in range(GROUP):
                            for c in range(kb // 4, 2):
                                lo = max(kb * P, c * BANK)
                                hi = (c + 1) * BANK
                                act.wait_ge(mst_done, b * (NG * 48) + g * 48 + use + 1)
                                if j == 0 and c == kb // 4 and kb >= 2:
                                    act.wait_ge(mpv_done, b * (NG * NT) + g * NT + kb - 1)
                                nc.scalar.activation(mprobs_t[kb % 2][:, j, lo:hi], ps[:, 3 + use % 3, 0:hi - lo],
                                                     ACT.Exp).then_inc(mexp_done, 1)
                                use += 1
                turn_copy(TURN_LATENT_OUT, None)
                turn_copy(TURN_GATE, None)

            def take_x(j, par):
                act.wait_ge(ex_turned, j + 1)
                nc.scalar.activation(xs_t[par].rearrange("p a n -> p (a n)"), ps[:, 0, 0:KT * P], ACT.Copy).then_inc(ex_taken, 1)

            def take_h(j, par):
                for n in range(2):
                    act.wait_ge(eh_turned, j * 2 + n + 1)
                    nc.scalar.activation(h_t[par][:, 4 * n:4 * n + 4, :].rearrange("p a n -> p (a n)"), ps[:, 5 + n, :],
                                         ACT.Relu).then_inc(ehT_taken, 1)

            take_x(0, 0)
            with act.Fori(0, MOE_TILES // 2 - 1) as i:
                for u in range(2):
                    take_x(i * 2 + u + 1, (u + 1) % 2)
                    take_h(i * 2 + u, u)
            take_x(MOE_TILES - 1, 1)
            take_h(MOE_TILES - 2, 0)
            take_h(MOE_TILES - 1, 1)

            with act.Fori(0, BATCH) as b:
                act.dma_start(xres[:], d["resid"][b].rearrange("(t p) n -> p t n", p=P)).then_inc(resid_in, 16)
                act.wait_ge(fin_ready, b * NT + NT)
                act.dma_start(d["out"][b].rearrange("(t p) n -> p t n", p=P), xres[:]).then_inc(fin_out, 16)
                act.wait_ge(fin_out, b * 16 + 16)
            act.wait_ge(fin_out, 16 * BATCH)

        @block.tensor
        def _(pe):
            pe.wait_ge(consts_in, CONSTS)
            pe.wait_ge(consts_made, MADE)

            with pe.Fori(0, BATCH) as b:
                def turn(use):
                    for n in range(2):
                        pe.wait_ge(rows_ready, b * (TURNS * NT) + use * NT + 4 * n + 4)
                        for kt in range(KT):
                            i = KT * n + kt
                            for t in range(4):
                                last = nc.tensor.transpose(ps[:, 4 + i, t * P:(t + 1) * P],
                                                           rows[:, 4 * n + t, kt * P:(kt + 1) * P], ident[:])
                            last.then_inc(turn_done, 1)

                def turned(use):
                    pe.wait_ge(turn_taken, b * (4 * TURNS) + 4 * use + 4)

                def project(use, lhs, rhs, bias=None):
                    for t in range(NT):
                        if t >= 4:
                            pe.wait_ge(proj_added, b * (PROJS * NT) + use * NT + t - 3)
                        out = ps[:, t % 4, 0:D]
                        for k, (l, w) in enumerate(zip(lhs, rhs)):
                            last = nc.tensor.matmul(out, l[:, t * P:(t + 1) * P], w, start=(k == 0),
                                                    stop=(k == len(lhs) - 1 and bias is None))
                        if bias is not None:
                            last = nc.tensor.matmul(out, ones_f[:], bias, start=False, stop=True)
                        last.then_inc(proj_done, 1)

                turn(TURN_SELF)
                turned(TURN_SELF)

                def project_q(h, par):
                    for i in range(4):
                        if i == 0:
                            pass
                        if i == 3:
                            pe.wait_ge(qk_taken, b * (4 * HEADS) + h * 4 + 1)
                        w = (i // 2) * HD
                        for kt in range(KT):
                            last = nc.tensor.matmul(ps[:, 4 + i % 3, :], w_head[par][:, kt, w:w + HD],
                                                    turned_t[:, kt, (i % 2) * BANK:(i % 2 + 1) * BANK],
                                                    start=(kt == 0), stop=(kt == KT - 1))
                        last.then_inc(qk_done, 1)

                def project_v(h, par):
                    for i in range(2):
                        pe.wait_ge(qk_taken, b * (4 * HEADS) + h * 4 + i + 2)
                        for t in range(4):
                            for kt in range(KT):
                                last = nc.tensor.matmul(ps[:, 4 + (4 + i) % 3, t * P:(t + 1) * P],
                                                        turned_t[:, kt, (4 * i + t) * P:(4 * i + t + 1) * P],
                                                        w_head[par][:, kt, 2 * HD:3 * HD],
                                                        start=(kt == 0), stop=(kt == KT - 1))
                        last.then_inc(v_done, 1)

                def scores(h, par, t):
                    n = (t + 1) * P
                    buf = 2 * (t % 2)
                    if t == 0:
                        pe.wait_ge(qk_taken, b * (4 * HEADS) + h * 4 + 4)
                    pe.wait_ge(exp_done, b * (HEADS * NT) + h * NT + t - 1) if not (isinstance(h, int) and h * NT + t < 2) else None
                    for c in range(0, n, BANK):
                        m = min(BANK, n - c)
                        diag = c + m == n
                        last = nc.tensor.matmul(ps[:, buf + c // BANK, 0:m], q_t[par][:, t * P:(t + 1) * P],
                                                k_t[par][:, c:c + m], start=True, stop=True)
                        if diag:
                            last = nc.tensor.matmul(ps[:, buf + c // BANK, m - P:m], ident_b[:], causal_b[:],
                                                    start=False, stop=True, skip_group_check=True)
                    last.then_inc(scores_done, 1)

                BLOCKS = [(0, kb) for kb in range(4)] + [(1, kb) for kb in range(8)]

                def turn_probs(h, par, u):
                    g, kb = BLOCKS[u]
                    t0 = max(kb, 4 * g)
                    if u >= 2:
                        pe.wait_ge(pt_taken, b * (HEADS * 12) + h * 12 + u - 1)
                    pe.wait_ge(probs_done, b * (HEADS * NT) + h * NT + 4 * g + 4)
                    for t in range(t0, 4 * g + 4):
                        last = nc.tensor.transpose(ps[:, 4 + u % 2, (t - 4 * g) * P:(t - 4 * g + 1) * P],
                                                   probs[par][:, TRI[t] + kb * P:TRI[t] + (kb + 1) * P], ident[:])
                    last.then_inc(pt_done, 1)

                def use_probs(h, par, u):
                    g, kb = BLOCKS[u]
                    lo = max(kb - 4 * g, 0) * P
                    if kb == 0:
                        pe.wait_ge(v_taken, b * (2 * HEADS) + h * 2 + 2)
                    pe.wait_ge(pt_taken, b * (HEADS * 12) + h * 12 + u + 1)
                    nc.tensor.matmul(ps[:, 6 + g, lo:BANK], v_rows[par][:, kb, :], probs_t[u % 4][:, lo:BANK],
                                     start=(kb == 0), stop=True, skip_group_check=True).then_inc(pv_done, 1)

                def products(h, par, part):
                    for u in range((12 * part) // 8, (12 * (part + 1)) // 8):
                        turn_probs(h, par, u)
                        if u > 0:
                            use_probs(h, par, u - 1)
                    if part == 7:
                        use_probs(h, par, 11)

                def wait_weights(h_pairs, slot):
                    pe.wait_ge(w_in[slot], b * (16 * HEADS // 2) + 16 * h_pairs + 16)

                wait_weights(0, 0)
                project_q(0, 0)
                project_v(0, 0)
                for t in range(NT):
                    scores(0, 0, t)
                wait_weights(0, 1)
                pe.wait_ge(v_taken, b * (2 * HEADS) + 2)
                project_q(1, 1)
                project_v(1, 1)
                with pe.Fori(0, HEADS // 2 - 1) as i:
                    for u in range(2):
                        h = i * 2 + u + 1
                        par = (u + 1) % 2
                        for t in range(NT):
                            scores(h, par, t)
                            if t == 0:
                                pe.wait_ge(v_taken, b * (2 * HEADS) + h * 2 + 2)
                            products(h - 1, u % 2, t)
                        pe.wait_ge(pt_taken, b * (HEADS * 12) + h * 12)
                        wait_weights(i + 1, u % 2)
                        project_q(h + 1, u % 2)
                        project_v(h + 1, u % 2)
                        pe.wait_ge(out_taken, b * (2 * HEADS) + h * 2)
                h = HEADS - 1
                for t in range(NT):
                    scores(h, h % 2, t)
                    if t == 0:
                        pe.wait_ge(v_taken, b * (2 * HEADS) + h * 2 + 2)
                    products(h - 1, (h - 1) % 2, t)
                pe.wait_ge(pt_taken, b * (HEADS * 12) + h * 12)
                pe.wait_ge(out_taken, b * (2 * HEADS) + h * 2)
                for t in range(NT):
                    products(h, h % 2, t)
                pe.wait_ge(out_taken, b * (2 * HEADS) + 2 * HEADS)
                project(PROJ_SELF, [attn_t[:, k, :] for k in range(HEADS)], [w_out[:, k, :] for k in range(HEADS)])

                pe.wait_ge(ctx_in, b * 32 + 32)
                pe.wait_ge(proj_added, b * (PROJS * NT) + NT)
                for m in range(KT):
                    for kt in range(KT):
                        last = nc.tensor.matmul(ps[:, m, 0:CTX], xw_k[:, kt, m * P:(m + 1) * P], ctx_t[:, kt, :],
                                                start=(kt == 0), stop=(kt == KT - 1))
                    last.then_inc(xkv_done, 1)
                for kt in range(KT):
                    last = nc.tensor.matmul(ps[0:CTX, 2, 0:D], ctx_t[:, kt, :], xw_v[:, kt, :],
                                            start=(kt == 0), stop=(kt == KT - 1))
                last.then_inc(xkv_done, 1)
                turn(TURN_CROSS)
                turned(TURN_CROSS)
                pe.wait_ge(xkv_taken, b * 3 + 3)
                for n in range(2):
                    for m in range(KT):
                        i = KT * n + m
                        for kt in range(KT):
                            last = nc.tensor.matmul(ps[:, i, :], xw_q[:, kt, m * P:(m + 1) * P],
                                                    turned_t[:, kt, n * BANK:(n + 1) * BANK],
                                                    start=(kt == 0), stop=(kt == KT - 1))
                        last.then_inc(xq_done, 1)

                def cross_scores(u):
                    t, half = divmod(u, 2)
                    if u == 0:
                        pe.wait_ge(xq_taken, b * 4 + 4)
                        pe.wait_ge(mask_made, b + 1)
                    if u >= 2:
                        pe.wait_ge(xs_taken, b * (2 * NT) + u - 1)
                    for j in range(2):
                        nc.tensor.matmul(ps[:, 2 * half + j, 0:GROUP * CTX], xq_t[:, half, t * P:(t + 1) * P],
                                         xk_blocks[:, half, GROUP * j:GROUP * (j + 1), :], start=True, stop=False)
                        last = nc.tensor.matmul(ps[:, 2 * half + j, 0:GROUP * CTX], ones_b[0:1, :],
                                                mask_row[:].rearrange("p h c -> p (h c)"), start=False, stop=True)
                    last.then_inc(xs_done, 1)

                cross_scores(0)
                cross_scores(1)
                for u in range(2 * NT):
                    t = u // 2
                    if u + 2 < 2 * NT:
                        cross_scores(u + 2)
                    pe.wait_ge(xexp_done, b * (2 * NT) + u + 1)
                    for j in range(2 * (u % 2), 2 * (u % 2) + 2):
                        if NG * t + j >= 2:
                            pe.wait_ge(xpt_taken, b * (NT * NG) + NG * t + j - 1)
                        for h in range(GROUP):
                            last = nc.tensor.transpose(ps[0:CTX, 4 + j % 2, h * P:(h + 1) * P],
                                                       xs[t % 2][:, GROUP * j + h, :], ident[:])
                        last.then_inc(xpt_done, 1)
                    if u % 8 == 7:
                        pe.wait_ge(xpt_taken, b * (NT * NG) + NG * t + NG)
                        for j in range(NG):
                            use = NG * (t // 4) + j
                            if use >= 2:
                                pe.wait_ge(xpv_taken, b * (2 * NG) + use - 1)
                            for h in range(GROUP):
                                last = nc.tensor.matmul(ps[SLOT * h:SLOT * (h + 1), 6 + j % 2, :], xv[:, GROUP * j + h, :],
                                                        xprobs_t[:, GROUP * j + h, :], start=True, stop=True)
                            last.then_inc(xpv_done, 1)

                def back(turn_use, src, taken, count):
                    pe.wait_ge(taken, count)
                    for t in range(NT):
                        if t >= 2:
                            pe.wait_ge(rows_ready, b * (TURNS * NT) + turn_use * NT + t - 1)
                        for g in range(NG):
                            last = nc.tensor.transpose(ps[:, t % 2, g * P:(g + 1) * P], src[:, g, t * P:(t + 1) * P], ident[:])
                        last.then_inc(back_done, 1)

                back(TURN_CROSS_OUT, xout_t, xpv_taken, b * (2 * NG) + 2 * NG)
                turn(TURN_CROSS_OUT)
                turned(TURN_CROSS_OUT)
                project(PROJ_CROSS, [turned_t[:, k, :] for k in range(KT)], [xw_o[:, k, :] for k in range(KT)], bo[:])

                turn(TURN_LATENT)
                turned(TURN_LATENT)
                for t in range(NT):
                    if t >= 4:
                        pe.wait_ge(mq_taken, b * NT + t - 3)
                        pe.wait_ge(mlat_taken, b * NT + t - 3)
                    for kt in range(KT):
                        last = nc.tensor.matmul(ps[:, t % 4, 0:D + LAT], turned_t[:, kt, t * P:(t + 1) * P], mw_qd[:, kt, :],
                                                start=(kt == 0), stop=(kt == KT - 1))
                    last.then_inc(mq_done, 1)
                for n in range(2):
                    pe.wait_ge(lat_ready, b * NT + 4 * n + 4)
                    for t in range(4):
                        last = nc.tensor.transpose(ps[:, 4 + n, t * P:(t + 1) * P], lat_rows[:, 4 * n + t, :], ident[:])
                    last.then_inc(lat_turned, 1)
                pe.wait_ge(mq_taken, b * NT + NT)
                for t in range(NT):
                    if t % 4 == 0:
                        pe.wait_ge(lat_taken, b * 2 + t // 4 + 1)
                    if t >= 4:
                        pe.wait_ge(mk_taken, b * NT + t - 3)
                        pe.wait_ge(mv_taken, b * NT + t - 3)
                    nc.tensor.matmul(ps[:, t % 4, :], lat_t[:, t * P:(t + 1) * P], mw_kv[:], start=True,
                                     stop=True).then_inc(mkv_done, 1)
                def turn_stacks(t):
                    for stack, split, done, taken, bank in ((q_stack, q_split, qs_turned, qs_taken, 4),
                                                            (k_stack, k_split, ks_turned, ks_taken, 6)):
                        pe.wait_ge(split, b * NT + t + 1)
                        for i in range(2):
                            if t >= 1:
                                pe.wait_ge(taken, b * (2 * NT) + 2 * t + i - 1)
                            for h in range(8):
                                last = nc.tensor.transpose(ps[:, bank + i, :].bitcast(BF16)[:, h * P:(h + 1) * P],
                                                           stack[t % 2][:, 8 * i + h, :], ident_b[:])
                            last.then_inc(done, 1)

                def max_chunk(g, u):
                    j, t, c = (FIRST_CHUNKS if isinstance(g, int) and g == 0 else MAX_CHUNKS)[u]
                    n = min(BANK, (t + 1) * P - c * BANK)
                    diag = c == t // 4
                    if u >= 3:
                        pe.wait_ge(ms_taken, b * (NG * 48) + g * 48 + u - 2)
                    head = g * GROUP + j
                    last = nc.tensor.matmul(ps[:, u % 3, 0:n], q_stack_t[:, head, t * P:(t + 1) * P],
                                            k_stack_t[:, head, c * BANK:c * BANK + n], start=True, stop=True)
                    if diag:
                        last = nc.tensor.matmul(ps[:, u % 3, n - P:n], ident_b[:], causal_b[:], start=False, stop=True,
                                                skip_group_check=True)
                    last.then_inc(ms_done, 1)

                def turn_max(g):
                    pe.wait_ge(mmax_step, b * (NG * 6) + g * 6 + 6)
                    for j in range(GROUP):
                        if j == 3:
                            pe.wait_ge(mx_taken, b * (NG * GROUP) + g * GROUP + 1)
                        for t in range(NT):
                            last = nc.tensor.transpose(ps[P - SLOT:P, j % 3, :].bitcast(BF16)[:, t * P:(t + 1) * P],
                                                       max_stack[:, t, j, :], ident_b[:])
                        last.then_inc(mx_turned, 1)

                ST_CHUNKS = [(kb, j, c) for kb in range(NT) for j in range(GROUP) for c in range(kb // 4, 2)]

                def key_chunk(g, u):
                    kb, j, c = ST_CHUNKS[u]
                    lo, hi = max(kb * P, c * BANK), (c + 1) * BANK
                    if u >= 3:
                        pe.wait_ge(mexp_done, b * (NG * 48) + g * 48 + u - 2)
                    head = g * GROUP + j
                    diag = lo == kb * P and c == kb // 4
                    last = nc.tensor.matmul(ps[:, 3 + u % 3, 0:hi - lo], k_stack_t[:, head, kb * P:(kb + 1) * P],
                                            q_stack_t[:, head, lo:hi], start=True, stop=True)
                    if diag:
                        last = nc.tensor.matmul(ps[:, 3 + u % 3, 0:P], ident_b[:], causal_t_b[:], start=False, stop=True,
                                                skip_group_check=True)
                    last.then_inc(mst_done, 1)

                def key_products(g, kb):
                    pe.wait_ge(mexp_done, b * (NG * 48) + g * 48 + sum(1 for x in ST_CHUNKS if x[0] <= kb))
                    if kb == 0:
                        pe.wait_ge(vg_ready, b * NG + g + 1)
                    for c in range(kb // 4, 2):
                        lo, hi = max(kb * P, c * BANK), (c + 1) * BANK
                        for j in range(GROUP):
                            last = nc.tensor.matmul(ps[SLOT * j:SLOT * (j + 1), 6 + c, lo - c * BANK:BANK],
                                                    v_group[:, kb, SLOT * j:SLOT * (j + 1)], mprobs_t[kb % 2][:, j, lo:hi],
                                                    start=(kb == 0), stop=True, skip_group_check=True)
                    last.then_inc(mpv_done, 1)

                def keys(g, ahead):
                    pe.wait_ge(mx_taken, b * (NG * GROUP) + g * GROUP + GROUP)
                    kb_done = -1
                    for u in range(48):
                        kb = ST_CHUNKS[u][0]
                        key_chunk(g, u)
                        if ahead:
                            max_chunk(g + 1, u)
                        if u + 1 < 48 and ST_CHUNKS[u + 1][0] != kb and kb >= 1:
                            key_products(g, kb - 1)
                            kb_done = kb - 1
                    for kb in range(kb_done + 1, NT):
                        key_products(g, kb)
                    if ahead:
                        turn_max(g + 1)
                        pe.wait_ge(mout_taken, b * (NG * 2) + g * 2 + 2)

                for t in range(NT + 1):
                    if t < NT:
                        turn_stacks(t)
                    if t == 1:
                        pe.wait_ge(mk_taken, b * NT + NT)
                        pe.wait_ge(mv_taken, b * NT + NT)
                    if t >= 1:
                        pe.wait_ge(qs_taken, b * (2 * NT) + 2 * t)
                        pe.wait_ge(ks_taken, b * (2 * NT) + 2 * t)
                        for u, chunk in enumerate(FIRST_CHUNKS):
                            if chunk[1] == t - 1:
                                max_chunk(0, u)
                turn_max(0)
                with pe.Fori(0, NG - 1) as g:
                    keys(g, True)
                keys(NG - 1, False)

                back(TURN_LATENT_OUT, mout_t, mout_taken, b * (NG * 2) + NG * 2)
                turn(TURN_LATENT_OUT)
                turned(TURN_LATENT_OUT)
                project(PROJ_LATENT, [turned_t[:, k, :] for k in range(KT)], [mw_o[:, k, :] for k in range(KT)])

                turn(TURN_GATE)
                turned(TURN_GATE)
                for t in range(NT):
                    for kt in range(KT):
                        last = nc.tensor.matmul(ps[:, 0, t * EXPERTS:(t + 1) * EXPERTS], turned_t[:, kt, t * P:(t + 1) * P],
                                                w_gate[:, kt, :], start=(kt == 0), stop=(kt == KT - 1))
                last.then_inc(gate_done, 1)

            pe.wait_ge(counts_ready, 1)
            oh = onehot_b.rearrange("p t e -> p (t e)")
            nc.tensor.matmul(ps[:, 1, 0:ROW_TILES * EXPERTS], before_b[:], oh, start=True, stop=True).then_inc(counts_done, 1)
            nc.tensor.matmul(ps[:, 2, 0:ROW_TILES * EXPERTS], ones_b[:], oh, start=True, stop=True).then_inc(counts_done, 1)

            pe.wait_ge(route_ready, 1)
            pe.wait_ge(moe_w_in, 64)

            def expert_in(j, par, pairs):
                pe.wait_ge(et_in[par], 16 * pairs + 16 if isinstance(pairs, int) else pairs * 16 + 16)
                for kt in range(KT):
                    last = nc.tensor.transpose(ps[:, 0, kt * P:(kt + 1) * P], xs_in[par][:, kt * P:(kt + 1) * P], ident[:])
                last.then_inc(ex_turned, 1)
                e = pe.value_load(tile_ei[0:1, bass.ds(j, 1)], min_val=0, max_val=EXPERTS - 1)
                pe.wait_ge(ex_taken, j + 1)
                for n in range(2):
                    if not isinstance(j, int) or j >= 2:
                        pe.wait_ge(eh_taken, j * 2 + n - 3)
                    for kt in range(KT):
                        last = nc.tensor.matmul(ps[:, 1 + 2 * par + n, :], xs_t[par][:, kt, :],
                                                w1[:, kt, bass.ds(e * HID + n * BANK, BANK)],
                                                start=(kt == 0), stop=(kt == KT - 1))
                    last.then_inc(eh_done, 1)

            def expert_out(j, par):
                e = pe.value_load(tile_ei[0:1, bass.ds(j, 1)], min_val=0, max_val=EXPERTS - 1)
                for n in range(2):
                    pe.wait_ge(eh_taken, j * 2 + n + 1)
                    if not isinstance(j, int) or j >= 1:
                        pe.wait_ge(ehT_taken, j * 2 + n - 1)
                    for k in range(4):
                        last = nc.tensor.transpose(ps[:, 5 + n, k * P:(k + 1) * P],
                                                   h_rows[par][:, (4 * n + k) * P:(4 * n + k + 1) * P], ident[:])
                    last.then_inc(eh_turned, 1)
                if not isinstance(j, int) or j >= 1:
                    pe.wait_ge(ey_taken, j)
                for k in range(HK):
                    if k % 4 == 0:
                        pe.wait_ge(ehT_taken, j * 2 + k // 4 + 1)
                    last = nc.tensor.matmul(ps[:, 7, 0:D], h_t[par][:, k, :], w2[:, bass.ds(e * HK + k, 1), :].rearrange("p o n -> p (o n)"),
                                            start=(k == 0), stop=(k == HK - 1))
                last.then_inc(ey_done, 1)

            expert_in(0, 0, 0)
            expert_in(1, 1, 0)
            expert_out(0, 0)
            expert_in(2, 0, 1)
            expert_out(1, 1)
            with pe.Fori(1, MOE_TILES // 2 - 1) as i:
                expert_in(i * 2 + 1, 1, i)
                expert_out(i * 2, 0)
                expert_in(i * 2 + 2, 0, i + 1)
                expert_out(i * 2 + 1, 1)
            expert_in(MOE_TILES - 1, 1, MOE_TILES // 2 - 1)
            expert_out(MOE_TILES - 2, 0)
            expert_out(MOE_TILES - 1, 1)

        @block.vector
        def _(dve):
            dve.wait_ge(consts_in, CONSTS)
            dve.wait_ge(consts_made, MADE)

            with dve.Fori(0, BATCH) as b:
                step = Count(b * DVE_STEPS)

                def row_stats(src, use):
                    for t in range(NT):
                        last = nc.vector.bn_stats(stats[:, t, :], src[:, t, :])
                    finish_stats(last, use)

                def finish_stats(last, use):
                    last.then_inc(dve_step, 1)
                    dve.wait_ge(dve_step, step())
                    nc.vector.memset(pause[:], 0.0)
                    for t in range(NT):
                        last = nc.vector.bn_aggr(mv[:, t, :], stats[:, t, :])
                    last.then_inc(stats_ready, 1)
                    dve.wait_ge(scales_ready, b * NORMS + use + 1)

                def normed_rows(src):
                    for t in range(NT):
                        nc.vector.tensor_scalar(rows[:, t, :], src[:, t, :], mv[:, t, 0:1], scale[:, t:t + 1],
                                                ALU.subtract, ALU.mult).then_inc(rows_ready, 1)

                def add_projection(use, src, dst, norm):
                    for t in range(NT):
                        dve.wait_ge(proj_done, b * (PROJS * NT) + use * NT + t + 1)
                        nc.vector.tensor_tensor(dst[:, t, :], src[:, t, :], ps[:, t % 4, 0:D], ALU.add).then_inc(proj_added, 1)
                        if t >= 1:
                            dve.wait_ge(proj_added, b * (PROJS * NT) + use * NT + t)
                            nc.vector.bn_stats(stats[:, t - 1, :], dst[:, t - 1, :])
                    dve.wait_ge(proj_added, b * (PROJS * NT) + (use + 1) * NT)
                    finish_stats(nc.vector.bn_stats(stats[:, NT - 1, :], dst[:, NT - 1, :]), norm)

                dve.wait_ge(x_in, b * 16 + 16)
                row_stats(xin, NORM_SELF)
                dve.wait_ge(rows_free, b * 16 + 16)
                dve.wait_ge(xres_free, b * 16 + 16)
                normed_rows(xin)

                def tile_max(h, par, t):
                    n = (t + 1) * P
                    buf = 2 * (t % 2)
                    dve.wait_ge(scores_done, b * (HEADS * NT) + h * NT + t + 1)
                    nc.vector.tensor_reduce(neg_max[:, par, t:t + 1],
                                            ps[:, buf:buf + 2, :].rearrange("p a n -> p (a n)")[:, 0:n],
                                            AX.X, ALU.max, negate=True).then_inc(max_done, 1)

                def tile_inv(h, par, t):
                    dve.wait_ge(exp_done, b * (HEADS * NT) + h * NT + t + 1)
                    nc.vector.reciprocal(inv_sum[:, par, t:t + 1], row_sum[:, par, t:t + 1]).then_inc(inv_done, 1)

                def tile_norm(h, par, t):
                    n = (t + 1) * P
                    dve.wait_ge(inv_done, b * (HEADS * NT) + h * NT + t + 1)
                    nc.vector.tensor_scalar(probs[par][:, TRI[t]:TRI[t] + n], probs[par][:, TRI[t]:TRI[t] + n],
                                            inv_sum[:, par, t:t + 1], None, ALU.mult).then_inc(probs_done, 1)

                def take_out(h, g):
                    dve.wait_ge(pv_done, b * (HEADS * 12) + h * 12 + (4 if g == 0 else 12))
                    dve.wait_ge(consts_made, MADE)
                    nc.vector.tensor_copy(attn_t[:, h, g * BANK:(g + 1) * BANK] if isinstance(h, int) else
                                          attn_t[:, bass.ds(h, 1), g * BANK:(g + 1) * BANK].rearrange("p o n -> p (o n)"),
                                          ps[:, 6 + g, :]).then_inc(out_taken, 1)

                def head(h, par, before):
                    for t in range(NT):
                        tile_max(h, par, t)
                        if t > 0:
                            tile_inv(h, par, t - 1)
                            tile_norm(h, par, t - 1)
                        if before is not None and t == 5:
                            take_out(before, 0)
                    tile_inv(h, par, NT - 1)
                    tile_norm(h, par, NT - 1)
                    if before is not None:
                        take_out(before, 1)

                head(0, 0, None)
                with dve.Fori(0, HEADS // 2 - 1) as i:
                    for u in range(2):
                        head(i * 2 + u + 1, (u + 1) % 2, i * 2 + u)
                head(HEADS - 1, (HEADS - 1) % 2, HEADS - 2)
                take_out(HEADS - 1, 0)
                take_out(HEADS - 1, 1)
                add_projection(PROJ_SELF, xin, xres, NORM_CROSS)

                normed_rows(xres)
                dve.wait_ge(ctx_in, b * 32 + 32)
                nc.vector.tensor_scalar(mask_row[:], mask_u8[:].unsqueeze(1).to_broadcast([1, GROUP, CTX]),
                                        -1.0, -MASKED, ALU.add, ALU.mult).then_inc(mask_made, 1)
                for m in range(KT):
                    dve.wait_ge(xkv_done, b * 3 + m + 1)
                    for h in range(NT):
                        last = nc.vector.tensor_scalar(xk_blocks[:, m, h, :], ps[:, m, 0:CTX], bk[:, m:m + 1],
                                                       head_rows[:, h:h + 1], ALU.add, ALU.mult)
                    last.then_inc(xkv_taken, 1)
                dve.wait_ge(xkv_done, b * 3 + 3)
                nc.vector.tensor_tensor(xv[:, :, 0:XHD], ps[0:CTX, 2, 0:D].rearrange("p (h e) -> p h e", h=XHEADS),
                                        bv[:].rearrange("p (h e) -> p h e", h=XHEADS), ALU.add).then_inc(xkv_taken, 1)
                for i in range(4):
                    n, m = divmod(i, KT)
                    dve.wait_ge(xq_done, b * 4 + i + 1)
                    nc.vector.tensor_scalar(xq_t[:, m, n * BANK:(n + 1) * BANK], ps[:, i, :], bq[:, m:m + 1],
                                            float(XHD) ** -0.5, ALU.add, ALU.mult).then_inc(xq_taken, 1)

                def cross_out(c):
                    for j in range(NG):
                        dve.wait_ge(xpv_done, b * (2 * NG) + NG * c + j + 1)
                        nc.vector.tensor_copy(xout_t[:, j, c * BANK:(c + 1) * BANK], ps[:, 6 + j % 2, :]).then_inc(xpv_taken, 1)

                for u in range(2 * NT):
                    t, half = divmod(u, 2)
                    s4 = ps[:, 2 * half:2 * half + 2, 0:GROUP * CTX].rearrange("p j (h c) -> p j h c", h=GROUP)
                    neg = xneg[half].rearrange("p (j h) -> p j h", j=2)
                    dve.wait_ge(xs_done, b * (2 * NT) + u + 1)
                    nc.vector.tensor_reduce(neg, s4, AX.X, ALU.max, negate=True).then_inc(xneg_done, 1)
                    if t >= 2:
                        dve.wait_ge(xpt_done, b * (NT * NG) + NG * (t - 2) + 2 * half + 2)
                    dve.wait_ge(xneg_done, b * (2 * NT) + u + 1)
                    nc.vector.tensor_tensor(xs[t % 2][:, 8 * half:8 * half + 8, :].rearrange("p (j h) c -> p j h c", j=2), s4,
                                            neg.unsqueeze(3).to_broadcast([P, 2, GROUP, CTX]), ALU.add).then_inc(xs_taken, 1)
                    if u == 9:
                        cross_out(0)
                cross_out(1)

                def back_rows(use, inv):
                    for t in range(NT):
                        heads = ps[:, t % 2, :].rearrange("p (h e) -> p h e", e=SLOT)
                        dve.wait_ge(back_done, b * (2 * NT) + use * NT + t + 1)
                        nc.vector.reciprocal(inv[:, t, :], heads[:, :, XHD]).then_inc(dve_step, 1)
                        dve.wait_ge(dve_step, step())
                        nc.vector.tensor_tensor(rows[:, t, :].rearrange("p (h e) -> p h e", e=XHD), heads[:, :, 0:XHD],
                                                inv[:, t, :].unsqueeze(2).to_broadcast([P, XHEADS, XHD]),
                                                ALU.mult).then_inc(rows_ready, 1)

                back_rows(0, xinv)
                add_projection(PROJ_CROSS, xres, xres, NORM_LATENT)

                dve.wait_ge(zeros_out, 16)
                for t in range(NT):
                    last = nc.vector.tensor_scalar(xp[:, t, :], xres[:, t, :], mv[:, t, 0:1], scale[:, t:t + 1],
                                                   ALU.subtract, ALU.mult)
                last.then_inc(dve_step, 1)
                dve.wait_ge(dve_step, step())
                for t in range(NT):
                    nc.vector.tensor_scalar(rows[:, t, :], xp[:, t, :], scale2[:, t:t + 1], None, ALU.mult).then_inc(rows_ready, 1)

                def rope(dst, src, table, t):
                    x = src.rearrange("p (h e) -> p h e", h=MHEADS)
                    y = dst[:, t, :].rearrange("p (h e) -> p h e", h=MHEADS)
                    half = MHD // 2
                    cos = table[:, t, 0:MHD].unsqueeze(1).to_broadcast([P, MHEADS, MHD])
                    u = rope_tmp.rearrange("p (h e) -> p h e", h=MHEADS)
                    nc.vector.tensor_tensor(y, x, cos, ALU.mult).then_inc(dve_step, 1)
                    for a in range(2):
                        sin = table[:, t, MHD + a * half:MHD + (a + 1) * half].unsqueeze(1).to_broadcast([P, MHEADS, half])
                        nc.vector.tensor_tensor(u[:, :, a * half:(a + 1) * half], x[:, :, (1 - a) * half:(2 - a) * half], sin,
                                                ALU.mult).then_inc(dve_step, 1)
                    dve.wait_ge(dve_step, step(3))

                rope_tmp = q_rest[:, 0, :, :].rearrange("p h e -> p (h e)")
                for t in range(NT):
                    dve.wait_ge(mq_done, b * NT + t + 1)
                    rope(q_rope, ps[:, t % 4, 0:D], rope_q, t)
                    nc.vector.tensor_tensor(q_rope[:, t, :], q_rope[:, t, :], rope_tmp, ALU.add).then_inc(mq_taken, 1)
                    dve.wait_ge(mq_taken, b * NT + t + 1)
                dve.wait_ge(mlat_taken, b * NT + NT)
                row_stats(lat_rows, NORM_KV)
                for t in range(NT):
                    nc.vector.tensor_scalar(lat_rows[:, t, :], lat_rows[:, t, :], mv[:, t, 0:1], scale[:, t:t + 1],
                                            ALU.subtract, ALU.mult).then_inc(lat_ready, 1)
                for t in range(NT):
                    dve.wait_ge(mkv_done, b * NT + t + 1)
                    rope(k_rope, ps[:, t % 4, 0:D], rope_k, t)
                    nc.vector.tensor_tensor(k_rope[:, t, :], k_rope[:, t, :], rope_tmp, ALU.add).then_inc(mk_taken, 1)
                    dve.wait_ge(mk_taken, b * NT + t + 1)
                def split_queries(t):
                    s = t % 2
                    qr = q_rope[:, t, :].rearrange("p (h e) -> p h e", h=MHEADS)
                    qs = q_stack[s].rearrange("p h (c e) -> p h c e", e=MHD)
                    dve.wait_ge(q_high, b * NT + t + 1)
                    nc.vector.tensor_tensor(q_rest[:, s, :, :], qr, qs[:, :, 0, :], ALU.subtract).then_inc(q_rest_done, 1)
                    dve.wait_ge(q_rest_done, b * (2 * NT) + 2 * t + 1)
                    dve.wait_ge(consts_made, MADE)
                    nc.vector.tensor_copy(qs[:, :, 3:5, :], q_rest[:, s, :, :].unsqueeze(2).to_broadcast([P, MHEADS, 2, MHD])).then_inc(q_rest_done, 1)
                    dve.wait_ge(q_rest_done, b * (2 * NT) + 2 * t + 2)
                    nc.vector.tensor_tensor(qs[:, :, 5, :], q_rest[:, s, :, :], qs[:, :, 3, :], ALU.subtract).then_inc(q_split, 1)

                def max_chunk(g, u):
                    j, t, c = (FIRST_CHUNKS if isinstance(g, int) and g == 0 else MAX_CHUNKS)[u]
                    n = min(BANK, (t + 1) * P - c * BANK)
                    dve.wait_ge(ms_done, b * (NG * 48) + g * 48 + u + 1)
                    nc.vector.tensor_reduce(max_part[:, j, t, c:c + 1], ps[:, u % 3, 0:n], AX.X, ALU.max).then_inc(ms_taken, 1)

                def stack_max(g):
                    dve.wait_ge(ms_taken, b * (NG * 48) + g * 48 + 48)
                    first = b * (NG * 6) + g * 6
                    top = max_part
                    neg = max_neg.rearrange("p t j -> p j t")
                    rest = max_rest.rearrange("p t j -> p j t")
                    nc.vector.tensor_scalar(neg[:, :, 0:4], top[:, :, 0:4, 0], -1.0, None, ALU.mult).then_inc(mmax_step, 1)
                    nc.vector.tensor_reduce(neg[:, :, 4:NT], top[:, :, 4:NT, :], AX.X, ALU.max, negate=True).then_inc(mmax_step, 1)
                    dve.wait_ge(mmax_step, first + 2)
                    dve.wait_ge(consts_made, MADE)
                    nc.vector.tensor_copy(max_stack[:, :, :, 0], max_neg).then_inc(mmax_step, 1)
                    dve.wait_ge(mmax_step, first + 3)
                    nc.vector.tensor_tensor(max_rest, max_neg, max_stack[:, :, :, 0], ALU.subtract).then_inc(mmax_step, 1)
                    dve.wait_ge(mmax_step, first + 4)
                    dve.wait_ge(consts_made, MADE)
                    nc.vector.tensor_copy(max_stack[:, :, :, 1], max_rest).then_inc(mmax_step, 1)
                    dve.wait_ge(mmax_step, first + 5)
                    nc.vector.tensor_tensor(max_stack[:, :, :, 2], max_rest, max_stack[:, :, :, 1], ALU.subtract).then_inc(mmax_step, 1)
                    for j in range(GROUP):
                        dve.wait_ge(mx_turned, b * (NG * GROUP) + g * GROUP + j + 1)
                        dve.wait_ge(consts_made, MADE)
                        head_at = g * GROUP + j
                        dst = q_stack_t[P - SLOT:P, head_at, :] if isinstance(g, int) else \
                            q_stack_t[P - SLOT:P, bass.ds(head_at, 1), :].rearrange("p o n -> p (o n)")
                        nc.vector.tensor_copy(dst, ps[P - SLOT:P, j % 3, :].bitcast(BF16)).then_inc(mx_taken, 1)

                def group_out(g):
                    for c in range(2):
                        dve.wait_ge(mpv_done, b * (NG * NT) + g * NT + NT)
                        dve.wait_ge(consts_made, MADE)
                        dst = mout_t[:, g, c * BANK:(c + 1) * BANK] if isinstance(g, int) else \
                            mout_t[:, bass.ds(g, 1), c * BANK:(c + 1) * BANK].rearrange("p o n -> p (o n)")
                        nc.vector.tensor_copy(dst, ps[:, 6 + c, :]).then_inc(mout_taken, 1)

                split_queries(0)
                for t in range(NT + 1):
                    if t + 1 < NT:
                        split_queries(t + 1)
                    if t < NT:
                        for i in range(2):
                            dve.wait_ge(qs_turned, b * (2 * NT) + 2 * t + i + 1)
                            nc.vector.tensor_copy(q_stack_t[:, 8 * i:8 * i + 8, t * P:(t + 1) * P],
                                                  ps[:, 4 + i, :].bitcast(BF16).rearrange("p (h n) -> p h n", h=8)).then_inc(qs_taken, 1)
                    for u, chunk in enumerate(FIRST_CHUNKS):
                        if chunk[1] == t - 1:
                            max_chunk(0, u)
                stack_max(0)
                with dve.Fori(0, NG - 1) as g:
                    for u in range(48):
                        max_chunk(g + 1, u)
                    group_out(g)
                    stack_max(g + 1)
                group_out(NG - 1)

                back_rows(1, minv)
                add_projection(PROJ_LATENT, xp, xp, NORM_GATE)

                for t in range(NT):
                    nc.vector.scalar_tensor_tensor(rows[:, t, :], xp[:, t, :], scale[:, t:t + 1], norm2[:], ALU.mult,
                                                   ALU.mult).then_inc(rows_ready, 1)
                for t in range(NT):
                    last = nc.vector.tensor_tensor(xres[:, t, :], xres[:, t, :], xp[:, t, :], ALU.add)
                last.then_inc(resid_ready, 1)
                dve.wait_ge(gate_done, b + 1)
                nc.vector.tensor_tensor(logits[:, bass.ds(b * NT, NT), :],
                                        ps[:, 0, 0:NT * EXPERTS].rearrange("p (t e) -> p t e", t=NT),
                                        gate_b[:].unsqueeze(1).to_broadcast([P, NT, EXPERTS]), ALU.add).then_inc(logits_done, 1)
                assert step.n == DVE_STEPS, ("DVE_STEPS", step.n)

            route = Count()
            dve.wait_ge(logits_done, BATCH)
            nc.vector.tensor_reduce(best, logits[:], AX.X, ALU.max).then_inc(route_step, 1)
            dve.wait_ge(route_step, route())
            nc.vector.tensor_tensor(logits[:], logits[:], best.unsqueeze(2).to_broadcast([P, ROW_TILES, EXPERTS]),
                                    ALU.is_equal).then_inc(route_step, 1)
            dve.wait_ge(route_step, route())
            nc.vector.tensor_copy(onehot[:, :, 0], logits[:, :, 0]).then_inc(route_step, 1)
            nc.vector.tensor_copy(best, logits[:, :, 0]).then_inc(route_step, 1)
            dve.wait_ge(route_step, route(2))
            for e in range(1, EXPERTS):
                nc.vector.tensor_tensor(onehot[:, :, e], logits[:, :, e], best, ALU.is_gt).then_inc(route_step, 1)
                nc.vector.tensor_tensor(best, best, logits[:, :, e], ALU.max).then_inc(route_step, 1)
                dve.wait_ge(route_step, route(2))
            nc.vector.tensor_copy(onehot_b, onehot).then_inc(counts_ready, 1)
            dve.wait_ge(counts_done, 2)
            nc.vector.tensor_copy(cum[0].rearrange("p t e -> p (t e)"), ps[:, 2, 0:ROW_TILES * EXPERTS]).then_inc(route_step, 1)
            dve.wait_ge(route_step, route())
            cur, shift = 0, 1
            while shift < ROW_TILES:
                nc.vector.tensor_copy(cum[1 - cur][:, 0:shift, :], cum[cur][:, 0:shift, :]).then_inc(route_step, 1)
                nc.vector.tensor_tensor(cum[1 - cur][:, shift:, :], cum[cur][:, shift:, :], cum[cur][:, 0:ROW_TILES - shift, :],
                                        ALU.add).then_inc(route_step, 1)
                dve.wait_ge(route_step, route(2))
                cur, shift = 1 - cur, 2 * shift
            total, other = cum[cur], cum[1 - cur]
            nc.vector.tensor_scalar(e_more[:, 0, :], tile_at[:, 0:ROW_TILES], float(P), None, ALU.mult).then_inc(route_step, 1)
            dve.wait_ge(route_step, route())
            for e in range(EXPERTS - 1, -1, -1):
                nc.vector.tensor_scalar(e_more[:, e, :], e_more[:, 0, :], total[:, ROW_TILES - 1, e:e + 1], None,
                                        ALU.is_lt).then_inc(route_step, 1)
                dve.wait_ge(route_step, route())
            nc.vector.tensor_reduce(e_tiles, e_more[:], AX.X, ALU.add).then_inc(route_step, 1)
            nc.vector.memset(e_start, 0.0).then_inc(route_step, 1)
            dve.wait_ge(route_step, route(2))
            for e in range(1, EXPERTS):
                nc.vector.tensor_tensor(e_start[:, e:e + 1], e_start[:, e - 1:e], e_tiles[:, e - 1:e], ALU.add).then_inc(route_step, 1)
                dve.wait_ge(route_step, route())
            nc.vector.tensor_scalar(tile_e, tile_at[:], e_start[:, 1:2], None, ALU.is_ge).then_inc(route_step, 1)
            dve.wait_ge(route_step, route())
            for e in range(2, EXPERTS):
                nc.vector.scalar_tensor_tensor(tile_e, tile_at[:], e_start[:, e:e + 1], tile_e, ALU.is_ge, ALU.add).then_inc(route_step, 1)
                dve.wait_ge(route_step, route())
            nc.vector.tensor_copy(tile_ei, tile_e).then_inc(route_step, 1)
            nc.vector.tensor_tensor(other.rearrange("p t e -> p (t e)"), total.rearrange("p t e -> p (t e)"),
                                    ps[:, 2, 0:ROW_TILES * EXPERTS], ALU.subtract).then_inc(route_step, 1)
            dve.wait_ge(route_step, route(2))
            nc.vector.tensor_tensor(other.rearrange("p t e -> p (t e)"), other.rearrange("p t e -> p (t e)"),
                                    ps[:, 1, 0:ROW_TILES * EXPERTS], ALU.add).then_inc(route_step, 1)
            nc.vector.tensor_scalar(e_tiles, e_start, float(P), None, ALU.mult).then_inc(route_step, 1)
            dve.wait_ge(route_step, route(2))
            nc.vector.tensor_tensor(other, other, e_tiles.unsqueeze(1).to_broadcast([P, ROW_TILES, EXPERTS]),
                                    ALU.add).then_inc(route_step, 1)
            dve.wait_ge(route_step, route())
            nc.vector.tensor_tensor(other, other, onehot, ALU.mult).then_inc(route_step, 1)
            dve.wait_ge(route_step, route())
            nc.vector.tensor_reduce(dest_f, other, AX.X, ALU.add).then_inc(route_step, 1)
            dve.wait_ge(route_step, route())
            nc.vector.tensor_copy(dest, dest_f).then_inc(route_ready, 1)

            dve.wait_ge(route_ready, 1)
            dve.wait_ge(moe_w_in, 64)

            def take_h(j, par):
                e = dve.value_load(tile_ei[0:1, bass.ds(j, 1)], min_val=0, max_val=EXPERTS - 1)
                for n in range(2):
                    dve.wait_ge(eh_done, j * 2 + n + 1)
                    if not isinstance(j, int) or j >= 2:
                        dve.wait_ge(eh_turned, j * 2 - 2)
                    nc.vector.tensor_tensor(h_rows[par][:, n * BANK:(n + 1) * BANK], ps[:, 1 + 2 * par + n, :],
                                            b1[:, bass.ds(e * HID + n * BANK, BANK)], ALU.add).then_inc(eh_taken, 1)

            def take_y(j, par, pairs):
                e = dve.value_load(tile_ei[0:1, bass.ds(j, 1)], min_val=0, max_val=EXPERTS - 1)
                dve.wait_ge(ey_done, j + 1)
                if not isinstance(j, int) or j >= 2:
                    dve.wait_ge(ey_out[par], pairs * 16)
                nc.vector.tensor_tensor(y_rows[par], ps[:, 7, 0:D], b2[:, bass.ds(e * D, D)], ALU.add).then_inc(ey_taken, 1)

            take_h(0, 0)
            take_h(1, 1)
            take_y(0, 0, 0)
            take_h(2, 0)
            take_y(1, 1, 0)
            with dve.Fori(1, MOE_TILES // 2 - 1) as i:
                take_h(i * 2 + 1, 1)
                take_y(i * 2, 0, i)
                take_h(i * 2 + 2, 0)
                take_y(i * 2 + 1, 1, i)
            take_h(MOE_TILES - 1, 1)
            take_y(MOE_TILES - 2, 0, MOE_TILES // 2 - 1)
            take_y(MOE_TILES - 1, 1, MOE_TILES // 2 - 1)

            dve.wait_ge(gathered, 16 * ROW_TILES)
            with dve.Fori(0, BATCH) as b:
                dve.wait_ge(resid_in, b * 16 + 16)
                for t in range(NT):
                    nc.vector.tensor_tensor(xres[:, t, :], xres[:, t, :],
                                            moe_rows[:, bass.ds(b * NT + t, 1), :].rearrange("p o n -> p (o n)"),
                                            ALU.add).then_inc(fin_ready, 1)


def arrange(x, ctx_1024, mask_Bx1xS2_bf1, L0_attn_gamma, L0_attn_w_qkv, L0_attn_w_out, L0_xattn_Wk, L0_xattn_bk,
            L0_xattn_Wv, L0_xattn_bv, L0_xattn_Wq, L0_xattn_bq, L0_xattn_Wo, L0_xattn_bo, L0_ffn_norm1_w,
            L0_ffn_norm2_w, L0_ffn_Wq, L0_ffn_Wdkv, L0_ffn_Wuk, L0_ffn_Wuv, L0_ffn_Wo, L0_ffn_ln_g, L0_ffn_ln_b,
            L0_ffn_gate_w, L0_ffn_gate_b, L0_ffn_W1, L0_ffn_b1, L0_ffn_W2, L0_ffn_b2):
    def bf16_bits(a):
        return (np.ascontiguousarray(a, np.float32).view(np.uint32) >> 16).astype(np.uint16)

    def by_partition(w):
        return w.reshape(-1, P, w.shape[1]).transpose(1, 0, 2)

    a = {
        "x": x,
        "ctx": ctx_1024.transpose(0, 2, 1).reshape(BATCH, KT, P, CTX).transpose(0, 2, 1, 3),
        "mask": mask_Bx1xS2_bf1.view(np.uint8),
        "gamma": L0_attn_gamma.reshape(KT, P).T,
        "norm1": L0_ffn_norm1_w.reshape(KT, P).T,
        "lat_gb": np.stack([L0_ffn_ln_g, L0_ffn_ln_b], 1),
        "bq": L0_xattn_bq.reshape(KT, P).T,
        "bk": L0_xattn_bk.reshape(KT, P).T,
        "bv": np.tile(L0_xattn_bv, (CTX, 1)),
        "bo": L0_xattn_bo.reshape(1, D),
        "norm2": np.tile(L0_ffn_norm2_w, (P, 1)),
        "gate_b": np.tile(L0_ffn_gate_b, (P, 1)),
        "b2": L0_ffn_b2.reshape(1, -1),
        "b1": L0_ffn_b1.reshape(1, -1),
        "w_qkv": L0_attn_w_qkv.reshape(3, HEADS, HD, KT, P).transpose(1, 4, 3, 0, 2).reshape(HEADS, P, KT * 3 * HD),
        "w_out": by_partition(L0_attn_w_out.T),
        "xw_q": by_partition(L0_xattn_Wq.T),
        "xw_k": by_partition(L0_xattn_Wk.T),
        "xw_v": by_partition(L0_xattn_Wv.T),
        "xw_o": by_partition(L0_xattn_Wo.T),
        "mw_qd": by_partition(np.concatenate([L0_ffn_Wq, L0_ffn_Wdkv]).T),
        "mw_kv": np.concatenate([L0_ffn_Wuk, L0_ffn_Wuv]).T,
        "mw_o": by_partition(L0_ffn_Wo.T),
        "w_gate": by_partition(L0_ffn_gate_w.T),
        "w1": by_partition(L0_ffn_W1.reshape(EXPERTS * HID, D).T),
        "w2": by_partition(L0_ffn_W2.transpose(0, 2, 1).reshape(EXPERTS * HID, D)),
    }
    half = MHD // 2
    freq = (1.0 / np.float32(10000.0) ** (np.arange(half, dtype=np.float32) / np.float32(half))).astype(np.float32)
    ang = np.arange(T, dtype=np.float32)[:, None] * freq[None, :]
    sin, cos = np.sin(ang), np.cos(ang)
    table = np.concatenate([cos, cos, -sin, sin], 1).astype(np.float32).reshape(NT, P, 2 * MHD).transpose(1, 0, 2)
    upper = np.triu(np.full((P, P), MASKED, np.float32), 1)
    a |= {
        "ident": np.eye(P, dtype=np.float32),
        "ident_b": bf16_bits(np.eye(P)),
        "causal_b": bf16_bits(upper),
        "causal_t_b": bf16_bits(upper.T),
        "before_b": bf16_bits(np.triu(np.ones((P, P)), 1)),
        "head_rows": np.kron(np.eye(NT, dtype=np.float32), np.ones((XHD, 1), np.float32)),
        "rope_q": table * np.float32(MHD ** -0.5),
        "rope_k": table,
        "tile_at": np.tile(np.arange(MOE_TILES, dtype=np.float32), (P, 1)),
    }
    return {k: np.ascontiguousarray(v) for k, v in a.items()}


def kernel(**inputs):
    import concourse.bacc as bacc
    from concourse.bass_utils import run_bass_kernel_spmd

    arrays = arrange(**{k: np.asarray(v) for k, v in inputs.items()})
    nc = bacc.Bacc("TRN2", target_bir_lowering=False, num_devices=1)
    d = {k: nc.dram_tensor("in_" + k, a.shape, mybir.dt.from_np(a.dtype), kind="ExternalInput").ap()
         for k, a in arrays.items()}
    d["out"] = nc.dram_tensor("out", (BATCH, T, D), F32, kind="ExternalOutput").ap()
    for name, shape in (("gate_rows", (BATCH, T, D)), ("resid", (BATCH, T, D)),
                        ("sorted_rows", (MOE_TILES * P, D)), ("sorted_out", (MOE_TILES * P, D))):
        d[name] = nc.dram_tensor(name, shape, F32, kind="Internal").ap()
    decoder_block(nc, d)
    r = run_bass_kernel_spmd(nc, [{"in_" + k: a for k, a in arrays.items()}], core_ids=[0])
    return r.results[0]["out"]
```

```python
from contextlib import ExitStack

import numpy as np

import concourse.bass as bass
from concourse import mybir

F32 = mybir.dt.float32
BF16 = mybir.dt.bfloat16
I32 = mybir.dt.int32
U32 = mybir.dt.uint32
U8 = mybir.dt.uint8
U16 = mybir.dt.uint16
ALU = mybir.AluOpType
ACT = mybir.ActivationFunctionType
AX = mybir.AxisListType

P = 128
BATCH, T, D = 4, 1024, 256
NT = T // P
KT = D // P
BANK = 512
HEADS, HD = 8, 128
XHEADS, XHD, CTX = 16, 16, 77
MHEADS, MHD, LAT = 16, 16, 128
GROUP = 4
NG = MHEADS // GROUP
SLOT = 32
EXPERTS, HID = 4, 1024
ROW_TILES = BATCH * NT
MOE_TILES = ROW_TILES + EXPERTS
HK = HID // P
MASKED = -3.0e38
LIST = BATCH * T + P
SLOTS = 4
TRI = [P * t * (t + 1) // 2 for t in range(NT + 1)]

TURN_SELF, TURN_CROSS, TURN_CROSS_OUT, TURN_LATENT, TURN_NEXT, TURN_LATENT_OUT, TURN_GATE = range(7)
TURNS = 6
PROJ_SELF, PROJ_CROSS, PROJ_LATENT = range(3)
PROJS = 3
NORM_SELF, NORM_CROSS, NORM_LATENT, NORM_KV, NORM_NEXT, NORM_GATE = range(6)
NORMS = 5
HALF = NT // 2


def norm_count(b, use, half):
    return b * (2 * NORMS) + 2 * use + half + 1


MAX_CHUNKS = [(j, t, c) for j in range(GROUP) for t in range(NT) for c in range(t // 4 + 1)]
FIRST_CHUNKS = sorted(MAX_CHUNKS, key=lambda x: (x[1], x[0], x[2]))
CHUNKS = len(MAX_CHUNKS)


class Count:

    def __init__(self, base=0):
        self.base, self.n = base, 0

    def __call__(self, more=1):
        self.n += more
        return self.base + self.n


DVE_STEPS, POOL_STEPS, ROUTE_STEPS = 76, 43, 16


def decoder_block(nc, d):
    with ExitStack() as ctx:
        def sb(name, shape, dt=F32):
            return ctx.enter_context(nc.sbuf_tensor(name, shape, dt))

        def sem(name):
            return ctx.enter_context(nc.semaphore(name))

        ident = sb("ident", [P, P])
        ident_b = sb("ident_b", [P, P], BF16)
        causal_b = sb("causal_b", [P, P], BF16)
        causal_t_b = sb("causal_t_b", [P, P], BF16)
        before_b = sb("before_b", [P, P], BF16)
        ones_b = sb("ones_b", [P, P], BF16)
        ones_f = sb("ones_f", [1, P])
        gamma = sb("gamma", [P, KT])
        norm1 = sb("norm1", [P, KT])
        lat_gb = sb("lat_gb", [P, 2])
        bq = sb("bq", [P, KT])
        bk = sb("bk", [P, KT])
        bv = sb("bv", [CTX, D])
        bo = sb("bo", [1, D])
        norm2 = sb("norm2", [P, D])
        gate_b = sb("gate_b", [P, EXPERTS])
        head_rows = sb("head_rows", [P, NT])
        rope_q = sb("rope_q", [P, NT, 2 * MHD])
        rope_k = sb("rope_k", [P, NT, 2 * MHD])
        tile_at = sb("tile_at", [P, MOE_TILES])
        list_at = sb("list_at", [P, EXPERTS])
        pad_id = sb("pad_id", [P, 1])
        w_out = sb("w_out", [P, HEADS, D])
        xw_q = sb("xw_q", [P, KT, D])
        xw_k = sb("xw_k", [P, KT, D])
        xw_v = sb("xw_v", [P, KT, D])
        xw_o = sb("xw_o", [P, KT, D])
        mw_qd = sb("mw_qd", [P, KT, D + LAT])
        mw_kv = sb("mw_kv", [P, 2 * D])
        mw_o = sb("mw_o", [P, KT, D])
        w_gate = sb("w_gate", [P, KT, EXPERTS])
        first_consts = [(ident, "ident"), (gamma, "gamma"), (ident_b, "ident_b"), (causal_b, "causal_b")]
        consts = [
            (causal_t_b, "causal_t_b"), (before_b, "before_b"), (norm1, "norm1"), (lat_gb, "lat_gb"), (bq, "bq"),
            (bk, "bk"), (bv, "bv"), (bo, "bo"), (norm2, "norm2"), (gate_b, "gate_b"),
            (head_rows, "head_rows"), (rope_q, "rope_q"), (rope_k, "rope_k"), (tile_at, "tile_at"), (list_at, "list_at"),
            (pad_id, "pad_id"),
            (w_out, "w_out"), (xw_q, "xw_q"), (xw_k, "xw_k"), (xw_v, "xw_v"), (xw_o, "xw_o"),
            (mw_qd, "mw_qd"), (mw_kv, "mw_kv"), (mw_o, "mw_o"), (w_gate, "w_gate"),
        ]
        SCATTERS = 16 * 2 * NT
        FIRST_CONSTS, CONSTS = 16 * len(first_consts), 16 * (len(consts) + 1)
        MADE = 13

        xin = sb("xin", [P, NT, D])
        xres_ids = sb("xres_ids", [P, NT, D + 2])
        xres = xres_ids[:, :, 0:D]
        xp = sb("xp", [P, NT, D])
        rows = sb("rows", [P, NT, D])
        turned_t = sb("turned_t", [P, KT, T])
        stats = sb("stats", [P, NT, 6])
        mv = sb("mv", [P, NT, 2])
        scale = sb("scale", [P, NT])
        scale2 = sb("scale2", [P, NT])
        tmp1 = sb("tmp1", [P, NT])
        tmp2 = sb("tmp2", [P, NT])
        pause = sb("pause", [P, 1])
        pool_pause = sb("pool_pause", [P, NT])
        lists_pause = sb("lists_pause", [P, NT])
        c_eps5 = sb("c_eps5", [P, NT])
        c_eps6 = sb("c_eps6", [P, NT])
        c_nhalf = sb("c_nhalf", [P, NT])
        c_half = sb("c_half", [P, NT])
        c_neg1 = sb("c_neg1", [P, NT])
        c_root = sb("c_root", [P, NT])
        logits = sb("logits", [P, NT, EXPERTS])
        list_end = sb("list_end", [P, EXPERTS])
        out_row = [sb(f"out_row{i}", [P, 1], U32) for i in range(2)]
        ctx_t = sb("ctx_t", [P, KT, CTX])
        mask_u8 = sb("mask_u8", [1, CTX], U8)
        mask_row = sb("mask_row", [1, GROUP, CTX], BF16)
        xv = sb("xv", [CTX, XHEADS, SLOT])
        mv_rows = sb("mv_rows", [P, NT, MHEADS, SLOT])
        neg_max = sb("neg_max", [P, 2, NT])
        row_sum = sb("row_sum", [P, 2, NT])
        inv_sum = sb("inv_sum", [P, 2, NT])

        ARENA = 29800
        arena = sb("arena", [P, ARENA])

        class Region:
            def __init__(self, at=0):
                self.at = at

            def __call__(self, *dims, dt=F32, rows=P):
                n = int(np.prod(dims))
                words = n // 2 if dt == BF16 else n
                ap = arena[0:rows, self.at:self.at + words]
                self.at += words
                assert self.at <= ARENA, self.at
                if dt != F32:
                    ap = ap.bitcast(dt)
                if len(dims) == 1:
                    return ap
                names = "abcd"[:len(dims)]
                return ap.rearrange(f"p ({' '.join(names)}) -> p {' '.join(names)}",
                                    **dict(zip(names[1:], dims[1:])))

        r = Region()
        attn_t = r(HEADS, T)
        q_t = [r(T) for _ in range(2)]
        k_t = [r(T) for _ in range(2)]
        v_rows = [r(NT, HD) for _ in range(2)]
        w_head = [r(KT, 3 * HD) for _ in range(2)]
        probs = [r(TRI[NT]) for _ in range(2)]
        probs_t = [r(BANK) for _ in range(4)]
        self_end = r.at
        r = Region()
        xprobs_t = r(XHEADS, BANK, rows=CTX)
        xout_t = r(NG, T)
        xq_t = r(KT, T)
        xs = [r(XHEADS, CTX) for _ in range(2)]
        xinv = r(NT, XHEADS)
        xneg = [r(XHEADS // 2) for _ in range(2)]
        r = Region()
        q_stack_t = r(MHEADS, T, dt=BF16)
        k_stack_t = r(MHEADS, T, dt=BF16)
        at = r.at
        lat_rows = r(NT, LAT)
        lat_t = r(T)
        q_rest = r(2, MHEADS, MHD)
        k_rest = r(2, MHEADS, MHD)
        r = Region(at)
        mout_t = r(NG, T)
        v_group = rows[:, 0:4, :].rearrange("p t (a n) -> p (t a) n", n=P)
        max_part = r(GROUP, NT, 2)
        max_neg = r(NT, GROUP)
        max_rest = r(NT, GROUP)
        max_stack = r(NT, GROUP, SLOT, dt=BF16)
        minv = r(NT, MHEADS)
        at = r.at
        q_rope = r(NT, D)
        k_rope = r(NT, D)
        q_stack = [r(MHEADS, P, dt=BF16) for _ in range(2)]
        k_stack = [r(MHEADS, P, dt=BF16) for _ in range(2)]
        r = Region(at)
        mprobs_t = [r(GROUP, T) for _ in range(2)]
        self_rows = Region()(NT, D)
        r = Region(self_end)
        xk_blocks = Region(r.at)(KT, NT, CTX)
        late_t = r(KT, T)
        best = r(NT)
        onehot = r(NT, EXPERTS)
        onehot_b = r(NT, EXPERTS, dt=BF16)
        cum = [r(NT, EXPERTS) for _ in range(2)]
        dest_f = r(NT)
        dest = r(NT, dt=U32)
        r = Region()
        w1 = r(KT, EXPERTS * HID)
        w2 = r(EXPERTS * HK, D)
        e_count = r(EXPERTS)
        e_more = r(EXPERTS, ROW_TILES)
        e_tiles = r(EXPERTS)
        e_start = r(EXPERTS)
        tile_e = r(MOE_TILES)
        tile_ei = r(MOE_TILES, dt=I32)
        tile_list = r(MOE_TILES)
        tile_of = r(EXPERTS, MOE_TILES)
        tile_place = r(EXPERTS, MOE_TILES)
        tile_row = r(MOE_TILES)
        tile_rowi = r(MOE_TILES, dt=I32)
        pad_rowi = r(EXPERTS, dt=I32)
        b1 = mv_rows[:].rearrange("p t h e -> p (t h e)")
        b2 = turned_t[:, 1, :]
        h_rows = [xp[:, 4 * i:4 * i + 4, :].rearrange("p t n -> p (t n)") for i in range(2)]
        h_t = [rows[:, 4 * i:4 * i + 4, :].rearrange("p t (a n) -> p (t a) n", n=P) for i in range(2)]
        xs_t = [turned_t[:, 0, KT * P * i:KT * P * (i + 1)].rearrange("p (a n) -> p a n", a=KT) for i in range(2)]
        xs_in = [xin[:, i, :] for i in range(SLOTS)]
        res_in = [xres_ids[:, i, :] for i in range(SLOTS)]
        y_rows = [xin[:, SLOTS + i, :] for i in range(2)]
        pad_row = xin[:, SLOTS + 2:SLOTS + 4, :].rearrange("p a n -> p (a n)")[:, 0:D + 2]

        def max_rows(head):
            if isinstance(head, int):
                return q_stack_t[P - SLOT:P, head, :]
            return q_stack_t[P - SLOT:P, bass.ds(head, 1), :].rearrange("p o n -> p (o n)")

        ps = ctx.enter_context(nc.psum_tensor("ps", [P, 8, BANK], F32))

        first_in = sem("first_in")
        consts_in = sem("consts_in")
        consts_made = sem("consts_made")
        x_in = sem("x_in")
        ctx_in = sem("ctx_in")
        w_in = [sem(f"w_in{i}") for i in range(2)]
        dve_step = sem("dve_step")
        pool_step = sem("pool_step")
        pool_paused = sem("pool_paused")
        act_step = sem("act_step")
        stats_ready = sem("stats_ready")
        scales_ready = sem("scales_ready")
        rows_ready = sem("rows_ready")
        turn_done = sem("turn_done")
        turn_taken = sem("turn_taken")
        qk_done = sem("qk_done")
        qk_taken = sem("qk_taken")
        v_done = sem("v_done")
        v_taken = sem("v_taken")
        scores_done = sem("scores_done")
        max_done = sem("max_done")
        exp_done = sem("exp_done")
        inv_done = sem("inv_done")
        probs_done = sem("probs_done")
        pt_done = sem("pt_done")
        pt_taken = sem("pt_taken")
        pv_done = sem("pv_done")
        out_taken = sem("out_taken")
        proj_done = sem("proj_done")
        proj_added = sem("proj_added")
        mask_made = sem("mask_made")
        xkv_done = sem("xkv_done")
        xkv_taken = sem("xkv_taken")
        xq_done = sem("xq_done")
        xq_taken = sem("xq_taken")
        xs_done = sem("xs_done")
        xs_taken = sem("xs_taken")
        xneg_done = sem("xneg_done")
        xexp_done = sem("xexp_done")
        xpt_done = sem("xpt_done")
        xpt_taken = sem("xpt_taken")
        xpv_done = sem("xpv_done")
        xpv_taken = sem("xpv_taken")
        back_done = sem("back_done")
        mq_done = sem("mq_done")
        mq_taken = sem("mq_taken")
        mlat_taken = sem("mlat_taken")
        lat_ready = sem("lat_ready")
        lat_turned = sem("lat_turned")
        lat_taken = sem("lat_taken")
        mkv_done = sem("mkv_done")
        mk_taken = sem("mk_taken")
        mv_taken = sem("mv_taken")
        q_high = sem("q_high")
        k_high = sem("k_high")
        q_split = sem("q_split")
        k_split = sem("k_split")
        q_rest_done = sem("q_rest_done")
        k_rest_done = sem("k_rest_done")
        qs_turned = sem("qs_turned")
        qs_taken = sem("qs_taken")
        ks_turned = sem("ks_turned")
        ks_taken = sem("ks_taken")
        ms_done = sem("ms_done")
        ms_taken = sem("ms_taken")
        mmax_step = sem("mmax_step")
        mx_turned = sem("mx_turned")
        mx_taken = sem("mx_taken")
        mx2_taken = sem("mx2_taken")
        mst_done = sem("mst_done")
        mexp_done = sem("mexp_done")
        vg_ready = sem("vg_ready")
        mpv_done = sem("mpv_done")
        mout_taken = sem("mout_taken")
        gate_done = sem("gate_done")
        logits_done = sem("logits_done")
        zeros_out = sem("zeros_out")
        moe_w_in = sem("moe_w_in")
        counts_ready = sem("counts_ready")
        counts_done = sem("counts_done")
        route_step = sem("route_step")
        route_ready = sem("route_ready")
        scattered = sem("scattered")
        lists_done = sem("lists_done")
        table_step = sem("table_step")
        tables_ready = sem("tables_ready")
        pads_out = sem("pads_out")
        et_in = [sem(f"et_in{i}") for i in range(SLOTS)]
        ex_turned = sem("ex_turned")
        ex_taken = sem("ex_taken")
        eh_done = sem("eh_done")
        eh_taken = sem("eh_taken")
        eh_turned = sem("eh_turned")
        ehT_taken = sem("ehT_taken")
        ey_done = sem("ey_done")
        ey_base = sem("ey_base")
        ey_taken = sem("ey_taken")
        ey_out = [sem(f"ey_out{i}") for i in range(2)]

        block = ctx.enter_context(nc.Block())

        @block.sync
        def _(sp):
            def load_head(h, slot):
                sp.dma_start(w_head[slot], d["w_qkv"][h].rearrange("p (a c) -> p a c", a=KT)).then_inc(w_in[slot], 16)

            def load_rows(row):
                sp.dma_start(xin[:], d["x"].rearrange("b t n -> (b t) n")[bass.ds(row, T), :].rearrange(
                    "(t p) n -> p t n", p=P)).then_inc(x_in, 16)

            load_rows(0)
            for tile, name in first_consts:
                sp.dma_start(tile[:].bitcast(U16) if tile.dtype == BF16 else tile[:], d[name]).then_inc(first_in, 16)
            load_head(0, 0)
            load_head(1, 1)
            for tile, name in consts:
                sp.dma_start(tile[:].bitcast(U16) if tile.dtype == BF16 else tile[:], d[name]).then_inc(consts_in, 16)
            sp.dma_start(xres_ids[:, :, D:D + 2], d["row_ids"]).then_inc(consts_in, 16)
            sp.wait_ge(consts_made, MADE)
            sp.dma_start(d["out"][BATCH * T:BATCH * T + 2 * P, :].rearrange("(a p) n -> p a n", p=P),
                         xp[:, 0:1, :].to_broadcast([P, 2, D])).then_inc(zeros_out, 16)

            def batch_io(b, next_row):
                sp.dma_start(ctx_t[:], d["ctx"][b]).then_inc(ctx_in, 16)
                sp.dma_start(mask_u8[:], d["mask"][b]).then_inc(ctx_in, 16)
                for h in range(2, HEADS):
                    sp.wait_ge(v_done, b * (2 * HEADS) + 2 * (h - 1))
                    load_head(h, h % 2)
                sp.wait_ge(proj_added, b * (PROJS * NT) + NT)
                load_rows(next_row)
                sp.wait_ge(turn_done, b * (4 * TURNS) + 4 * TURN_NEXT + 4)

            with sp.Fori(0, BATCH - 1) as b:
                batch_io(b, sp.snap(b * T + T))
                load_head(0, 0)
                load_head(1, 1)
            batch_io(BATCH - 1, 0)

            sp.wait_ge(vg_ready, BATCH * NG)
            sp.wait_ge(turn_taken, (BATCH - 1) * (4 * TURNS) + 4 * TURN_NEXT + 4)
            sp.dma_start(w1, d["w1"]).then_inc(moe_w_in, 16)
            sp.dma_start(w2, d["w2"]).then_inc(moe_w_in, 16)
            sp.dma_start(b1, d["b1"].partition_broadcast(P).rearrange("p o n -> p (o n)")).then_inc(moe_w_in, 16)
            sp.dma_start(b2, d["b2"].partition_broadcast(P).rearrange("p o n -> p (o n)")).then_inc(moe_w_in, 16)

            sp.wait_ge(tables_ready, 1)
            for e in range(EXPERTS):
                row = sp.value_load(pad_rowi[0:1, e:e + 1], min_val=0, max_val=EXPERTS * LIST - P)
                sp.dma_start(d["sorted_rows"][bass.ds(row, P), :], pad_row[:, 0:D]).then_inc(pads_out, 16)
                sp.dma_start(d["sorted_res"][bass.ds(row, P), :], pad_row).then_inc(pads_out, 16)
            sp.wait_ge(lists_done, BATCH + 1)
            sp.wait_ge(pads_out, 32 * EXPERTS)

            def tile_at_row(j):
                return sp.value_load(tile_rowi[0:1, bass.ds(j, 1)], min_val=0, max_val=EXPERTS * LIST - P)

            def load_tile(row, slot):
                sp.dma_start(xs_in[slot], d["sorted_rows"][bass.ds(row, P), :]).then_inc(et_in[slot], 16)
                sp.dma_start(res_in[slot], d["sorted_res"][bass.ds(row, P), :]).then_inc(et_in[slot], 16)

            for u in range(SLOTS):
                load_tile(tile_at_row(u), u)
            with sp.Fori(0, MOE_TILES // SLOTS - 1) as i:
                for u in range(SLOTS):
                    row = tile_at_row(i * SLOTS + u + SLOTS)
                    sp.wait_ge(ey_taken, i * SLOTS + u + 1)
                    load_tile(row, u)

        @block.gpsimd
        def _(pool):
            nc.gpsimd.memset(mv_rows[:], 0.0).then_inc(consts_made, 1)
            pool.wait_ge(consts_made, 1)
            nc.gpsimd.memset(mv_rows[:, :, :, MHD:MHD + 1], 1.0).then_inc(consts_made, 1)
            nc.gpsimd.memset(xv[:], 0.0).then_inc(consts_made, 1)
            pool.wait_ge(consts_made, 3)
            nc.gpsimd.memset(xv[:, :, XHD:XHD + 1], 1.0).then_inc(consts_made, 1)
            nc.gpsimd.memset(ones_b[:], 1.0).then_inc(consts_made, 1)
            nc.gpsimd.memset(ones_f[:], 1.0).then_inc(consts_made, 1)
            nc.gpsimd.memset(xp[:, 0, :], 0.0).then_inc(consts_made, 1)
            for tile, value in ((c_eps5, 1e-5), (c_eps6, 1e-6), (c_nhalf, -0.5), (c_half, 0.5), (c_neg1, -1.0),
                                (c_root, float(D) ** 0.5)):
                nc.gpsimd.memset(tile[:], value).then_inc(consts_made, 1)
            pool.wait_ge(consts_made, MADE)
            pool.sem_inc(lists_done, 1)

            def part(tile, half):
                return tile[:, HALF * half:HALF * (half + 1)]

            def combine(step, out, x, y, op):
                nc.gpsimd.tensor_tensor(out, x, y, op).then_inc(pool_step, 1)
                pool.wait_ge(pool_step, step())

            def self_scales(step, b, use):
                for h in range(2):
                    var, u, v, s2 = part(mv[:, :, 1], h), part(tmp1, h), part(tmp2, h), part(scale2, h)
                    pool.wait_ge(stats_ready, norm_count(b, use, h))
                    combine(step, u, var, part(c_eps5, h), ALU.add)
                    combine(step, s2, u, part(c_nhalf, h), ALU.pow)
                    combine(step, u, var, part(c_half, h), ALU.pow)
                    combine(step, v, u, s2, ALU.mult)
                    nc.gpsimd.tensor_tensor(pool_pause[:], c_half[:], c_half[:], ALU.add)
                    nc.gpsimd.tensor_scalar(u, v, float(D) ** 0.5, 1e-12, ALU.mult, ALU.max).then_inc(pool_step, 1)
                    pool.wait_ge(pool_step, step())
                    combine(step, v, u, part(c_neg1, h), ALU.pow)
                    combine(step, u, v, s2, ALU.mult)
                    nc.gpsimd.tensor_tensor(part(scale, h), u, part(c_root, h), ALU.mult).then_inc(scales_ready, 1)

            def layer_scales(step, b, use):
                for h in range(2):
                    pool.wait_ge(stats_ready, norm_count(b, use, h))
                    combine(step, part(tmp1, h), part(mv[:, :, 1], h), part(c_eps5, h), ALU.add)
                    nc.gpsimd.tensor_tensor(part(scale, h), part(tmp1, h), part(c_nhalf, h), ALU.pow).then_inc(scales_ready, 1)

            first = Count()
            self_scales(first, 0, NORM_SELF)

            with pool.Fori(0, BATCH) as b:
                step = Count(b * POOL_STEPS + first.n)

                layer_scales(step, b, NORM_CROSS)

                for h in range(2):
                    var, u, v = part(mv[:, :, 1], h), part(tmp1, h), part(tmp2, h)
                    pool.wait_ge(stats_ready, norm_count(b, NORM_LATENT, h))
                    combine(step, u, var, part(c_eps5, h), ALU.add)
                    combine(step, part(scale, h), u, part(c_nhalf, h), ALU.pow)
                    combine(step, u, part(scale, h), part(scale, h), ALU.mult)
                    combine(step, v, u, var, ALU.mult)
                    combine(step, u, v, part(c_eps6, h), ALU.add)
                    combine(step, v, u, part(c_nhalf, h), ALU.pow)
                    nc.gpsimd.tensor_tensor(part(scale2, h), v, part(scale, h), ALU.mult).then_inc(scales_ready, 1)

                pool.wait_ge(rows_ready, b * (TURNS * NT) + (TURN_LATENT + 1) * NT)
                nc.gpsimd.tensor_tensor(pool_pause[:], c_half[:], c_half[:], ALU.add)
                for s in range(2):
                    nc.gpsimd.memset(q_stack[s][:, :, 6 * MHD:P], 0.0).then_inc(pool_step, 1)
                    nc.gpsimd.memset(k_stack[s][:, :, 6 * MHD + 3:P], 0.0).then_inc(pool_step, 1)
                    nc.gpsimd.memset(k_stack[s][:, :, 6 * MHD:6 * MHD + 3], 1.0).then_inc(pool_step, 1)
                nc.gpsimd.memset(max_stack, 0.0).then_inc(pool_step, 1)
                pool.wait_ge(pool_step, step(7))

                layer_scales(step, b, NORM_KV)

                for t in range(NT):
                    s = t % 2
                    kr = k_rope[:, t, :].rearrange("p (h e) -> p h e", h=MHEADS)
                    ks = k_stack[s].rearrange("p h (c e) -> p h c e", e=MHD)
                    pool.wait_ge(k_high, b * NT + t + 1)
                    nc.gpsimd.tensor_tensor(k_rest[:, s, :, :], kr, ks[:, :, 0, :], ALU.subtract).then_inc(k_rest_done, 1)
                    nc.gpsimd.tensor_tensor(ks[:, :, 1, :], kr, ks[:, :, 0, :], ALU.subtract).then_inc(k_rest_done, 1)
                    nc.gpsimd.tensor_tensor(ks[:, :, 3, :], kr, ks[:, :, 0, :], ALU.subtract).then_inc(k_rest_done, 1)
                    pool.wait_ge(k_rest_done, b * (3 * NT) + 3 * t + 3)
                    nc.gpsimd.tensor_tensor(ks[:, :, 2, :], k_rest[:, s, :, :], ks[:, :, 1, :],
                                            ALU.subtract).then_inc(k_split, 1)

                pool.wait_ge(mv_taken, b * NT + NT)
                nc.gpsimd.tensor_tensor(pool_pause[:], c_half[:], c_half[:], ALU.add)
                nc.gpsimd.tensor_copy(v_group.rearrange("p t (h e) -> p t h e", e=SLOT),
                                      mv_rows[:, :, 0:GROUP, :]).then_inc(vg_ready, 1)
                with pool.Fori(1, NG) as g:
                    pool.wait_ge(mpv_done, b * (NG * NT) + g * NT)
                    nc.gpsimd.tensor_tensor(pool_pause[:], c_half[:], c_half[:], ALU.add)
                    nc.gpsimd.tensor_copy(v_group.rearrange("p t (h e) -> p t h e", e=SLOT),
                                          mv_rows[:, :, bass.ds(g * GROUP, GROUP), :]).then_inc(vg_ready, 1)

                self_scales(step, b, NORM_NEXT)

                for h in range(2):
                    mean, var, u = part(mv[:, :, 0], h), part(mv[:, :, 1], h), part(tmp1, h)
                    pool.wait_ge(stats_ready, norm_count(b, NORM_GATE, h))
                    combine(step, part(tmp2, h), mean, mean, ALU.mult)
                    combine(step, part(scale2, h), part(tmp2, h), var, ALU.add)
                    combine(step, u, part(scale2, h), part(c_eps6, h), ALU.add)
                    nc.gpsimd.tensor_tensor(part(scale, h), u, part(c_nhalf, h), ALU.pow).then_inc(scales_ready, 1)
                assert step.n == POOL_STEPS, ("POOL_STEPS", step.n)

                pool.wait_ge(route_ready, b + 1)
                nc.gpsimd.tensor_tensor(pool_pause[:], c_half[:], c_half[:], ALU.add)
                for t in range(NT):
                    place = bass.IndirectOffsetOnAxis(ap=dest[:, t:t + 1], axis=0)
                    nc.gpsimd.indirect_dma_start(d["sorted_rows"], place, rows[:, t, :], None).then_inc(scattered, 16)
                    nc.gpsimd.indirect_dma_start(d["sorted_res"], place, xres_ids[:, t, :], None).then_inc(scattered, 16)
                pool.wait_ge(scattered, b * SCATTERS + SCATTERS)
                nc.gpsimd.tensor_tensor(lists_pause[:], c_half[:], c_half[:], ALU.add).then_inc(lists_done, 1)

            def rows_out(j, u):
                pool.wait_ge(ey_taken, j + 1)
                nc.gpsimd.tensor_tensor(pool_pause[:], c_half[:], c_half[:], ALU.add).then_inc(pool_paused, 1)
                nc.gpsimd.indirect_dma_start(d["out"], bass.IndirectOffsetOnAxis(ap=out_row[u][:, 0:1], axis=0),
                                             y_rows[u], None).then_inc(ey_out[u], 16)

            rows_out(0, 0)
            pool.wait_ge(pool_paused, 1)
            rows_out(1, 1)
            with pool.Fori(1, MOE_TILES // 2) as i:
                for u in range(2):
                    pool.wait_ge(pool_paused, i * 2 + u)
                    rows_out(i * 2 + u, u)
            for u in range(2):
                pool.wait_ge(ey_out[u], 16 * (MOE_TILES // 2))

        @block.scalar
        def _(act):
            act.wait_ge(first_in, FIRST_CONSTS)

            def turn_copy(b, use, dst, vec):
                for n in range(2):
                    for kt in range(KT):
                        i = KT * n + kt
                        act.wait_ge(turn_done, b * (4 * TURNS) + 4 * use + i + 1)
                        nc.scalar.activation(dst[:, kt, n * BANK:(n + 1) * BANK], ps[:, 4 + i, :], ACT.Copy,
                                             scale=vec[:, kt:kt + 1] if vec is not None else 1.0).then_inc(turn_taken, 1)

            turn_copy(0, TURN_SELF, turned_t, gamma)

            with act.Fori(0, BATCH) as b:

                def take_qkv(h, par):
                    for i in range(4):
                        act.wait_ge(qk_done, b * (4 * HEADS) + h * 4 + i + 1)
                        dst = (q_t if i < 2 else k_t)[par][:, (i % 2) * BANK:(i % 2 + 1) * BANK]
                        nc.scalar.activation(dst, ps[:, 4 + i % 3, :], ACT.Copy,
                                             scale=float(HD) ** -0.5 if i < 2 else 1.0).then_inc(qk_taken, 1)
                    for i in range(2):
                        act.wait_ge(v_done, b * (2 * HEADS) + h * 2 + i + 1)
                        nc.scalar.activation(v_rows[par][:, 4 * i:4 * i + 4, :].rearrange("p t e -> p (t e)"),
                                             ps[:, 4 + (4 + i) % 3, :], ACT.Copy).then_inc(v_taken, 1)

                def take_probs(h, part):
                    for u in range((12 * part) // 8, (12 * (part + 1)) // 8):
                        g, kb = (0, u) if u < 4 else (1, u - 4)
                        lo = max(kb - 4 * g, 0) * P
                        act.wait_ge(pt_done, b * (HEADS * 12) + h * 12 + u + 1)
                        if u >= 4:
                            act.wait_ge(pv_done, b * (HEADS * 12) + h * 12 + u - 3)
                        nc.scalar.activation(probs_t[u % 4][:, lo:BANK], ps[:, 4 + u % 2, lo:BANK], ACT.Copy).then_inc(pt_taken, 1)

                def self_exps(h, par, before):
                    for t in range(NT):
                        if before is not None:
                            take_probs(before, t)
                        n = (t + 1) * P
                        buf = 2 * (t % 2)
                        act.wait_ge(max_done, b * (HEADS * NT) + h * NT + t + 1)
                        nc.scalar.activation(probs[par][:, TRI[t]:TRI[t] + n],
                                             ps[:, buf:buf + 2, :].rearrange("p a n -> p (a n)")[:, 0:n], ACT.Exp,
                                             bias=neg_max[:, par, t:t + 1],
                                             accum_out=row_sum[:, par, t:t + 1]).then_inc(exp_done, 1)

                take_qkv(0, 0)
                self_exps(0, 0, None)
                take_qkv(1, 1)
                with act.Fori(0, HEADS // 2 - 1) as i:
                    for u in range(2):
                        self_exps(i * 2 + u + 1, (u + 1) % 2, i * 2 + u)
                        take_qkv(i * 2 + u + 2, u % 2)
                self_exps(HEADS - 1, (HEADS - 1) % 2, HEADS - 2)
                for part in range(8):
                    take_probs(HEADS - 1, part)

                act.wait_ge(consts_in, CONSTS)
                turn_copy(b, TURN_CROSS, turned_t, None)
                def cross_exp(u):
                    act.wait_ge(xs_taken, b * (2 * NT) + u + 1)
                    half = xs[u // 2 % 2][:, 8 * (u % 2):8 * (u % 2) + 8, :]
                    nc.scalar.activation(half, half, ACT.Exp).then_inc(xexp_done, 1)

                cross_exp(0)
                for u in range(2 * NT):
                    t = u // 2
                    if u + 1 < 2 * NT:
                        cross_exp(u + 1)
                    for j in range(2 * (u % 2), 2 * (u % 2) + 2):
                        act.wait_ge(xpt_done, b * (NT * NG) + NG * t + j + 1)
                        if t >= 4:
                            act.wait_ge(xpv_done, b * (2 * NG) + j + 1)
                        nc.scalar.activation(xprobs_t[:, GROUP * j:GROUP * (j + 1), (t % 4) * P:(t % 4 + 1) * P],
                                             ps[0:CTX, 4 + j % 2, :].rearrange("p (h n) -> p h n", h=GROUP),
                                             ACT.Copy).then_inc(xpt_taken, 1)
                turn_copy(b, TURN_CROSS_OUT, turned_t, None)

                turn_copy(b, TURN_LATENT, turned_t, norm1)
                for t in range(NT):
                    act.wait_ge(mq_taken, b * NT + t + 1)
                    nc.scalar.activation(lat_rows[:, t, :], ps[:, t % 4, D:D + LAT], ACT.Copy).then_inc(mlat_taken, 1)
                for n in range(2):
                    act.wait_ge(lat_turned, b * 2 + n + 1)
                    nc.scalar.activation(lat_t[:, n * BANK:(n + 1) * BANK], ps[:, 4 + n, :], ACT.Identity,
                                         scale=lat_gb[:, 0:1], bias=lat_gb[:, 1:2]).then_inc(lat_taken, 1)
                for t in range(NT):
                    act.wait_ge(mk_taken, b * NT + t + 1)
                    nc.scalar.activation(mv_rows[:, t, :, 0:MHD],
                                         ps[:, t % 4, D:2 * D].rearrange("p (h e) -> p h e", h=MHEADS),
                                         ACT.Copy).then_inc(mv_taken, 1)
                def high_parts(t):
                    s = t % 2
                    if t >= 2:
                        act.wait_ge(qs_turned, b * (2 * NT) + 2 * (t - 1))
                        act.wait_ge(ks_turned, b * (2 * NT) + 2 * (t - 1))
                    qr = q_rope[:, t, :].rearrange("p (h e) -> p h e", h=MHEADS).unsqueeze(2)
                    kr = k_rope[:, t, :].rearrange("p (h e) -> p h e", h=MHEADS).unsqueeze(2)
                    qs = q_stack[s].rearrange("p h (c e) -> p h c e", e=MHD)
                    ks = k_stack[s].rearrange("p h (c e) -> p h c e", e=MHD)
                    act.wait_ge(mq_taken, b * NT + t + 1)
                    nc.scalar.activation(qs[:, :, 0:3, :], qr.to_broadcast([P, MHEADS, 3, MHD]),
                                         ACT.Copy).then_inc(q_high, 1)
                    act.wait_ge(mk_taken, b * NT + t + 1)
                    nc.scalar.activation(ks[:, :, 4:6, :], kr.to_broadcast([P, MHEADS, 2, MHD]), ACT.Copy).then_inc(act_step, 1)
                    act.wait_ge(act_step, b * NT + t + 1)
                    nc.scalar.activation(ks[:, :, 0, :], k_rope[:, t, :].rearrange("p (h e) -> p h e", h=MHEADS),
                                         ACT.Copy).then_inc(k_high, 1)

                high_parts(0)
                for t in range(NT):
                    if t + 1 < NT:
                        high_parts(t + 1)
                    for i in range(2):
                        act.wait_ge(ks_turned, b * (2 * NT) + 2 * t + i + 1)
                        nc.scalar.activation(k_stack_t[:, 8 * i:8 * i + 8, t * P:(t + 1) * P],
                                             ps[:, 6 + i, :].bitcast(BF16).rearrange("p (h n) -> p h n", h=8),
                                             ACT.Copy).then_inc(ks_taken, 1)

                def take_max(g):
                    for j in (1, 3):
                        act.wait_ge(mx_turned, b * (NG * GROUP) + g * GROUP + j + 1)
                        nc.scalar.activation(max_rows(g * GROUP + j), ps[P - SLOT:P, j % 3, :].bitcast(BF16),
                                             ACT.Copy).then_inc(mx2_taken, 1)

                def key_exps(g):
                    use = 0
                    for kb in range(NT):
                        for j in range(GROUP):
                            for c in range(kb // 4, 2):
                                lo = max(kb * P, c * BANK)
                                hi = (c + 1) * BANK
                                act.wait_ge(mst_done, b * (NG * CHUNKS) + g * CHUNKS + use + 1)
                                if j == 0 and c == kb // 4 and kb >= 2:
                                    act.wait_ge(mpv_done, b * (NG * NT) + g * NT + kb - 1)
                                nc.scalar.activation(mprobs_t[kb % 2][:, j, lo:hi], ps[:, 3 + use % 3, 0:hi - lo],
                                                     ACT.Exp).then_inc(mexp_done, 1)
                                use += 1

                take_max(0)
                with act.Fori(0, NG - 1) as g:
                    key_exps(g)
                    take_max(g + 1)
                key_exps(NG - 1)
                turn_copy(b, TURN_NEXT, turned_t, gamma)
                turn_copy(b, TURN_LATENT_OUT, late_t, None)
                turn_copy(b, TURN_GATE, late_t, None)

            def take_x(j, par):
                act.wait_ge(ex_turned, j + 1)
                nc.scalar.activation(xs_t[par].rearrange("p a n -> p (a n)"), ps[:, 0, 0:KT * P], ACT.Copy).then_inc(ex_taken, 1)

            def take_h(j, par):
                for n in range(2):
                    act.wait_ge(eh_turned, j * 2 + n + 1)
                    nc.scalar.activation(h_t[par][:, 4 * n:4 * n + 4, :].rearrange("p a n -> p (a n)"), ps[:, 5 + n, :],
                                         ACT.Relu).then_inc(ehT_taken, 1)

            take_x(0, 0)
            with act.Fori(0, MOE_TILES // 2 - 1) as i:
                for u in range(2):
                    take_x(i * 2 + u + 1, (u + 1) % 2)
                    take_h(i * 2 + u, u)
            take_x(MOE_TILES - 1, 1)
            take_h(MOE_TILES - 2, 0)
            take_h(MOE_TILES - 1, 1)

        @block.tensor
        def _(pe):
            pe.wait_ge(first_in, FIRST_CONSTS)
            pe.wait_ge(consts_made, MADE)

            def turn_half(b, use, src, n):
                pe.wait_ge(rows_ready, b * (TURNS * NT) + use * NT + 4 * n + 4)
                if use == TURN_NEXT and n == 1:
                    pe.wait_ge(mout_taken, b * (NG * 2) + NG * 2)
                for kt in range(KT):
                    i = KT * n + kt
                    for t in range(4):
                        last = nc.tensor.transpose(ps[:, 4 + i, t * P:(t + 1) * P],
                                                   src[:, 4 * n + t, kt * P:(kt + 1) * P], ident[:])
                    last.then_inc(turn_done, 1)

            def turn_rows(b, use, src):
                for n in range(2):
                    turn_half(b, use, src, n)

            turn_rows(0, TURN_SELF, self_rows)
            pe.wait_ge(turn_taken, 4 * TURN_SELF + 4)

            with pe.Fori(0, BATCH) as b:
                def turn(use):
                    turn_rows(b, use, rows)

                def turned(use):
                    pe.wait_ge(turn_taken, b * (4 * TURNS) + 4 * use + 4)

                def project(use, lhs, rhs, bias=None):
                    for t in range(NT):
                        if t >= 4:
                            pe.wait_ge(proj_added, b * (PROJS * NT) + use * NT + t - 3)
                        out = ps[:, t % 4, 0:D]
                        for k, (l, w) in enumerate(zip(lhs, rhs)):
                            last = nc.tensor.matmul(out, l[:, t * P:(t + 1) * P], w, start=(k == 0),
                                                    stop=(k == len(lhs) - 1 and bias is None))
                        if bias is not None:
                            last = nc.tensor.matmul(out, ones_f[:], bias, start=False, stop=True)
                        last.then_inc(proj_done, 1)

                def project_q(h, par):
                    for i in range(4):
                        if i == 0:
                            pass
                        if i == 3:
                            pe.wait_ge(qk_taken, b * (4 * HEADS) + h * 4 + 1)
                        w = (i // 2) * HD
                        for kt in range(KT):
                            last = nc.tensor.matmul(ps[:, 4 + i % 3, :], w_head[par][:, kt, w:w + HD],
                                                    turned_t[:, kt, (i % 2) * BANK:(i % 2 + 1) * BANK],
                                                    start=(kt == 0), stop=(kt == KT - 1))
                        last.then_inc(qk_done, 1)

                def project_v(h, par):
                    for i in range(2):
                        pe.wait_ge(qk_taken, b * (4 * HEADS) + h * 4 + i + 2)
                        for t in range(4):
                            for kt in range(KT):
                                last = nc.tensor.matmul(ps[:, 4 + (4 + i) % 3, t * P:(t + 1) * P],
                                                        turned_t[:, kt, (4 * i + t) * P:(4 * i + t + 1) * P],
                                                        w_head[par][:, kt, 2 * HD:3 * HD],
                                                        start=(kt == 0), stop=(kt == KT - 1))
                        last.then_inc(v_done, 1)

                def scores(h, par, t):
                    n = (t + 1) * P
                    buf = 2 * (t % 2)
                    if t == 0:
                        pe.wait_ge(qk_taken, b * (4 * HEADS) + h * 4 + 4)
                    pe.wait_ge(exp_done, b * (HEADS * NT) + h * NT + t - 1) if not (isinstance(h, int) and h * NT + t < 2) else None
                    for c in range(0, n, BANK):
                        m = min(BANK, n - c)
                        diag = c + m == n
                        last = nc.tensor.matmul(ps[:, buf + c // BANK, 0:m], q_t[par][:, t * P:(t + 1) * P],
                                                k_t[par][:, c:c + m], start=True, stop=True)
                        if diag:
                            last = nc.tensor.matmul(ps[:, buf + c // BANK, m - P:m], ident_b[:], causal_b[:],
                                                    start=False, stop=True, skip_group_check=True)
                    last.then_inc(scores_done, 1)

                BLOCKS = [(0, kb) for kb in range(4)] + [(1, kb) for kb in range(8)]

                def turn_probs(h, par, u):
                    g, kb = BLOCKS[u]
                    t0 = max(kb, 4 * g)
                    if u >= 2:
                        pe.wait_ge(pt_taken, b * (HEADS * 12) + h * 12 + u - 1)
                    pe.wait_ge(probs_done, b * (HEADS * NT) + h * NT + 4 * g + 4)
                    for t in range(t0, 4 * g + 4):
                        last = nc.tensor.transpose(ps[:, 4 + u % 2, (t - 4 * g) * P:(t - 4 * g + 1) * P],
                                                   probs[par][:, TRI[t] + kb * P:TRI[t] + (kb + 1) * P], ident[:])
                    last.then_inc(pt_done, 1)

                def use_probs(h, par, u):
                    g, kb = BLOCKS[u]
                    lo = max(kb - 4 * g, 0) * P
                    if kb == 0:
                        pe.wait_ge(v_taken, b * (2 * HEADS) + h * 2 + 2)
                    pe.wait_ge(pt_taken, b * (HEADS * 12) + h * 12 + u + 1)
                    nc.tensor.matmul(ps[:, 6 + g, lo:BANK], v_rows[par][:, kb, :], probs_t[u % 4][:, lo:BANK],
                                     start=(kb == 0), stop=True, skip_group_check=True).then_inc(pv_done, 1)

                def products(h, par, part):
                    for u in range((12 * part) // 8, (12 * (part + 1)) // 8):
                        turn_probs(h, par, u)
                        if u > 0:
                            use_probs(h, par, u - 1)
                    if part == 7:
                        use_probs(h, par, 11)

                def wait_weights(h_pairs, slot):
                    pe.wait_ge(w_in[slot], b * (16 * HEADS // 2) + 16 * h_pairs + 16)

                wait_weights(0, 0)
                project_q(0, 0)
                project_v(0, 0)
                for t in range(NT):
                    scores(0, 0, t)
                wait_weights(0, 1)
                pe.wait_ge(v_taken, b * (2 * HEADS) + 2)
                project_q(1, 1)
                project_v(1, 1)
                with pe.Fori(0, HEADS // 2 - 1) as i:
                    for u in range(2):
                        h = i * 2 + u + 1
                        par = (u + 1) % 2
                        for t in range(NT):
                            scores(h, par, t)
                            if t == 0:
                                pe.wait_ge(v_taken, b * (2 * HEADS) + h * 2 + 2)
                            products(h - 1, u % 2, t)
                        pe.wait_ge(pt_taken, b * (HEADS * 12) + h * 12)
                        wait_weights(i + 1, u % 2)
                        project_q(h + 1, u % 2)
                        project_v(h + 1, u % 2)
                        pe.wait_ge(out_taken, b * (2 * HEADS) + h * 2)
                h = HEADS - 1
                for t in range(NT):
                    scores(h, h % 2, t)
                    if t == 0:
                        pe.wait_ge(v_taken, b * (2 * HEADS) + h * 2 + 2)
                    products(h - 1, (h - 1) % 2, t)
                pe.wait_ge(pt_taken, b * (HEADS * 12) + h * 12)
                pe.wait_ge(out_taken, b * (2 * HEADS) + h * 2)
                pe.wait_ge(ctx_in, b * 32 + 32)
                pe.wait_ge(exp_done, b * (HEADS * NT) + HEADS * NT)
                pe.wait_ge(consts_in, CONSTS)
                for m in range(KT):
                    for kt in range(KT):
                        last = nc.tensor.matmul(ps[:, m, 0:CTX], xw_k[:, kt, m * P:(m + 1) * P], ctx_t[:, kt, :],
                                                start=(kt == 0), stop=(kt == KT - 1))
                    last.then_inc(xkv_done, 1)
                for kt in range(KT):
                    last = nc.tensor.matmul(ps[0:CTX, 2, 0:D], ctx_t[:, kt, :], xw_v[:, kt, :],
                                            start=(kt == 0), stop=(kt == KT - 1))
                last.then_inc(xkv_done, 1)
                for t in range(NT):
                    products(h, h % 2, t)
                pe.wait_ge(out_taken, b * (2 * HEADS) + 2 * HEADS)
                pe.wait_ge(xkv_taken, b * 3 + 3)
                project(PROJ_SELF, [attn_t[:, k, :] for k in range(HEADS)], [w_out[:, k, :] for k in range(HEADS)])

                turn(TURN_CROSS)
                turned(TURN_CROSS)
                for n in range(2):
                    for m in range(KT):
                        i = KT * n + m
                        for kt in range(KT):
                            last = nc.tensor.matmul(ps[:, i, :], xw_q[:, kt, m * P:(m + 1) * P],
                                                    turned_t[:, kt, n * BANK:(n + 1) * BANK],
                                                    start=(kt == 0), stop=(kt == KT - 1))
                        last.then_inc(xq_done, 1)

                def cross_scores(u):
                    t, half = divmod(u, 2)
                    if u == 0:
                        pe.wait_ge(xq_taken, b * 4 + 4)
                        pe.wait_ge(mask_made, b + 1)
                    if u >= 2:
                        pe.wait_ge(xs_taken, b * (2 * NT) + u - 1)
                    for j in range(2):
                        nc.tensor.matmul(ps[:, 2 * half + j, 0:GROUP * CTX], xq_t[:, half, t * P:(t + 1) * P],
                                         xk_blocks[:, half, GROUP * j:GROUP * (j + 1), :], start=True, stop=False)
                        last = nc.tensor.matmul(ps[:, 2 * half + j, 0:GROUP * CTX], ones_b[0:1, :],
                                                mask_row[:].rearrange("p h c -> p (h c)"), start=False, stop=True)
                    last.then_inc(xs_done, 1)

                cross_scores(0)
                cross_scores(1)
                for u in range(2 * NT):
                    t = u // 2
                    if u + 2 < 2 * NT:
                        cross_scores(u + 2)
                    pe.wait_ge(xexp_done, b * (2 * NT) + u + 1)
                    for j in range(2 * (u % 2), 2 * (u % 2) + 2):
                        if NG * t + j >= 2:
                            pe.wait_ge(xpt_taken, b * (NT * NG) + NG * t + j - 1)
                        for h in range(GROUP):
                            last = nc.tensor.transpose(ps[0:CTX, 4 + j % 2, h * P:(h + 1) * P],
                                                       xs[t % 2][:, GROUP * j + h, :], ident[:])
                        last.then_inc(xpt_done, 1)
                    if u % 8 == 7:
                        pe.wait_ge(xpt_taken, b * (NT * NG) + NG * t + NG)
                        for j in range(NG):
                            use = NG * (t // 4) + j
                            if use >= 2:
                                pe.wait_ge(xpv_taken, b * (2 * NG) + use - 1)
                            for h in range(GROUP):
                                last = nc.tensor.matmul(ps[SLOT * h:SLOT * (h + 1), 6 + j % 2, :], xv[:, GROUP * j + h, :],
                                                        xprobs_t[:, GROUP * j + h, :], start=True, stop=True)
                            last.then_inc(xpv_done, 1)

                def back(turn_use, src, taken, count):
                    pe.wait_ge(taken, count)
                    for t in range(NT):
                        if t >= 4:
                            pe.wait_ge(rows_ready, b * (TURNS * NT) + turn_use * NT + t - 3)
                        for g in range(NG):
                            last = nc.tensor.transpose(ps[:, t % 4, g * P:(g + 1) * P], src[:, g, t * P:(t + 1) * P], ident[:])
                        last.then_inc(back_done, 1)

                back(TURN_CROSS_OUT, xout_t, xpv_taken, b * (2 * NG) + 2 * NG)
                turn(TURN_CROSS_OUT)
                turned(TURN_CROSS_OUT)
                project(PROJ_CROSS, [turned_t[:, k, :] for k in range(KT)], [xw_o[:, k, :] for k in range(KT)], bo[:])

                turn(TURN_LATENT)
                turned(TURN_LATENT)
                for t in range(NT):
                    if t >= 4:
                        pe.wait_ge(mq_taken, b * NT + t - 3)
                        pe.wait_ge(mlat_taken, b * NT + t - 3)
                    for kt in range(KT):
                        last = nc.tensor.matmul(ps[:, t % 4, 0:D + LAT], turned_t[:, kt, t * P:(t + 1) * P], mw_qd[:, kt, :],
                                                start=(kt == 0), stop=(kt == KT - 1))
                    last.then_inc(mq_done, 1)
                for n in range(2):
                    pe.wait_ge(lat_ready, b * NT + 4 * n + 4)
                    for t in range(4):
                        last = nc.tensor.transpose(ps[:, 4 + n, t * P:(t + 1) * P], lat_rows[:, 4 * n + t, :], ident[:])
                    last.then_inc(lat_turned, 1)
                pe.wait_ge(mq_taken, b * NT + NT)
                for t in range(NT):
                    if t % 4 == 0:
                        pe.wait_ge(lat_taken, b * 2 + t // 4 + 1)
                    if t >= 4:
                        pe.wait_ge(mk_taken, b * NT + t - 3)
                        pe.wait_ge(mv_taken, b * NT + t - 3)
                    nc.tensor.matmul(ps[:, t % 4, :], lat_t[:, t * P:(t + 1) * P], mw_kv[:], start=True,
                                     stop=True).then_inc(mkv_done, 1)
                def turn_stacks(t):
                    for stack, split, done, taken, bank in ((q_stack, q_split, qs_turned, qs_taken, 4),
                                                            (k_stack, k_split, ks_turned, ks_taken, 6)):
                        pe.wait_ge(split, b * NT + t + 1)
                        for i in range(2):
                            if t >= 1:
                                pe.wait_ge(taken, b * (2 * NT) + 2 * t + i - 1)
                            for h in range(8):
                                last = nc.tensor.transpose(ps[:, bank + i, :].bitcast(BF16)[:, h * P:(h + 1) * P],
                                                           stack[t % 2][:, 8 * i + h, :], ident_b[:])
                            last.then_inc(done, 1)

                def max_chunk(g, u):
                    j, t, c = (FIRST_CHUNKS if isinstance(g, int) and g == 0 else MAX_CHUNKS)[u]
                    n = min(BANK, (t + 1) * P - c * BANK)
                    diag = c == t // 4
                    if u >= 3:
                        pe.wait_ge(ms_taken, b * (NG * CHUNKS) + g * CHUNKS + u - 2)
                    head = g * GROUP + j
                    last = nc.tensor.matmul(ps[:, u % 3, 0:n], q_stack_t[:, head, t * P:(t + 1) * P],
                                            k_stack_t[:, head, c * BANK:c * BANK + n], start=True, stop=True)
                    if diag:
                        last = nc.tensor.matmul(ps[:, u % 3, n - P:n], ident_b[:], causal_b[:], start=False, stop=True,
                                                skip_group_check=True)
                    last.then_inc(ms_done, 1)

                def turn_max(g):
                    pe.wait_ge(mmax_step, b * (NG * 6) + g * 6 + 6)
                    for j in range(GROUP):
                        if j == 3:
                            pe.wait_ge(mx_taken, b * (NG * 2) + g * 2 + 1)
                        for t in range(NT):
                            last = nc.tensor.transpose(ps[P - SLOT:P, j % 3, :].bitcast(BF16)[:, t * P:(t + 1) * P],
                                                       max_stack[:, t, j, :], ident_b[:])
                        last.then_inc(mx_turned, 1)

                ST_CHUNKS = [(kb, j, c) for kb in range(NT) for j in range(GROUP) for c in range(kb // 4, 2)]

                def key_chunk(g, u):
                    kb, j, c = ST_CHUNKS[u]
                    lo, hi = max(kb * P, c * BANK), (c + 1) * BANK
                    if u >= 3:
                        pe.wait_ge(mexp_done, b * (NG * CHUNKS) + g * CHUNKS + u - 2)
                    head = g * GROUP + j
                    diag = lo == kb * P and c == kb // 4
                    last = nc.tensor.matmul(ps[:, 3 + u % 3, 0:hi - lo], k_stack_t[:, head, kb * P:(kb + 1) * P],
                                            q_stack_t[:, head, lo:hi], start=True, stop=True)
                    if diag:
                        last = nc.tensor.matmul(ps[:, 3 + u % 3, 0:P], ident_b[:], causal_t_b[:], start=False, stop=True,
                                                skip_group_check=True)
                    last.then_inc(mst_done, 1)

                def key_products(g, kb):
                    pe.wait_ge(mexp_done, b * (NG * CHUNKS) + g * CHUNKS + sum(1 for x in ST_CHUNKS if x[0] <= kb))
                    if kb == 0:
                        pe.wait_ge(vg_ready, b * NG + g + 1)
                    for c in range(kb // 4, 2):
                        lo, hi = max(kb * P, c * BANK), (c + 1) * BANK
                        for j in range(GROUP):
                            last = nc.tensor.matmul(ps[SLOT * j:SLOT * (j + 1), 6 + c, lo - c * BANK:BANK],
                                                    v_group[:, kb, SLOT * j:SLOT * (j + 1)], mprobs_t[kb % 2][:, j, lo:hi],
                                                    start=(kb == 0), stop=True, skip_group_check=True)
                    last.then_inc(mpv_done, 1)

                def keys(g, ahead):
                    pe.wait_ge(mx_taken, b * (NG * 2) + g * 2 + 2)
                    pe.wait_ge(mx2_taken, b * (NG * 2) + g * 2 + 2)
                    kb_done = -1
                    for u in range(CHUNKS):
                        kb = ST_CHUNKS[u][0]
                        key_chunk(g, u)
                        if ahead:
                            max_chunk(g + 1, u)
                        if u + 1 < 48 and ST_CHUNKS[u + 1][0] != kb and kb >= 1:
                            key_products(g, kb - 1)
                            kb_done = kb - 1
                    for kb in range(kb_done + 1, NT):
                        key_products(g, kb)
                    if ahead:
                        turn_max(g + 1)
                        pe.wait_ge(mout_taken, b * (NG * 2) + g * 2 + 2)

                for t in range(NT + 1):
                    if t < NT:
                        turn_stacks(t)
                    if t == 1:
                        pe.wait_ge(mk_taken, b * NT + NT)
                        pe.wait_ge(mv_taken, b * NT + NT)
                    if t >= 1:
                        pe.wait_ge(qs_taken, b * (2 * NT) + 2 * t)
                        pe.wait_ge(ks_taken, b * (2 * NT) + 2 * t)
                        for u, chunk in enumerate(FIRST_CHUNKS):
                            if chunk[1] == t - 1:
                                max_chunk(0, u)
                turn_max(0)
                with pe.Fori(0, NG - 1) as g:
                    keys(g, True)
                keys(NG - 1, False)

                turn_rows(b, TURN_NEXT, self_rows)
                back(TURN_LATENT_OUT, mout_t, mout_taken, b * (NG * 2) + NG * 2)
                turned(TURN_NEXT)
                turn(TURN_LATENT_OUT)
                turned(TURN_LATENT_OUT)
                project(PROJ_LATENT, [late_t[:, k, :] for k in range(KT)], [mw_o[:, k, :] for k in range(KT)])

                for t in range(NT):
                    if t % HALF == 0:
                        turn_half(b, TURN_GATE, rows, t // HALF)
                        pe.wait_ge(turn_taken, b * (4 * TURNS) + 4 * TURN_GATE + KT * (t // HALF) + KT)
                    for kt in range(KT):
                        last = nc.tensor.matmul(ps[:, 0, t * EXPERTS:(t + 1) * EXPERTS], late_t[:, kt, t * P:(t + 1) * P],
                                                w_gate[:, kt, :], start=(kt == 0), stop=(kt == KT - 1))
                last.then_inc(gate_done, 1)

                pe.wait_ge(counts_ready, b + 1)
                oh = onehot_b.rearrange("p t e -> p (t e)")
                nc.tensor.matmul(ps[:, 7, 0:NT * EXPERTS], before_b[:], oh, start=True, stop=True)
                nc.tensor.matmul(ps[:, 7, NT * EXPERTS:2 * NT * EXPERTS], ones_b[:], oh, start=True, stop=True,
                                 skip_group_check=True).then_inc(counts_done, 1)

            pe.wait_ge(tables_ready, 1)
            pe.wait_ge(moe_w_in, 64)

            def expert_of(j):
                return pe.value_load(tile_ei[0:1, bass.ds(j, 1)], min_val=0, max_val=EXPERTS - 1)

            def turn_x(slot, landed):
                pe.wait_ge(et_in[slot], landed)
                for kt in range(KT):
                    last = nc.tensor.transpose(ps[:, 0, kt * P:(kt + 1) * P], xs_in[slot][:, kt * P:(kt + 1) * P], ident[:])
                last.then_inc(ex_turned, 1)

            def first_layer(j, par, e):
                pe.wait_ge(ex_taken, j + 1)
                for n in range(2):
                    for kt in range(KT):
                        last = nc.tensor.matmul(ps[:, 1 + 2 * par + n, :], xs_t[par][:, kt, :],
                                                w1[:, kt, bass.ds(e * HID + n * BANK, BANK)],
                                                start=(kt == 0), stop=(kt == KT - 1))
                    last.then_inc(eh_done, 1)

            def turn_h(j, par):
                for n in range(2):
                    pe.wait_ge(eh_taken, j * 2 + n + 1)
                    for k in range(4):
                        last = nc.tensor.transpose(ps[:, 5 + n, k * P:(k + 1) * P],
                                                   h_rows[par][:, (4 * n + k) * P:(4 * n + k + 1) * P], ident[:])
                    last.then_inc(eh_turned, 1)

            def second_layer(j, par, e, first=False):
                if not first:
                    pe.wait_ge(ey_taken, j)
                for k in range(HK):
                    if k % 4 == 0:
                        pe.wait_ge(ehT_taken, j * 2 + k // 4 + 1)
                    last = nc.tensor.matmul(ps[:, 7, 0:D], h_t[par][:, k, :], w2[:, bass.ds(e * HK + k, 1), :].rearrange("p o n -> p (o n)"),
                                            start=(k == 0), stop=(k == HK - 1))
                last.then_inc(ey_done, 1)

            def expert_step(j, u, landed, first=False):
                e, e_next = expert_of(j), expert_of(j + 1)
                turn_x((u + 1) % SLOTS, landed)
                turn_h(j, u % 2)
                first_layer(j + 1, (u + 1) % 2, e_next)
                second_layer(j, u % 2, e, first)

            e = expert_of(0)
            turn_x(0, 32)
            first_layer(0, 0, e)
            expert_step(0, 0, 32, True)
            for u in range(1, SLOTS):
                expert_step(u, u, 32 + 32 * ((u + 1) // SLOTS))
            with pe.Fori(1, MOE_TILES // SLOTS - 1) as i:
                for u in range(SLOTS):
                    expert_step(i * SLOTS + u, u, i * 32 + 32 + 32 * ((u + 1) // SLOTS))
            for u in range(SLOTS - 1):
                expert_step(MOE_TILES - SLOTS + u, u, 32 * (MOE_TILES // SLOTS))
            e = expert_of(MOE_TILES - 1)
            turn_h(MOE_TILES - 1, 1)
            second_layer(MOE_TILES - 1, 1, e)

        @block.vector
        def _(dve):
            dve.wait_ge(consts_made, MADE)

            def finish_stats(step, last, half):
                last.then_inc(dve_step, 1)
                dve.wait_ge(dve_step, step())
                nc.vector.memset(pause[:], 0.0)
                for t in range(HALF * half, HALF * (half + 1)):
                    last = nc.vector.bn_aggr(mv[:, t, :], stats[:, t, :])
                last.then_inc(stats_ready, 1)

            def row_stats(step, src, half):
                for t in range(HALF * half, HALF * (half + 1)):
                    last = nc.vector.bn_stats(stats[:, t, :], src[:, t, :])
                finish_stats(step, last, half)

            def normed_rows(b, use, half, src, dst, by, done):
                dve.wait_ge(scales_ready, norm_count(b, use, half))
                for t in range(HALF * half, HALF * (half + 1)):
                    nc.vector.tensor_scalar(dst[:, t, :], src[:, t, :], mv[:, t, 0:1], by[:, t:t + 1],
                                            ALU.subtract, ALU.mult).then_inc(done, 1)

            def self_norm(step, b, use):
                for h in range(2):
                    row_stats(step, xin, h)
                for h in range(2):
                    normed_rows(b, use, h, xin, self_rows, scale, rows_ready)

            first = Count()
            dve.wait_ge(x_in, 16)
            self_norm(first, 0, NORM_SELF)
            dve.wait_ge(consts_in, CONSTS)
            nc.vector.tensor_copy(list_end[:], list_at[:]).then_inc(dve_step, 1)
            dve.wait_ge(dve_step, first())

            with dve.Fori(0, BATCH) as b:
                step = Count(b * DVE_STEPS + first.n)

                def add_projection(use, src, dst, norm_rows):
                    count = b * (PROJS * NT) + use * NT
                    for t in range(NT):
                        dve.wait_ge(proj_done, count + t + 1)
                        nc.vector.tensor_tensor(dst[:, t, :], src[:, t, :], ps[:, t % 4, 0:D], ALU.add).then_inc(proj_added, 1)
                        if t % HALF >= 1:
                            dve.wait_ge(proj_added, count + t)
                            nc.vector.bn_stats(stats[:, t - 1, :], dst[:, t - 1, :])
                        if t % HALF == HALF - 1:
                            dve.wait_ge(proj_added, count + t + 1)
                            finish_stats(step, nc.vector.bn_stats(stats[:, t, :], dst[:, t, :]), t // HALF)
                        if t == HALF + 1:
                            norm_rows(0)
                    norm_rows(1)

                def tile_max(h, par, t):
                    n = (t + 1) * P
                    buf = 2 * (t % 2)
                    dve.wait_ge(scores_done, b * (HEADS * NT) + h * NT + t + 1)
                    nc.vector.tensor_reduce(neg_max[:, par, t:t + 1],
                                            ps[:, buf:buf + 2, :].rearrange("p a n -> p (a n)")[:, 0:n],
                                            AX.X, ALU.max, negate=True).then_inc(max_done, 1)

                def tile_inv(h, par, t):
                    dve.wait_ge(exp_done, b * (HEADS * NT) + h * NT + t + 1)
                    nc.vector.reciprocal(inv_sum[:, par, t:t + 1], row_sum[:, par, t:t + 1]).then_inc(inv_done, 1)

                def tile_norm(h, par, t):
                    n = (t + 1) * P
                    dve.wait_ge(inv_done, b * (HEADS * NT) + h * NT + t + 1)
                    nc.vector.tensor_scalar(probs[par][:, TRI[t]:TRI[t] + n], probs[par][:, TRI[t]:TRI[t] + n],
                                            inv_sum[:, par, t:t + 1], None, ALU.mult).then_inc(probs_done, 1)

                def take_out(h, g):
                    dve.wait_ge(pv_done, b * (HEADS * 12) + h * 12 + (4 if g == 0 else 12))
                    dve.wait_ge(consts_made, MADE)
                    nc.vector.tensor_copy(attn_t[:, h, g * BANK:(g + 1) * BANK] if isinstance(h, int) else
                                          attn_t[:, bass.ds(h, 1), g * BANK:(g + 1) * BANK].rearrange("p o n -> p (o n)"),
                                          ps[:, 6 + g, :]).then_inc(out_taken, 1)

                def head(h, par, before):
                    for t in range(NT):
                        tile_max(h, par, t)
                        if t > 0:
                            tile_inv(h, par, t - 1)
                            tile_norm(h, par, t - 1)
                        if before is not None and t == 5:
                            take_out(before, 0)
                    tile_inv(h, par, NT - 1)
                    tile_norm(h, par, NT - 1)
                    if before is not None:
                        take_out(before, 1)

                head(0, 0, None)
                with dve.Fori(0, HEADS // 2 - 1) as i:
                    for u in range(2):
                        head(i * 2 + u + 1, (u + 1) % 2, i * 2 + u)
                head(HEADS - 1, (HEADS - 1) % 2, HEADS - 2)
                dve.wait_ge(ctx_in, b * 32 + 32)
                nc.vector.tensor_scalar(mask_row[:], mask_u8[:].unsqueeze(1).to_broadcast([1, GROUP, CTX]),
                                        -1.0, -MASKED, ALU.add, ALU.mult).then_inc(mask_made, 1)
                for m in range(KT):
                    dve.wait_ge(xkv_done, b * 3 + m + 1)
                    for h in range(NT):
                        last = nc.vector.tensor_scalar(xk_blocks[:, m, h, :], ps[:, m, 0:CTX], bk[:, m:m + 1],
                                                       head_rows[:, h:h + 1], ALU.add, ALU.mult)
                    last.then_inc(xkv_taken, 1)
                dve.wait_ge(xkv_done, b * 3 + 3)
                nc.vector.tensor_tensor(xv[:, :, 0:XHD], ps[0:CTX, 2, 0:D].rearrange("p (h e) -> p h e", h=XHEADS),
                                        bv[:].rearrange("p (h e) -> p h e", h=XHEADS), ALU.add).then_inc(xkv_taken, 1)
                take_out(HEADS - 1, 0)
                take_out(HEADS - 1, 1)
                dve.wait_ge(lists_done, b + 1)
                nc.vector.tensor_scalar(xres_ids[:, :, D:D + 2], xres_ids[:, :, D:D + 2], float(T), None, ALU.add).then_inc(dve_step, 1)
                dve.wait_ge(dve_step, step())
                add_projection(PROJ_SELF, xin, xres,
                               lambda h: normed_rows(b, NORM_CROSS, h, xres, rows, scale, rows_ready))

                for i in range(4):
                    n, m = divmod(i, KT)
                    dve.wait_ge(xq_done, b * 4 + i + 1)
                    nc.vector.tensor_scalar(xq_t[:, m, n * BANK:(n + 1) * BANK], ps[:, i, :], bq[:, m:m + 1],
                                            float(XHD) ** -0.5, ALU.add, ALU.mult).then_inc(xq_taken, 1)

                def cross_out(c):
                    for j in range(NG):
                        dve.wait_ge(xpv_done, b * (2 * NG) + NG * c + j + 1)
                        nc.vector.tensor_copy(xout_t[:, j, c * BANK:(c + 1) * BANK], ps[:, 6 + j % 2, :]).then_inc(xpv_taken, 1)

                for u in range(2 * NT):
                    t, half = divmod(u, 2)
                    s4 = ps[:, 2 * half:2 * half + 2, 0:GROUP * CTX].rearrange("p j (h c) -> p j h c", h=GROUP)
                    neg = xneg[half].rearrange("p (j h) -> p j h", j=2)
                    dve.wait_ge(xs_done, b * (2 * NT) + u + 1)
                    nc.vector.tensor_reduce(neg, s4, AX.X, ALU.max, negate=True).then_inc(xneg_done, 1)
                    if t >= 2:
                        dve.wait_ge(xpt_done, b * (NT * NG) + NG * (t - 2) + 2 * half + 2)
                    dve.wait_ge(xneg_done, b * (2 * NT) + u + 1)
                    nc.vector.tensor_tensor(xs[t % 2][:, 8 * half:8 * half + 8, :].rearrange("p (j h) c -> p j h c", j=2), s4,
                                            neg.unsqueeze(3).to_broadcast([P, 2, GROUP, CTX]), ALU.add).then_inc(xs_taken, 1)
                    if u == 9:
                        cross_out(0)
                cross_out(1)

                def back_rows(use, inv):
                    def heads(t):
                        return ps[:, t % 4, :].rearrange("p (h e) -> p h e", e=SLOT)

                    for t in range(NT + 1):
                        if t < NT:
                            dve.wait_ge(back_done, b * (2 * NT) + use * NT + t + 1)
                            nc.vector.reciprocal(inv[:, t, :], heads(t)[:, :, XHD]).then_inc(dve_step, 1)
                        if t >= 1:
                            dve.wait_ge(dve_step, step())
                            nc.vector.tensor_tensor(rows[:, t - 1, :].rearrange("p (h e) -> p h e", e=XHD), heads(t - 1)[:, :, 0:XHD],
                                                    inv[:, t - 1, :].unsqueeze(2).to_broadcast([P, XHEADS, XHD]),
                                                    ALU.mult).then_inc(rows_ready, 1)

                back_rows(0, xinv)
                add_projection(PROJ_CROSS, xres, xres,
                               lambda h: normed_rows(b, NORM_LATENT, h, xres, rows, scale2, rows_ready))

                dve.wait_ge(zeros_out, 16)
                for t in range(NT):
                    last = nc.vector.tensor_scalar(xp[:, t, :], xres[:, t, :], mv[:, t, 0:1], scale[:, t:t + 1],
                                                   ALU.subtract, ALU.mult)
                last.then_inc(dve_step, 1)
                dve.wait_ge(dve_step, step())

                def rope(dst, src, table, t):
                    x = src.rearrange("p (h e) -> p h e", h=MHEADS)
                    y = dst[:, t, :].rearrange("p (h e) -> p h e", h=MHEADS)
                    half = MHD // 2
                    cos = table[:, t, 0:MHD].unsqueeze(1).to_broadcast([P, MHEADS, MHD])
                    u = rope_tmp.rearrange("p (h e) -> p h e", h=MHEADS)
                    nc.vector.tensor_tensor(y, x, cos, ALU.mult).then_inc(dve_step, 1)
                    for a in range(2):
                        sin = table[:, t, MHD + a * half:MHD + (a + 1) * half].unsqueeze(1).to_broadcast([P, MHEADS, half])
                        nc.vector.tensor_tensor(u[:, :, a * half:(a + 1) * half], x[:, :, (1 - a) * half:(2 - a) * half], sin,
                                                ALU.mult).then_inc(dve_step, 1)
                    dve.wait_ge(dve_step, step(3))

                rope_tmp = q_rest[:, 0, :, :].rearrange("p h e -> p (h e)")
                for t in range(NT):
                    if t == HALF + 1:
                        dve.wait_ge(mlat_taken, b * NT + HALF)
                        row_stats(step, lat_rows, 0)
                    dve.wait_ge(mq_done, b * NT + t + 1)
                    rope(q_rope, ps[:, t % 4, 0:D], rope_q, t)
                    nc.vector.tensor_tensor(q_rope[:, t, :], q_rope[:, t, :], rope_tmp, ALU.add).then_inc(mq_taken, 1)
                    dve.wait_ge(mq_taken, b * NT + t + 1)
                dve.wait_ge(mlat_taken, b * NT + NT)
                row_stats(step, lat_rows, 1)
                for h in range(2):
                    normed_rows(b, NORM_KV, h, lat_rows, lat_rows, scale, lat_ready)
                for t in range(NT):
                    dve.wait_ge(mkv_done, b * NT + t + 1)
                    rope(k_rope, ps[:, t % 4, 0:D], rope_k, t)
                    nc.vector.tensor_tensor(k_rope[:, t, :], k_rope[:, t, :], rope_tmp, ALU.add).then_inc(mk_taken, 1)
                    dve.wait_ge(mk_taken, b * NT + t + 1)
                def split_queries(t):
                    s = t % 2
                    qr = q_rope[:, t, :].rearrange("p (h e) -> p h e", h=MHEADS)
                    qs = q_stack[s].rearrange("p h (c e) -> p h c e", e=MHD)
                    dve.wait_ge(q_high, b * NT + t + 1)
                    nc.vector.tensor_tensor(q_rest[:, s, :, :], qr, qs[:, :, 0, :], ALU.subtract).then_inc(q_rest_done, 1)
                    dve.wait_ge(q_rest_done, b * (2 * NT) + 2 * t + 1)
                    dve.wait_ge(consts_made, MADE)
                    nc.vector.tensor_copy(qs[:, :, 3:5, :], q_rest[:, s, :, :].unsqueeze(2).to_broadcast([P, MHEADS, 2, MHD])).then_inc(q_rest_done, 1)
                    dve.wait_ge(q_rest_done, b * (2 * NT) + 2 * t + 2)
                    nc.vector.tensor_tensor(qs[:, :, 5, :], q_rest[:, s, :, :], qs[:, :, 3, :], ALU.subtract).then_inc(q_split, 1)

                def max_chunk(g, u):
                    j, t, c = (FIRST_CHUNKS if isinstance(g, int) and g == 0 else MAX_CHUNKS)[u]
                    n = min(BANK, (t + 1) * P - c * BANK)
                    dve.wait_ge(ms_done, b * (NG * CHUNKS) + g * CHUNKS + u + 1)
                    nc.vector.tensor_reduce(max_part[:, j, t, c:c + 1], ps[:, u % 3, 0:n], AX.X, ALU.max).then_inc(ms_taken, 1)

                def stack_max(g):
                    dve.wait_ge(ms_taken, b * (NG * CHUNKS) + g * CHUNKS + 48)
                    first = b * (NG * 6) + g * 6
                    top = max_part
                    neg = max_neg.rearrange("p t j -> p j t")
                    rest = max_rest.rearrange("p t j -> p j t")
                    nc.vector.tensor_scalar(neg[:, :, 0:4], top[:, :, 0:4, 0], -1.0, None, ALU.mult).then_inc(mmax_step, 1)
                    nc.vector.tensor_reduce(neg[:, :, 4:NT], top[:, :, 4:NT, :], AX.X, ALU.max, negate=True).then_inc(mmax_step, 1)
                    dve.wait_ge(mmax_step, first + 2)
                    dve.wait_ge(consts_made, MADE)
                    nc.vector.tensor_copy(max_stack[:, :, :, 0], max_neg).then_inc(mmax_step, 1)
                    dve.wait_ge(mmax_step, first + 3)
                    nc.vector.tensor_tensor(max_rest, max_neg, max_stack[:, :, :, 0], ALU.subtract).then_inc(mmax_step, 1)
                    dve.wait_ge(mmax_step, first + 4)
                    dve.wait_ge(consts_made, MADE)
                    nc.vector.tensor_copy(max_stack[:, :, :, 1], max_rest).then_inc(mmax_step, 1)
                    dve.wait_ge(mmax_step, first + 5)
                    nc.vector.tensor_tensor(max_stack[:, :, :, 2], max_rest, max_stack[:, :, :, 1], ALU.subtract).then_inc(mmax_step, 1)
                    for j in (0, 2):
                        dve.wait_ge(mx_turned, b * (NG * GROUP) + g * GROUP + j + 1)
                        dve.wait_ge(consts_made, MADE)
                        nc.vector.tensor_copy(max_rows(g * GROUP + j), ps[P - SLOT:P, j % 3, :].bitcast(BF16)).then_inc(mx_taken, 1)

                def group_out(g):
                    for c in range(2):
                        dve.wait_ge(mpv_done, b * (NG * NT) + g * NT + NT)
                        dve.wait_ge(consts_made, MADE)
                        dst = mout_t[:, g, c * BANK:(c + 1) * BANK] if isinstance(g, int) else \
                            mout_t[:, bass.ds(g, 1), c * BANK:(c + 1) * BANK].rearrange("p o n -> p (o n)")
                        nc.vector.tensor_copy(dst, ps[:, 6 + c, :]).then_inc(mout_taken, 1)

                split_queries(0)
                for t in range(NT + 1):
                    if t + 1 < NT:
                        split_queries(t + 1)
                    if t < NT:
                        for i in range(2):
                            dve.wait_ge(qs_turned, b * (2 * NT) + 2 * t + i + 1)
                            nc.vector.tensor_copy(q_stack_t[:, 8 * i:8 * i + 8, t * P:(t + 1) * P],
                                                  ps[:, 4 + i, :].bitcast(BF16).rearrange("p (h n) -> p h n", h=8)).then_inc(qs_taken, 1)
                    for u, chunk in enumerate(FIRST_CHUNKS):
                        if chunk[1] == t - 1:
                            max_chunk(0, u)
                stack_max(0)
                with dve.Fori(0, NG - 1) as g:
                    for u in range(CHUNKS):
                        max_chunk(g + 1, u)
                    stack_max(g + 1)
                    group_out(g)
                dve.wait_ge(x_in, b * 16 + 32)
                self_norm(step, b, NORM_NEXT)
                group_out(NG - 1)

                back_rows(1, minv)
                def gate_rows(h):
                    dve.wait_ge(scales_ready, norm_count(b, NORM_GATE, h))
                    for t in range(HALF * h, HALF * (h + 1)):
                        nc.vector.scalar_tensor_tensor(rows[:, t, :], xp[:, t, :], scale[:, t:t + 1], norm2[:], ALU.mult,
                                                       ALU.mult).then_inc(rows_ready, 1)

                add_projection(PROJ_LATENT, xp, xp, gate_rows)
                for t in range(NT):
                    nc.vector.tensor_tensor(xres[:, t, :], xres[:, t, :], xp[:, t, :], ALU.add)

                route = Count(b * ROUTE_STEPS)
                dve.wait_ge(gate_done, b + 1)
                nc.vector.tensor_tensor(logits[:], ps[:, 0, 0:NT * EXPERTS].rearrange("p (t e) -> p t e", t=NT),
                                        gate_b[:].unsqueeze(1).to_broadcast([P, NT, EXPERTS]), ALU.add).then_inc(route_step, 1)
                dve.wait_ge(route_step, route())
                nc.vector.tensor_reduce(best, logits[:], AX.X, ALU.max).then_inc(route_step, 1)
                dve.wait_ge(route_step, route())
                nc.vector.tensor_tensor(logits[:], logits[:], best.unsqueeze(2).to_broadcast([P, NT, EXPERTS]),
                                        ALU.is_equal).then_inc(route_step, 1)
                dve.wait_ge(route_step, route())
                nc.vector.memset(pause[:], 0.0)
                nc.vector.tensor_copy(onehot[:, :, 0], logits[:, :, 0])
                nc.vector.tensor_copy(best, logits[:, :, 0]).then_inc(route_step, 1)
                dve.wait_ge(route_step, route())
                for e in range(1, EXPERTS):
                    nc.vector.tensor_tensor(onehot[:, :, e], logits[:, :, e], best, ALU.is_gt)
                    nc.vector.tensor_tensor(best, best, logits[:, :, e], ALU.max).then_inc(route_step, 1)
                    dve.wait_ge(route_step, route())
                nc.vector.memset(pause[:], 0.0)
                nc.vector.tensor_copy(onehot_b, onehot).then_inc(counts_ready, 1)
                dve.wait_ge(counts_done, b + 1)
                before = ps[:, 7, 0:NT * EXPERTS].rearrange("p (t e) -> p t e", t=NT)
                counts = ps[:, 7, NT * EXPERTS:2 * NT * EXPERTS].rearrange("p (t e) -> p t e", t=NT)
                nc.vector.memset(pause[:], 0.0)
                nc.vector.tensor_copy(cum[0], counts).then_inc(route_step, 1)
                dve.wait_ge(route_step, route())
                cur, shift = 0, 1
                while shift < NT:
                    nc.vector.memset(pause[:], 0.0)
                    nc.vector.tensor_copy(cum[1 - cur][:, 0:shift, :], cum[cur][:, 0:shift, :])
                    nc.vector.tensor_tensor(cum[1 - cur][:, shift:, :], cum[cur][:, shift:, :], cum[cur][:, 0:NT - shift, :],
                                            ALU.add).then_inc(route_step, 1)
                    dve.wait_ge(route_step, route())
                    cur, shift = 1 - cur, 2 * shift
                total, other = cum[cur], cum[1 - cur]
                nc.vector.tensor_tensor(other, total, counts, ALU.subtract).then_inc(route_step, 1)
                dve.wait_ge(route_step, route())
                nc.vector.tensor_tensor(other, other, before, ALU.add).then_inc(route_step, 1)
                dve.wait_ge(route_step, route())
                nc.vector.tensor_tensor(other, other, list_end[:].unsqueeze(1).to_broadcast([P, NT, EXPERTS]), ALU.add).then_inc(route_step, 1)
                dve.wait_ge(route_step, route())
                nc.vector.tensor_tensor(other, other, onehot, ALU.mult)
                nc.vector.tensor_tensor(list_end[:], list_end[:], total[:, NT - 1, :], ALU.add).then_inc(route_step, 1)
                dve.wait_ge(route_step, route())
                nc.vector.tensor_reduce(dest_f, other, AX.X, ALU.add).then_inc(route_step, 1)
                dve.wait_ge(route_step, route())
                nc.vector.memset(pause[:], 0.0)
                nc.vector.tensor_copy(dest, dest_f).then_inc(route_ready, 1)
                assert step.n == DVE_STEPS, ("DVE_STEPS", step.n)
                assert route.n == ROUTE_STEPS, ("ROUTE_STEPS", route.n)

            table = Count()
            nc.vector.memset(pad_row[:, 0:D], 0.0).then_inc(table_step, 1)
            for i in range(2):
                nc.vector.tensor_scalar(pad_row[:, D + i:D + i + 1], pad_id[:], float(BATCH * T + i * P), None, ALU.add).then_inc(table_step, 1)
            nc.vector.tensor_tensor(e_count, list_end[:], list_at[:], ALU.subtract).then_inc(table_step, 1)
            nc.vector.tensor_copy(pad_rowi, list_end[:]).then_inc(table_step, 1)
            dve.wait_ge(table_step, table(5))
            nc.vector.tensor_tensor(e_more, tile_at[:, 0:ROW_TILES].unsqueeze(1).to_broadcast([P, EXPERTS, ROW_TILES]),
                                    e_count.unsqueeze(2).to_broadcast([P, EXPERTS, ROW_TILES]), ALU.is_lt).then_inc(table_step, 1)
            dve.wait_ge(table_step, table())
            nc.vector.tensor_reduce(e_tiles, e_more, AX.X, ALU.add).then_inc(table_step, 1)
            nc.vector.memset(e_start, 0.0).then_inc(table_step, 1)
            dve.wait_ge(table_step, table(2))
            nc.vector.tensor_scalar(e_tiles, e_tiles, float(P), None, ALU.mult).then_inc(table_step, 1)
            dve.wait_ge(table_step, table())
            for e in range(1, EXPERTS):
                nc.vector.tensor_tensor(e_start[:, e:e + 1], e_start[:, e - 1:e], e_tiles[:, e - 1:e], ALU.add).then_inc(table_step, 1)
                dve.wait_ge(table_step, table())
            nc.vector.tensor_scalar(tile_e, tile_at[:], e_start[:, 1:2], None, ALU.is_ge).then_inc(table_step, 1)
            dve.wait_ge(table_step, table())
            for e in range(2, EXPERTS):
                nc.vector.scalar_tensor_tensor(tile_e, tile_at[:], e_start[:, e:e + 1], tile_e, ALU.is_ge, ALU.add).then_inc(table_step, 1)
                dve.wait_ge(table_step, table())
            nc.vector.tensor_copy(tile_ei, tile_e).then_inc(table_step, 1)
            all_e = [P, EXPERTS, MOE_TILES]
            nc.vector.tensor_tensor(tile_place, tile_at[:].unsqueeze(1).to_broadcast(all_e), e_start.unsqueeze(2).to_broadcast(all_e),
                                    ALU.subtract).then_inc(table_step, 1)
            nc.vector.tensor_scalar(tile_list, tile_e, float(LIST), None, ALU.mult).then_inc(table_step, 1)
            dve.wait_ge(table_step, table(3))
            nc.vector.tensor_tensor(tile_of, tile_list.unsqueeze(1).to_broadcast(all_e), list_at[:].unsqueeze(2).to_broadcast(all_e),
                                    ALU.is_equal).then_inc(table_step, 1)
            nc.vector.tensor_tensor(tile_place, tile_place, e_count.unsqueeze(2).to_broadcast(all_e), ALU.min).then_inc(table_step, 1)
            dve.wait_ge(table_step, table(2))
            nc.vector.tensor_tensor(tile_place, tile_place, list_at[:].unsqueeze(2).to_broadcast(all_e), ALU.add).then_inc(table_step, 1)
            dve.wait_ge(table_step, table())
            nc.vector.tensor_tensor(tile_place, tile_place, tile_of, ALU.mult).then_inc(table_step, 1)
            dve.wait_ge(table_step, table())
            nc.vector.tensor_reduce(tile_row, tile_place.rearrange("p e j -> p j e"), AX.X, ALU.add).then_inc(table_step, 1)
            dve.wait_ge(table_step, table())
            nc.vector.tensor_copy(tile_rowi, tile_row).then_inc(tables_ready, 1)

            dve.wait_ge(tables_ready, 1)
            dve.wait_ge(moe_w_in, 64)

            def expert_of(j):
                return dve.value_load(tile_ei[0:1, bass.ds(j, 1)], min_val=0, max_val=EXPERTS - 1)

            def take_h(j, par, e):
                for n in range(2):
                    dve.wait_ge(eh_done, j * 2 + n + 1)
                    nc.vector.tensor_tensor(h_rows[par][:, n * BANK:(n + 1) * BANK], ps[:, 1 + 2 * par + n, :],
                                            b1[:, bass.ds(e * HID + n * BANK, BANK)], ALU.add).then_inc(eh_taken, 1)

            def start_y(j, u, e, landed, stored):
                dve.wait_ge(et_in[u], landed)
                if stored is not None:
                    dve.wait_ge(ey_out[u % 2], stored)
                dve.wait_ge(consts_made, MADE)
                nc.vector.memset(pause[:], 0.0)
                nc.vector.tensor_copy(out_row[u % 2][:], res_in[u][:, D + u % 2:D + u % 2 + 1])
                nc.vector.tensor_tensor(y_rows[u % 2], res_in[u][:, 0:D], b2[:, bass.ds(e * D, D)], ALU.add).then_inc(ey_base, 1)

            def take_y(j, u):
                dve.wait_ge(ey_base, j + 1)
                dve.wait_ge(ey_done, j + 1)
                nc.vector.tensor_tensor(y_rows[u % 2], y_rows[u % 2], ps[:, 7, 0:D], ALU.add).then_inc(ey_taken, 1)

            def expert_step(j, u, landed, stored, last=False):
                start_y(j, u, expert_of(j), landed, stored)
                if not last:
                    take_h(j + 1, (u + 1) % 2, expert_of(j + 1))
                take_y(j, u)

            take_h(0, 0, expert_of(0))
            for u in range(SLOTS):
                expert_step(u, u, 32, 16 * (u // 2) if u >= 2 else None)
            with dve.Fori(1, MOE_TILES // SLOTS - 1) as i:
                for u in range(SLOTS):
                    expert_step(i * SLOTS + u, u, i * 32 + 32, i * 32 + 16 * (u // 2))
            for u in range(SLOTS):
                j = MOE_TILES - SLOTS + u
                expert_step(j, u, 32 * (MOE_TILES // SLOTS), 16 * (j // 2), j == MOE_TILES - 1)


def arrange(x, ctx_1024, mask_Bx1xS2_bf1, L0_attn_gamma, L0_attn_w_qkv, L0_attn_w_out, L0_xattn_Wk, L0_xattn_bk,
            L0_xattn_Wv, L0_xattn_bv, L0_xattn_Wq, L0_xattn_bq, L0_xattn_Wo, L0_xattn_bo, L0_ffn_norm1_w,
            L0_ffn_norm2_w, L0_ffn_Wq, L0_ffn_Wdkv, L0_ffn_Wuk, L0_ffn_Wuv, L0_ffn_Wo, L0_ffn_ln_g, L0_ffn_ln_b,
            L0_ffn_gate_w, L0_ffn_gate_b, L0_ffn_W1, L0_ffn_b1, L0_ffn_W2, L0_ffn_b2):
    def bf16_bits(a):
        return (np.ascontiguousarray(a, np.float32).view(np.uint32) >> 16).astype(np.uint16)

    def by_partition(w):
        return w.reshape(-1, P, w.shape[1]).transpose(1, 0, 2)

    a = {
        "x": x,
        "ctx": ctx_1024.transpose(0, 2, 1).reshape(BATCH, KT, P, CTX).transpose(0, 2, 1, 3),
        "mask": mask_Bx1xS2_bf1.view(np.uint8),
        "gamma": L0_attn_gamma.reshape(KT, P).T,
        "norm1": L0_ffn_norm1_w.reshape(KT, P).T,
        "lat_gb": np.stack([L0_ffn_ln_g, L0_ffn_ln_b], 1),
        "bq": L0_xattn_bq.reshape(KT, P).T,
        "bk": L0_xattn_bk.reshape(KT, P).T,
        "bv": np.tile(L0_xattn_bv, (CTX, 1)),
        "bo": L0_xattn_bo.reshape(1, D),
        "norm2": np.tile(L0_ffn_norm2_w, (P, 1)),
        "gate_b": np.tile(L0_ffn_gate_b, (P, 1)),
        "b2": L0_ffn_b2.reshape(1, -1),
        "b1": L0_ffn_b1.reshape(1, -1),
        "w_qkv": L0_attn_w_qkv.reshape(3, HEADS, HD, KT, P).transpose(1, 4, 3, 0, 2).reshape(HEADS, P, KT * 3 * HD),
        "w_out": by_partition(L0_attn_w_out.T),
        "xw_q": by_partition(L0_xattn_Wq.T),
        "xw_k": by_partition(L0_xattn_Wk.T),
        "xw_v": by_partition(L0_xattn_Wv.T),
        "xw_o": by_partition(L0_xattn_Wo.T),
        "mw_qd": by_partition(np.concatenate([L0_ffn_Wq, L0_ffn_Wdkv]).T),
        "mw_kv": np.concatenate([L0_ffn_Wuk, L0_ffn_Wuv]).T,
        "mw_o": by_partition(L0_ffn_Wo.T),
        "w_gate": by_partition(L0_ffn_gate_w.T),
        "w1": by_partition(L0_ffn_W1.reshape(EXPERTS * HID, D).T),
        "w2": by_partition(L0_ffn_W2.transpose(0, 2, 1).reshape(EXPERTS * HID, D)),
    }
    half = MHD // 2
    freq = (1.0 / np.float32(10000.0) ** (np.arange(half, dtype=np.float32) / np.float32(half))).astype(np.float32)
    ang = np.arange(T, dtype=np.float32)[:, None] * freq[None, :]
    sin, cos = np.sin(ang), np.cos(ang)
    table = np.concatenate([cos, cos, -sin, sin], 1).astype(np.float32).reshape(NT, P, 2 * MHD).transpose(1, 0, 2)
    upper = np.triu(np.full((P, P), MASKED, np.float32), 1)
    a |= {
        "ident": np.eye(P, dtype=np.float32),
        "ident_b": bf16_bits(np.eye(P)),
        "causal_b": bf16_bits(upper),
        "causal_t_b": bf16_bits(upper.T),
        "before_b": bf16_bits(np.triu(np.ones((P, P)), 1)),
        "head_rows": np.kron(np.eye(NT, dtype=np.float32), np.ones((XHD, 1), np.float32)),
        "rope_q": table * np.float32(MHD ** -0.5),
        "rope_k": table,
        "tile_at": np.tile(np.arange(MOE_TILES, dtype=np.float32) * P, (P, 1)),
        "list_at": np.tile(np.arange(EXPERTS, dtype=np.float32) * LIST, (P, 1)),
        "pad_id": np.arange(P, dtype=np.float32)[:, None],
        "row_ids": np.repeat(np.arange(T, dtype=np.float32).reshape(NT, P).T[:, :, None] - T, 2, 2),
    }
    return {k: np.ascontiguousarray(v) for k, v in a.items()}


def kernel(**inputs):
    import concourse.bacc as bacc
    from concourse.bass_utils import run_bass_kernel_spmd

    arrays = arrange(**{k: np.asarray(v) for k, v in inputs.items()})
    nc = bacc.Bacc("TRN2", target_bir_lowering=False, num_devices=1)
    d = {k: nc.dram_tensor("in_" + k, a.shape, mybir.dt.from_np(a.dtype), kind="ExternalInput").ap()
         for k, a in arrays.items()}
    d["out"] = nc.dram_tensor("out", (BATCH * T + 2 * P, D), F32, kind="ExternalOutput").ap()
    for name, shape in (("sorted_rows", (EXPERTS * LIST, D)), ("sorted_res", (EXPERTS * LIST, D + 2))):
        d[name] = nc.dram_tensor(name, shape, F32, kind="Internal").ap()
    decoder_block(nc, d)
    r = run_bass_kernel_spmd(nc, [{"in_" + k: a for k, a in arrays.items()}], core_ids=[0])
    return r.results[0]["out"][:BATCH * T].reshape(BATCH, T, D)
```
